# Optimizing a Trainium2 kernel written in Bass

```python
import numpy as np
import jax
import jax.numpy as jnp

def _softmax(x, axis=-1):
    return jax.nn.softmax(x, axis=axis)

def _gelu(x):
    return jax.nn.gelu(x, approximate=True)

def _silu(x):
    return jax.nn.silu(x)

def _sigmoid(x):
    return jax.nn.sigmoid(x)

def _layernorm(x, axis=-1, eps=1e-05):
    m = jnp.mean(x, axis=axis, keepdims=True)
    v = jnp.var(x, axis=axis, keepdims=True)
    return (x - m) / jnp.sqrt(v + eps)

def _scatter_add(tgt, idx, src, axis=0):
    return tgt.at[idx].add(src)

def _segment_sum(src, seg, n):
    return jax.ops.segment_sum(src, seg, n)
kernel_name = 'mk_decoder_postln_d1_seqx_r4_1b0175'

def setup_inputs(seed: int=0):
    np.random.seed(seed)
    _w = jnp.asarray

    def _rec_inputs():
        import jax
        import jax.numpy as jnp
        _rk = jax.random.key(seed)
        x = 0.0003765 + 1 * jax.random.normal(jax.random.fold_in(_rk, 1), (8, 256, 512), jnp.float32)
        _lenS = 256 - jax.random.randint(jax.random.fold_in(_rk, 7), (8,), 0, max(1, 256 // 4) + 1, jnp.int32)
        _lenS2 = 256 - jax.random.randint(jax.random.fold_in(_rk, 8), (8,), 0, max(1, 256 // 4) + 1, jnp.int32)
        _ctx_2048P = jax.random.normal(jax.random.fold_in(_rk, 11), (8, 16, 512), jnp.float32)
        _ctx_2048c = jax.random.dirichlet(jax.random.fold_in(_rk, 511), 0.3 * jnp.ones((16,), jnp.float32), (8, 256))
        _ctx_2048t = jnp.einsum('bsk,bkd->bsd', _ctx_2048c, _ctx_2048P)
        _ctx_2048t = _ctx_2048t * jax.lax.rsqrt(jnp.mean(jnp.square(_ctx_2048t)) + 1e-12) * 0.953939
        ctx_2048 = -0.000292821 + 1.00034 * (_ctx_2048t + 0.3 * jax.random.normal(jax.random.fold_in(_rk, 611), (8, 256, 512), jnp.float32))
        return (x, ctx_2048)
    x, ctx_2048 = _rec_inputs()

    def _L0_attn_setup():
        import jax, jax.numpy as jnp
        import numpy as np
        EMBED_DIM = 512
        NUM_HEADS = 16
        HEAD_DIM = EMBED_DIM // NUM_HEADS
        SCALE = HEAD_DIM ** (-0.5)
        NEG = -9000000000000000.0

        def _act_quant(x):
            s = 127.0 / jnp.clip(jnp.max(jnp.abs(x), axis=-1, keepdims=True), 1e-05)
            return jnp.clip(jnp.round(x * s), -128.0, 127.0) / s

        def _weight_quant(w):
            s = 1.0 / jnp.clip(jnp.mean(jnp.abs(w)), 1e-05)
            return jnp.clip(jnp.round(w * s), -1.0, 1.0) / s

        def _bitlinear(x, w):
            xq = x + jax.lax.stop_gradient(_act_quant(x) - x)
            wq = w + jax.lax.stop_gradient(_weight_quant(w) - w)
            return jnp.einsum('bnc,oc->bno', xq, wq)
        key = jax.random.key(seed)
        k1, k2, k3 = jax.random.split(key, 3)
        x = jax.random.normal(k1, (2, 512, EMBED_DIM), dtype=jnp.float32)
        w_qkv = jax.random.normal(k2, (3 * EMBED_DIM, EMBED_DIM), dtype=jnp.float32) * EMBED_DIM ** (-0.5)
        w_proj = jax.random.normal(k3, (EMBED_DIM, EMBED_DIM), dtype=jnp.float32) * EMBED_DIM ** (-0.5)
        return {'x': x, 'w_qkv': w_qkv, 'w_proj': w_proj}
    _L0_attn_all = _L0_attn_setup()
    _L0_attn_in = {k: v for k, v in _L0_attn_all.items() if k in ('w_qkv', 'w_proj')}
    del _L0_attn_all

    def _L0_xattn_setup():
        import jax, jax.numpy as jnp
        import numpy as np
        key = jax.random.key(seed)
        k1, k2, k3, k4, k5 = jax.random.split(key, 5)
        B, D_MODEL, L = (2, 256, 512)
        HEAD_DIM = 8
        H = D_MODEL // HEAD_DIM
        return {'k': jax.random.normal(k1, (B, D_MODEL, L), dtype=jnp.float32), 'v': jax.random.normal(k2, (B, D_MODEL, L), dtype=jnp.float32), 'q': jax.random.normal(k3, (B, D_MODEL, L), dtype=jnp.float32), 'ssm_kernel': jax.random.normal(k4, (H, L), dtype=jnp.float32), 'D': jax.random.normal(k5, (H,), dtype=jnp.float32), 'head_dim': HEAD_DIM}
    _L0_xattn_all = _L0_xattn_setup()
    _L0_xattn_in = {k: v for k, v in _L0_xattn_all.items() if k in ('ssm_kernel', 'D')}
    del _L0_xattn_all

    def _L0_ffn_setup():
        import jax, jax.numpy as jnp
        import numpy as np
        from jax import lax
        E = 8
        K = 2
        D = 512
        H = 352
        NS = 2
        B, T = (2, 512)
        EPS = 1e-20
        HS = H * NS

        def _silu(v):
            return v * jax.nn.sigmoid(v)
        key = jax.random.key(seed)
        ks = jax.random.split(key, 8)
        s = 0.02
        return {'x': jax.random.normal(ks[0], (B, T, D), jnp.float32), 'router_w': jax.random.normal(ks[1], (E, D), jnp.float32) * 0.006, 'wg': jax.random.normal(ks[2], (E, D, H), jnp.float32) * s, 'wu': jax.random.normal(ks[3], (E, D, H), jnp.float32) * s, 'wd': jax.random.normal(ks[4], (E, H, D), jnp.float32) * s, 'sg': jax.random.normal(ks[5], (D, HS), jnp.float32) * s, 'su': jax.random.normal(ks[6], (D, HS), jnp.float32) * s, 'sd': jax.random.normal(ks[7], (HS, D), jnp.float32) * s}
    _L0_ffn_all = _L0_ffn_setup()
    _L0_ffn_in = {k: v for k, v in _L0_ffn_all.items() if k in ('router_w', 'wg', 'wu', 'wd', 'sg', 'su', 'sd')}
    del _L0_ffn_all
    return {'x': x, 'ctx_2048': ctx_2048, 'L0_attn_w_qkv': _L0_attn_in['w_qkv'], 'L0_attn_w_proj': _L0_attn_in['w_proj'], 'L0_xattn_ssm_kernel': _L0_xattn_in['ssm_kernel'], 'L0_xattn_D': _L0_xattn_in['D'], 'L0_ffn_router_w': _L0_ffn_in['router_w'], 'L0_ffn_wg': _L0_ffn_in['wg'], 'L0_ffn_wu': _L0_ffn_in['wu'], 'L0_ffn_wd': _L0_ffn_in['wd'], 'L0_ffn_sg': _L0_ffn_in['sg'], 'L0_ffn_su': _L0_ffn_in['su'], 'L0_ffn_sd': _L0_ffn_in['sd']}

def reference(x, ctx_2048, L0_attn_w_qkv, L0_attn_w_proj, L0_xattn_ssm_kernel, L0_xattn_D, L0_ffn_router_w, L0_ffn_wg, L0_ffn_wu, L0_ffn_wd, L0_ffn_sg, L0_ffn_su, L0_ffn_sd):
    import jax
    import jax.numpy as jnp

    def _L0_attn_ref(x, w_qkv, w_proj):
        import jax, jax.numpy as jnp
        import numpy as np
        EMBED_DIM = 512
        NUM_HEADS = 16
        HEAD_DIM = EMBED_DIM // NUM_HEADS
        SCALE = HEAD_DIM ** (-0.5)
        NEG = -9000000000000000.0

        def _act_quant(x):
            s = 127.0 / jnp.clip(jnp.max(jnp.abs(x), axis=-1, keepdims=True), 1e-05)
            return jnp.clip(jnp.round(x * s), -128.0, 127.0) / s

        def _weight_quant(w):
            s = 1.0 / jnp.clip(jnp.mean(jnp.abs(w)), 1e-05)
            return jnp.clip(jnp.round(w * s), -1.0, 1.0) / s

        def _bitlinear(x, w):
            xq = x + jax.lax.stop_gradient(_act_quant(x) - x)
            wq = w + jax.lax.stop_gradient(_weight_quant(w) - w)
            return jnp.einsum('bnc,oc->bno', xq, wq)
        B, N, C = x.shape
        H, D = (NUM_HEADS, HEAD_DIM)
        qkv = _bitlinear(x, w_qkv).reshape(B, N, 3, H, D)
        q, k, v = (qkv[:, :, 0], qkv[:, :, 1], qkv[:, :, 2])
        attn = jnp.einsum('bnhd,bmhd->bhnm', q, k) * SCALE
        causal = jnp.tril(jnp.ones((N, N), dtype=bool))
        attn = jnp.where(causal, attn, NEG)
        attn = jax.nn.softmax(attn, axis=-1)
        out = jnp.einsum('bhnm,bmhd->bnhd', attn, v).reshape(B, N, C)
        return _bitlinear(out, w_proj)

    def _L0_xattn_ref(k, v, q, ssm_kernel, D, head_dim):
        import jax, jax.numpy as jnp
        import numpy as np
        B, HD, L = k.shape
        H = HD // head_dim
        fft_size = 2 * L
        k_ = k.reshape(B, H, head_dim, L)
        v_ = v.reshape(B, H, head_dim, L)
        q_ = q.reshape(B, H, head_dim, L)
        kv = jnp.einsum('bhil,bhjl->bijhl', k_, v_)
        kv_f = jnp.fft.rfft(kv, n=fft_size)
        kernel_f = jnp.fft.rfft(ssm_kernel, n=fft_size)
        y = jnp.fft.irfft(kv_f * kernel_f, n=fft_size)[..., :L]
        out = y + kv * D[None, None, None, :, None]
        out = jnp.einsum('bijhl,bhil->bjhl', out, q_)
        out = jnp.transpose(out, (0, 2, 1, 3)).reshape(B, H * head_dim, L)
        return out.astype(k.dtype)

    def _L0_ffn_ref(x, router_w, wg, wu, wd, sg, su, sd):
        import jax, jax.numpy as jnp
        import numpy as np
        from jax import lax
        E = 8
        K = 2
        D = 512
        H = 352
        NS = 2
        B, T = (2, 512)
        EPS = 1e-20
        HS = H * NS

        def _silu(v):
            return v * jax.nn.sigmoid(v)
        b, t, d = x.shape
        xf = x.reshape(b * t, d)
        n = xf.shape[0]
        gates = jax.nn.softmax(xf @ router_w.T, axis=-1)
        topv, topi = lax.top_k(gates, K)
        masked = jnp.zeros_like(gates).at[jnp.arange(n)[:, None], topi].set(topv)
        masked = masked / (masked.sum(axis=-1, keepdims=True) + EPS)

        def step(acc, p):
            wg_e, wu_e, wd_e, g_e = p
            y = _silu(xf @ wg_e) * (xf @ wu_e) @ wd_e
            return (acc + y * g_e[:, None], None)
        routed, _ = lax.scan(step, jnp.zeros_like(xf), (wg, wu, wd, masked.T))
        shared = _silu(xf @ sg) * (xf @ su) @ sd
        return (routed + shared).reshape(b, t, d)
    x = _layernorm(x + _L0_attn_ref(x, L0_attn_w_qkv, L0_attn_w_proj), axis=-1)
    x = _layernorm(x + _L0_xattn_ref(ctx_2048, ctx_2048, x, L0_xattn_ssm_kernel, L0_xattn_D, 8), axis=-1)
    x = _layernorm(x + _L0_ffn_ref(x, L0_ffn_router_w, L0_ffn_wg, L0_ffn_wu, L0_ffn_wd, L0_ffn_sg, L0_ffn_su, L0_ffn_sd), axis=-1)
    return x

_drawn_inputs = setup_inputs


def setup_inputs(seed=0):
    import zlib

    import numpy as np

    out = dict(_drawn_inputs(seed))
    spreads = {}
    factors = {}
    for name, (base, spread) in spreads.items():
        noise = np.random.default_rng([zlib.crc32(name.encode()), seed]).standard_normal(out[name].shape)
        drawn = base * np.exp(spread * noise) if base else spread * noise
        out[name] = jnp.asarray(drawn.astype(out[name].dtype))
    for name, factor in factors.items():
        out[name] = (out[name] * factor).astype(out[name].dtype)
    return out
```

```python
from contextlib import ExitStack

import concourse.bass as bass
from concourse import mybir

STAGE = 3

F32 = mybir.dt.float32
F32R = mybir.dt.float32r
BF16 = mybir.dt.bfloat16
ALU = mybir.AluOpType
ACT = mybir.ActivationFunctionType
X = mybir.AxisListType.X
ds = bass.ds

P = 128
MAGIC = 12582912.0
MASKED = -1.0e30
LN_EPS = 1e-05


def build(nc, A):
    B, N, C = A["x"].shape
    H, DH = 16, C // 16
    TB = N // P
    NT = B * TB
    KC = C // P
    OG = 2 * C // P
    HG = P // DH
    NG = H // HG
    PAIRS = H // 2
    WT = 3 * C // P
    WALL = WT + C // P
    WCH = 4
    SCALE = float(DH) ** -0.5
    HK, L = A["ssm"].shape
    KP = P + L
    LB = L // P
    I = N // HK
    VW = DH + 1

    x_tok = A["x"].rearrange("b (t p) c -> p (b t) c", p=P)
    ctx_tok = A["ctx"].rearrange("b (t p) c -> p (b t) c", p=P)
    out_tok = A["out"].rearrange("b (t p) c -> p (b t) c", p=P)
    wqkv_v = A["w_qkv"].rearrange("(t p) c -> p t c", p=P)
    wproj_v = A["w_proj"].rearrange("(t p) c -> p t c", p=P)

    with ExitStack() as ctx:
        where = [(nc.sbuf_base + 31) // 32 * 32]

        def sb(name, shape, dt=F32):
            size = 4 if dt in (F32, F32R) else 2
            for n in shape[1:]:
                size *= n
            size = (size + 31) // 32 * 32
            where[0] += size
            assert where[0] <= nc.sbuf_usable_end, (name, where[0])
            return nc.alloc_sbuf_tensor_at(name, shape, dt, offset=where[0] - size)

        def sem(name):
            return ctx.enter_context(nc.semaphore(name))

        xs = sb("xs", [P, NT, C])
        ident = sb("ident", [P, P])
        identb = sb("identb", [P, P], BF16)
        ones = sb("ones", [P, P])
        psum = ctx.enter_context(nc.psum_tensor("psum", [P, 8, 512], F32))

        mark_b = where[0]
        wT = sb("wT", [P, KC, WALL * P], BF16)
        wsum = sb("wsum", [P, WALL])
        wtot = sb("wtot", [P, 2])
        wmean = sb("wmean", [P, 2])
        wscale = sb("wscale", [P, 2])
        mask_st = sb("mask_st", [P, P], BF16)
        mask_s = sb("mask_s", [P, P], BF16)
        sel_col = sb("sel_col", [P, NG])
        sel = sb("sel", [P, NG, P], F32R)
        xq_t = sb("xq_t", [P, TB, C])
        xq = sb("xq", [P, TB, C], BF16)
        amax = sb("amax", [P, TB])
        inv = sb("inv", [P, TB])
        qs_r = sb("qs_r", [P, TB])
        qs = sb("qs", [P, TB])
        vinv = sb("vinv", [P, TB])
        xqT = sb("xqT", [P, KC, N], BF16)
        rs = sb("rs", [P, N])
        real = sb("real", [P, OG, N])
        hi = sb("hi", [P, OG, N], F32R)
        lo = sb("lo", [P, OG, N], F32R)
        vx = sb("vx", [P, TB, H, VW])
        cx = sb("cx", [P, TB, P])
        ct = sb("ct", [P, N], F32R)
        pt = sb("pt", [P, 2, 2, N + P])
        rec = sb("rec", [P, NG, HG, TB])
        attn = sb("attn", [P, TB, C])
        amax2 = sb("amax2", [P, TB])
        inv2 = sb("inv2", [P, TB])
        qs2_r = sb("qs2_r", [P, TB])
        qs2 = sb("qs2", [P, TB])
        pscale = sb("pscale", [P, 2, TB])
        aq = sb("aq", [P, TB, C], BF16)
        aT = sb("aT", [P, KC, N], BF16)
        resid = sb("resid", [P, TB, C])
        stats = sb("stats", [P, TB, 6])
        mv = sb("mv", [P, TB, 2])
        ve = sb("ve", [P, TB])
        lnv = sb("lnv", [P, TB])
        r0 = sb("r0", [P, TB])
        nt1 = sb("nt1", [P, TB])
        nt2 = sb("nt2", [P, TB])
        rstd = sb("rstd", [P, TB])

        kin = sb("kin", [HK, KP])
        dcol = sb("dcol", [HK, 1])
        khl = sb("khl", [HK, 2, KP], F32R)
        krow = nc.dram_tensor("krow", (HK, 2, KP), F32, kind="Internal").ap()
        after_a = where[0]
        wraw = sb("wraw", [P, WALL, C])
        wtern = sb("wtern", [P, WALL, C], BF16)
        where[0] = after_a
        cin = sb("cin", [P, NT, C])
        end_a = where[0]

        s_const = sem("s_const")
        s_w = [sem(f"s_w{i}") for i in range(WALL // WCH)]
        s_x = [sem("s_x0"), sem("s_x1")]
        s_dve = sem("s_dve")
        s_wsum = sem("s_wsum")
        s_wtot_ps = sem("s_wtot_ps")
        s_tern = sem("s_tern")
        s_wT_ps = sem("s_wT_ps")
        s_wT = sem("s_wT")
        xq_ready = sem("xq_ready")
        xT_ps = sem("xT_ps")
        xT_sb = sem("xT_sb")
        r_ps = sem("r_ps")
        r_sb = sem("r_sb")
        qk_ps = sem("qk_ps")
        v_ps = sem("v_ps")
        v_sb = sem("v_sb")
        real_ready = sem("real_ready")
        hi_ready = sem("hi_ready")
        lo_ready = sem("lo_ready")
        s_ps = sem("s_ps")
        mx_done = sem("mx_done")
        c_ps = sem("c_ps")
        ct_ready = sem("ct_ready")
        st_ps = sem("st_ps")
        exp_done = sem("exp_done")
        pv_done = sem("pv_done")
        na_done = sem("na_done")
        aq_ready = sem("aq_ready")
        aT_ps = sem("aT_ps")
        aT_sb = sem("aT_sb")
        proj_ps = sem("proj_ps")
        res_done = sem("res_done")
        var_ready = sem("var_ready")
        ln_act = sem("ln_act")
        r0_ready = sem("r0_ready")
        x1_done = sem("x1_done")
        s_k = sem("s_k")
        k_ready = sem("k_ready")
        k_chain = sem("k_chain")
        s_krow = sem("s_krow")
        s_cin = sem("s_cin")
        s_out = sem("s_out")

        own_sem = {n: sem("own_" + n) for n in (
            'amax', 'clip', 'rec', 'scale', 'round', 'stats', 'aggr', 'nt1', 'nt2', 'nt3', 'nt4', 'srec', 'amax2', 'clip2', 'rec2', 'scale2', 'round2')}
        chain = [0]

        def bankbf(k):
            return psum[:, k, :].bitcast(BF16)

        stage_a = nc.Block()
        block = stage_a.__enter__()

        @block.sync
        def _(sp):
            sp.dma_start(wraw[:, 0:WCH, :], wqkv_v[:, 0:WCH, :]).then_inc(s_w[0], 16)
            sp.dma_start(xs[:, 0:TB, :], x_tok[:, 0:TB, :]).then_inc(s_x[0], 16)
            for i in range(1, WT // WCH):
                sp.dma_start(wraw[:, i * WCH:(i + 1) * WCH, :], wqkv_v[:, i * WCH:(i + 1) * WCH, :]).then_inc(s_w[i], 16)
            sp.dma_start(wraw[:, WT:WALL, :], wproj_v).then_inc(s_w[WT // WCH], 16)
            sp.dma_start(xs[:, TB:NT, :], x_tok[:, TB:NT, :]).then_inc(s_x[1], 16)
            sp.dma_start(kin[:, P:KP], A["ssm"]).then_inc(s_k, 16)
            sp.dma_start(dcol[:], A["D"].rearrange("(h a) -> h a", a=1)).then_inc(s_k, 16)
            sp.wait_ge(k_ready, 3)
            sp.dma_start(krow, khl[:].bitcast(F32)).then_inc(s_krow, 16)
            sp.wait_ge(s_wT, WALL // 2)
            sp.dma_start(cin[:], ctx_tok).then_inc(s_cin, 16)
            sp.wait_ge(s_krow, 16)
            sp.wait_ge(s_cin, 16)
            if STAGE == 1:
                sp.wait_ge(x1_done, B)
                sp.dma_start(out_tok, xs[:]).then_inc(s_out, 16)
                sp.wait_ge(s_out, 16)

        @block.gpsimd
        def _(pool):
            nc.gpsimd.memset(ones[:], 1.0).then_inc(s_const, 1)
            nc.gpsimd.memset(ident[:], 0.0).then_inc(s_const, 1)
            nc.gpsimd.memset(mask_st[:], 0.0).then_inc(s_const, 1)
            nc.gpsimd.memset(mask_s[:], 0.0).then_inc(s_const, 1)
            nc.gpsimd.memset(vx[:], 1.0).then_inc(s_const, 1)
            nc.gpsimd.memset(cx[:], 0.0).then_inc(s_const, 1)
            pool.wait_ge(s_const, 6)
            nc.gpsimd.affine_select(out=ident[:], in_=ident[:], compare_op=ALU.not_equal, fill=1.0, base=0,
                                    pattern=[[-1, P]], channel_multiplier=1).then_inc(s_const, 1)
            nc.gpsimd.affine_select(out=mask_st[:], in_=mask_st[:], compare_op=ALU.is_ge, fill=MASKED, base=0,
                                    pattern=[[1, P]], channel_multiplier=-1).then_inc(s_const, 1)
            nc.gpsimd.affine_select(out=mask_s[:], in_=mask_s[:], compare_op=ALU.is_ge, fill=MASKED, base=0,
                                    pattern=[[-1, P]], channel_multiplier=1).then_inc(s_const, 1)

            nc.gpsimd.memset(kin[:, 0:P], 0.0).then_inc(k_ready, 1)
            pool.wait_ge(s_k, 32)
            pool.wait_ge(k_ready, 1)
            nc.gpsimd.tensor_tensor(kin[:, P:P + 1], kin[:, P:P + 1], dcol[:], ALU.add).then_inc(k_chain, 1)
            pool.wait_ge(k_chain, 1)
            nc.gpsimd.tensor_copy(khl[:, 0, :], kin[:]).then_inc(k_ready, 1)
            pool.wait_ge(k_ready, 2)
            nc.gpsimd.tensor_tensor(khl[:, 1, :], kin[:], khl[:, 0, :].bitcast(F32), ALU.subtract).then_inc(k_ready, 1)

            def low_parts(b):
                for k in range(OG // 2):
                    pool.wait_ge(hi_ready, OG // 2 * b + k + 1)
                    part = slice(2 * k, 2 * k + 2)
                    nc.gpsimd.tensor_tensor(lo[:, part, :], real[:, part, :], hi[:, part, :].bitcast(F32),
                                            ALU.subtract).then_inc(lo_ready, 1)
            low_parts(0)
            with pool.Fori(1, B) as b:
                low_parts(b)

        @block.scalar
        def _(act):
            for i in range(WALL // 2):
                act.wait_ge(s_wT_ps, i + 1)
                nc.scalar.activation(wT[:, :, 2 * i * P:(2 * i + 2) * P].rearrange("p k (t o) -> p t k o", o=P),
                                     bankbf(i % 8)[:, 0:2 * KC * P].rearrange("p (t k o) -> p t k o", t=2, k=KC),
                                     ACT.Copy).then_inc(s_wT, 1)

            def evacuate_inputs(b):
                act.wait_ge(xT_ps, b + 1)
                nc.scalar.activation(xqT[:].rearrange("p k (t n) -> p t k n", n=P),
                                     bankbf(6).rearrange("p (t k n) -> p t k n", t=TB, k=KC), ACT.Copy).then_inc(xT_sb, 1)
                act.wait_ge(r_ps, b + 1)
                nc.scalar.activation(rs[:], psum[:, 7, 0:N], ACT.Copy).then_inc(r_sb, 1)
                for k in range(OG // 2):
                    act.wait_ge(real_ready, OG // 2 * b + k + 1)
                    nc.scalar.activation(hi[:, 2 * k:2 * k + 2, :], real[:, 2 * k:2 * k + 2, :], ACT.Copy).then_inc(hi_ready, 1)
                for t in range(TB):
                    act.wait_ge(v_ps, TB * b + t + 1)
                    nc.scalar.activation(vx[:, t, :, 0:DH], psum[:, 4 + t, :].rearrange("p (h d) -> p h d", d=DH),
                                         ACT.Copy, scale=vinv[:, t:t + 1]).then_inc(v_sb, 1)

            def attn_columns(b):
                act.wait_ge(aT_ps, b + 1)
                nc.scalar.activation(aT[:].rearrange("p k (t n) -> p t k n", n=P),
                                     bankbf(6).rearrange("p (t k n) -> p t k n", t=TB, k=KC), ACT.Copy).then_inc(aT_sb, 1)

            def rstd_guess(b):
                act.wait_ge(var_ready, b + 1)
                nc.scalar.activation(lnv[:], ve[:], ACT.Ln).then_inc(ln_act, 1)
                act.wait_ge(ln_act, b + 1)
                nc.scalar.activation(r0[:], lnv[:], ACT.Exp, scale=-0.5).then_inc(r0_ready, 1)

            def softmax(b, pairs):
                for p in pairs:
                    n = PAIRS * b + p
                    act.wait_ge(st_ps, n + 1)
                    if not (isinstance(b, int) and n < 2):
                        act.wait_ge(pv_done, n - 1)
                    s = 2 * (p % 2)
                    nc.scalar.activation(pt[:, p % 2], psum[:, s:s + 2, 0:N + P], ACT.Exp, scale=SCALE).then_inc(exp_done, 1)

            def batch(b, first):
                evacuate_inputs(b)
                if not first:
                    attn_columns(b - 1)
                act.wait_ge(c_ps, b + 1)
                nc.scalar.activation(ct[:], psum[:, 6, 0:N], ACT.Copy, scale=-1.0).then_inc(ct_ready, 1)
                softmax(b, range(0, 2))
                if not first:
                    rstd_guess(b - 1)
                softmax(b, range(2, PAIRS))

            batch(0, True)
            with act.Fori(1, B) as b:
                batch(b, False)
            attn_columns(B - 1)
            rstd_guess(B - 1)

        @block.vector
        def _(dve):
            def link(ins):
                chain[0] += 1
                ins.then_inc(s_dve, 1)
                dve.wait_ge(s_dve, chain[0])

            dve.wait_ge(s_const, 9)
            link(nc.vector.tensor_copy(identb[:], ident[:]))
            link(nc.vector.tensor_reduce(sel_col[:], ident[:].rearrange("p (j r) -> p r j", j=HG)[:, 0:NG, :], X, ALU.add))
            for g in range(NG):
                ins = nc.vector.tensor_scalar(sel[:, g, :], ones[:], sel_col[:, g:g + 1], None, ALU.mult)
            link(ins)
            for i in range(WALL // WCH):
                dve.wait_ge(s_w[i], 16)
                ins = nc.vector.tensor_reduce(wsum[:, i * WCH:(i + 1) * WCH], wraw[:, i * WCH:(i + 1) * WCH, :], X, ALU.add,
                                              apply_absolute_value=True)
            link(ins)
            nc.vector.tensor_reduce(wtot[:, 0:1], wsum[:, 0:WT], X, ALU.add)
            nc.vector.tensor_reduce(wtot[:, 1:2], wsum[:, WT:WALL], X, ALU.add).then_inc(s_wsum, 1)
            dve.wait_ge(s_wtot_ps, 1)
            nc.vector.tensor_scalar(wmean[:, 0:1], psum[:, 0, 0:1], 1.0 / (3 * C * C), 1e-05, ALU.mult, ALU.max)
            link(nc.vector.tensor_scalar(wmean[:, 1:2], psum[:, 0, 1:2], 1.0 / (C * C), 1e-05, ALU.mult, ALU.max))
            link(nc.vector.reciprocal(wscale[:], wmean[:]))
            for i in range(WALL // WCH):
                part = slice(i * WCH, (i + 1) * WCH)
                w = 0 if i < WT // WCH else 1
                link(nc.vector.tensor_scalar(wraw[:, part, :], wraw[:, part, :], wscale[:, w:w + 1], MAGIC, ALU.mult, ALU.add))
                link(nc.vector.tensor_scalar(wraw[:, part, :], wraw[:, part, :], MAGIC, 1.0, ALU.subtract, ALU.min))
                nc.vector.tensor_scalar(wtern[:, part, :], wraw[:, part, :], -1.0, None, ALU.max).then_inc(s_tern, 1)

            def step(b, name, ins):
                ins.then_inc(own_sem[name], 1)
                dve.wait_ge(own_sem[name], b + 1)

            def quantize(b, before=None):
                x_in = xs[:, ds(TB * b, TB), :]
                if isinstance(b, int):
                    dve.wait_ge(s_x[min(b, 1)], 16)
                nc.vector.tensor_reduce(amax[:], x_in, X, ALU.max, apply_absolute_value=True).then_inc(own_sem["amax"], 1)
                if before:
                    before()
                dve.wait_ge(own_sem["amax"], b + 1)
                step(b, "clip", nc.vector.tensor_scalar(amax[:], amax[:], 1e-05, None, ALU.max))
                nc.vector.tensor_scalar(inv[:], amax[:], 1.0 / 127.0, None, ALU.mult)
                step(b, "rec", nc.vector.reciprocal(qs_r[:], amax[:]))
                nc.vector.tensor_scalar(vinv[:], inv[:], wmean[:, 0:1], None, ALU.mult)
                step(b, "scale", nc.vector.tensor_scalar(qs[:], qs_r[:], 127.0, None, ALU.mult))
                for t in range(TB):
                    ins = nc.vector.tensor_scalar(xq_t[:, t, :], xs[:, ds(TB * b + t, 1), :].rearrange("p a c -> p (a c)"),
                                                  qs[:, t:t + 1], MAGIC, ALU.mult, ALU.add)
                step(b, "round", ins)
                nc.vector.tensor_scalar(xq[:], xq_t[:], MAGIC, 127.0, ALU.subtract, ALU.min).then_inc(xq_ready, 1)

            def scale_qk(b):
                dve.wait_ge(r_sb, b + 1)
                for k in range(OG // 2):
                    dve.wait_ge(qk_ps, OG // 2 * b + k + 1)
                    nc.vector.tensor_tensor(real[:, 2 * k:2 * k + 2, :], psum[:, k, :].rearrange("p (a n) -> p a n", n=N),
                                            rs[:].unsqueeze(1).to_broadcast([P, 2, N]), ALU.mult).then_inc(real_ready, 1)

            def row_max(b):
                for p in range(PAIRS):
                    g, j = p // 2, 2 * (p % 2)
                    s = 2 * (p % 2)
                    dve.wait_ge(s_ps, PAIRS * b + p + 1)
                    cols = cx[:].rearrange("p t (j r) -> p t j r", j=HG)
                    nc.vector.tensor_reduce(cols[:, 1, j:j + 2, g], psum[:, s:s + 2, 0:N], X, ALU.max)
                    nc.vector.tensor_reduce(cols[:, 0, j:j + 2, g], psum[:, s:s + 2, N:N + P], X, ALU.max).then_inc(mx_done, 1)

            def residual(b):
                for t in range(TB):
                    dve.wait_ge(proj_ps, TB * b + t + 1)
                    row = xs[:, ds(TB * b + t, 1), :].rearrange("p a c -> p (a c)")
                    ins = nc.vector.scalar_tensor_tensor(resid[:, t, :], psum[:, 4 + t, :], pscale[:, 1, t:t + 1], row, ALU.mult, ALU.add)
                    ins.then_inc(res_done, 1)
                for t in range(TB):
                    dve.wait_ge(res_done, TB * b + t + 1)
                    ins = nc.vector.bn_stats(stats[:, t, :], resid[:, t, :])
                ins.then_inc(own_sem["stats"], 1)
                dve.wait_ge(own_sem["stats"], b + 1)

            def variance(b):
                for t in range(TB):
                    ins = nc.vector.bn_aggr(mv[:, t, :], stats[:, t, :])
                step(b, "aggr", ins)
                nc.vector.tensor_scalar(ve[:], mv[:, :, 1], LN_EPS, None, ALU.add).then_inc(var_ready, 1)

            def normalise(b):
                dve.wait_ge(r0_ready, b + 1)
                step(b, "nt1", nc.vector.tensor_tensor(nt1[:], r0[:], r0[:], ALU.mult))
                step(b, "nt2", nc.vector.tensor_tensor(nt2[:], nt1[:], ve[:], ALU.mult))
                step(b, "nt3", nc.vector.tensor_scalar(nt1[:], nt2[:], -0.5, 1.5, ALU.mult, ALU.add))
                step(b, "nt4", nc.vector.tensor_tensor(rstd[:], nt1[:], r0[:], ALU.mult))
                for t in range(TB):
                    row = xs[:, ds(TB * b + t, 1), :].rearrange("p a c -> p (a c)")
                    ins = nc.vector.tensor_scalar(row, resid[:, t, :], mv[:, t, 0:1], rstd[:, t:t + 1], ALU.subtract, ALU.mult)
                ins.then_inc(x1_done, 1)

            def attention_rows(b):
                for g in range(NG):
                    dve.wait_ge(pv_done, PAIRS * b + 2 * g + 2)
                    o = psum[:, 4 + g % 2, 0:HG * TB * VW].rearrange("p (h t v) -> p h t v", h=HG, t=TB)
                    ins = nc.vector.reciprocal(rec[:, g], o[:, :, :, DH])
                    ins.then_inc(own_sem["srec"], 1)
                    dve.wait_ge(own_sem["srec"], NG * b + g + 1)
                    for t in range(TB):
                        ins = nc.vector.tensor_tensor(
                            attn[:, t, g * P:(g + 1) * P].rearrange("p (h d) -> p h d", d=DH), o[:, :, t, 0:DH],
                            rec[:, g, :, t].unsqueeze(2).to_broadcast([P, HG, DH]), ALU.mult)
                    ins.then_inc(na_done, 1)
                dve.wait_ge(na_done, NG * b + NG)
                step(b, "amax2", nc.vector.tensor_reduce(amax2[:], attn[:], X, ALU.max, apply_absolute_value=True))
                step(b, "clip2", nc.vector.tensor_scalar(amax2[:], amax2[:], 1e-05, None, ALU.max))
                nc.vector.tensor_scalar(inv2[:], amax2[:], 1.0 / 127.0, None, ALU.mult)
                step(b, "rec2", nc.vector.reciprocal(qs2_r[:], amax2[:]))
                nc.vector.tensor_scalar(pscale[:, 1, :], inv2[:], wmean[:, 1:2], None, ALU.mult)
                step(b, "scale2", nc.vector.tensor_scalar(qs2[:], qs2_r[:], 127.0, None, ALU.mult))
                for t in range(TB):
                    ins = nc.vector.tensor_scalar(attn[:, t, :], attn[:, t, :], qs2[:, t:t + 1], MAGIC, ALU.mult, ALU.add)
                step(b, "round2", ins)
                nc.vector.tensor_scalar(aq[:], attn[:], MAGIC, 127.0, ALU.subtract, ALU.min).then_inc(aq_ready, 1)

            def batch(b, first, last):
                scale_qk(b)
                row_max(b)
                if not first:
                    residual(b - 1)
                if last:
                    variance(b - 1)
                else:
                    dve.wait_ge(v_sb, TB * (b + 1))
                    quantize(b + 1, None if first else lambda: variance(b - 1))
                if not first:
                    normalise(b - 1)
                attention_rows(b)

            quantize(0)
            batch(0, True, False)
            with dve.Fori(1, B - 1) as b:
                batch(b, False, False)
            batch(B - 1, False, True)
            residual(B - 1)
            variance(B - 1)
            normalise(B - 1)

        @block.tensor
        def _(pe):
            mm = nc.tensor.matmul
            pe.wait_ge(s_wsum, 1)
            mm(psum[:, 0, 0:2], ones[:], wtot[:], start=True, stop=True).then_inc(s_wtot_ps, 1)
            for i in range(WALL // 2):
                pe.wait_ge(s_tern, 2 * i // WCH + 1)
                if i >= 8:
                    pe.wait_ge(s_wT, i - 7)
                for t in range(2):
                    for k in range(KC):
                        at = (t * KC + k) * P
                        ins = nc.tensor.transpose(bankbf(i % 8)[:, at:at + P], wtern[:, 2 * i + t, k * P:(k + 1) * P], identb[:])
                ins.then_inc(s_wT_ps, 1)
            pe.wait_ge(s_wT, WALL // 2)

            def qkv(b):
                pe.wait_ge(xq_ready, b + 1)
                for t in range(TB):
                    for k in range(KC):
                        at = (t * KC + k) * P
                        ins = nc.tensor.transpose(bankbf(6)[:, at:at + P], xq[:, t, k * P:(k + 1) * P], identb[:])
                ins.then_inc(xT_ps, 1)
                for t in range(TB):
                    ins = mm(psum[:, 7, t * P:(t + 1) * P], vinv[:, t:t + 1].to_broadcast([P, P]), ident[:], start=True, stop=True)
                ins.then_inc(r_ps, 1)
                pe.wait_ge(xT_sb, b + 1)
                if not (isinstance(b, int) and b == 0):
                    pe.wait_ge(exp_done, PAIRS * b)
                for o in range(OG):
                    for k in range(KC):
                        ins = mm(psum[:, o // 2, (o % 2) * N:(o % 2 + 1) * N], wT[:, k, o * P:(o + 1) * P], xqT[:, k, :],
                                 start=(k == 0), stop=(k == KC - 1))
                    if o % 2:
                        ins.then_inc(qk_ps, 1)
                if not (isinstance(b, int) and b == 0):
                    pe.wait_ge(na_done, NG * b)
                for t in range(TB):
                    for k in range(KC):
                        ins = mm(psum[:, 4 + t, :], xqT[:, k, t * P:(t + 1) * P], wT[:, k, OG * P:OG * P + C],
                                 start=(k == 0), stop=(k == KC - 1))
                    ins.then_inc(v_ps, 1)

            def scores_for_max(b):
                pe.wait_ge(hi_ready, OG // 2 * (b + 1))
                for p in range(PAIRS):
                    if p >= 2:
                        pe.wait_ge(mx_done, PAIRS * b + p - 1)
                    g = p // 2
                    for e in range(2):
                        bank = 2 * (p % 2) + e
                        mm(psum[:, bank, P:2 * P], identb[:], mask_s[:], start=True, stop=False, skip_group_check=True)
                        mm(psum[:, bank, N:N + P], identb[:], mask_s[:], start=False, stop=False, skip_group_check=True)
                    for e in range(2):
                        bank = 2 * (p % 2) + e
                        r = slice(DH * (2 * (p % 2) + e), DH * (2 * (p % 2) + e + 1))
                        mm(psum[:, bank, 0:N], hi[r, g, P:N], hi[r, NG + g, :], start=False, stop=False, skip_group_check=True)
                        ins = mm(psum[:, bank, N:N + P], hi[r, g, 0:P], hi[r, NG + g, 0:P], start=False, stop=True, skip_group_check=True)
                    ins.then_inc(s_ps, 1)

            def project(b):
                pe.wait_ge(aq_ready, b + 1)
                for t in range(TB):
                    for k in range(KC):
                        at = (t * KC + k) * P
                        ins = nc.tensor.transpose(bankbf(6)[:, at:at + P], aq[:, t, k * P:(k + 1) * P], identb[:])
                ins.then_inc(aT_ps, 1)
                pe.wait_ge(aT_sb, b + 1)
                for t in range(TB):
                    for k in range(KC):
                        ins = mm(psum[:, 4 + t, :], aT[:, k, t * P:(t + 1) * P], wT[:, k, WT * P:WALL * P],
                                 start=(k == 0), stop=(k == KC - 1))
                    ins.then_inc(proj_ps, 1)

            def scores(b, p):
                n = PAIRS * b + p
                if p >= 2:
                    pe.wait_ge(exp_done, n - 1)
                g = p // 2
                for e in range(2):
                    bank = 2 * (p % 2) + e
                    mm(psum[:, bank, 0:P], identb[:], mask_st[:], start=True, stop=False, skip_group_check=True)
                    mm(psum[:, bank, N:N + P], identb[:], mask_st[:], start=False, stop=False, skip_group_check=True)
                for e in range(2):
                    bank = 2 * (p % 2) + e
                    r = slice(DH * (2 * (p % 2) + e), DH * (2 * (p % 2) + e + 1))
                    mm(psum[:, bank, 0:N], sel[r, g, :], ct[r, :], start=False, stop=False, skip_group_check=True)
                    mm(psum[:, bank, N:N + P], sel[r, g, :], ct[r, P:N], start=False, stop=False, skip_group_check=True)
                for kk, qq in ((hi, hi), (hi, lo), (lo, hi)):
                    for e in range(2):
                        bank = 2 * (p % 2) + e
                        r = slice(DH * (2 * (p % 2) + e), DH * (2 * (p % 2) + e + 1))
                        mm(psum[:, bank, 0:N], kk[r, NG + g, 0:P], qq[r, g, :], start=False, stop=False, skip_group_check=True)
                        ins = mm(psum[:, bank, N:N + P], kk[r, NG + g, P:N], qq[r, g, P:N], start=False, stop=(kk is lo),
                                 skip_group_check=True)
                ins.then_inc(st_ps, 1)

            def values(b, p):
                g = p // 2
                pe.wait_ge(exp_done, PAIRS * b + p + 1)
                if p % 2 == 0 and g >= 2:
                    pe.wait_ge(na_done, NG * b + g - 1)
                for e in range(2):
                    h = 2 * p + e
                    at = (h % HG) * TB * VW
                    o = psum[:, 4 + g % 2, :]
                    mm(o[:, at:at + VW], pt[:, p % 2, e, 0:P], vx[:, 0, h, :], start=True, stop=True)
                    mm(o[:, at + VW:at + 2 * VW], pt[:, p % 2, e, P:N], vx[:, 0, h, :], start=True, stop=False)
                    ins = mm(o[:, at + VW:at + 2 * VW], pt[:, p % 2, e, N:N + P], vx[:, 1, h, :], start=False, stop=True)
                ins.then_inc(pv_done, 1)

            def batch(b, first):
                qkv(b)
                scores_for_max(b)
                pe.wait_ge(v_sb, TB * (b + 1))
                if not first:
                    project(b - 1)
                pe.wait_ge(mx_done, PAIRS * (b + 1))
                for t in range(TB):
                    ins = nc.tensor.transpose(psum[:, 6, t * P:(t + 1) * P], cx[:, t, :], ident[:])
                ins.then_inc(c_ps, 1)
                pe.wait_ge(lo_ready, OG // 2 * (b + 1))
                pe.wait_ge(ct_ready, b + 1)
                if not first:
                    pe.wait_ge(res_done, TB * b)
                for p in range(PAIRS):
                    scores(b, p)
                    if p:
                        values(b, p - 1)
                values(b, PAIRS - 1)

            batch(0, True)
            with pe.Fori(1, B) as b:
                batch(b, False)
            project(B - 1)


        stage_a.__exit__(None, None, None)
        if STAGE == 1:
            return

        PAIRN = I * (I + 1) // 2
        off = [sum(I - r for r in range(s)) for s in range(I)]
        where[0] = mark_b
        cT = sb("cT", [P, LB, B, N])
        qT = sb("qT", [P, LB, B, N])
        mark_t = where[0]
        yT = sb("yT", [P, LB, B, N])
        kv = [sb(f"kv{i}", [P, LB * B, PAIRN]) for i in range(2)]
        kvh = [sb(f"kvh{i}", [P, LB, B * PAIRN], F32R) for i in range(2)]
        kvl = [sb(f"kvl{i}", [P, LB, B * PAIRN], F32R) for i in range(2)]
        prod = [sb(f"prod{i}", [P, LB * B, I, I]) for i in range(2)]
        toep = [sb(f"toep{i}", [P, 2, L], F32R) for i in range(2)]
        stats2 = sb("stats2", [P, NT, 6])
        mv2 = sb("mv2", [P, NT, 2])
        ve2 = sb("ve2", [P, NT])
        lnv2 = sb("lnv2", [P, NT])
        g2 = sb("g2", [P, NT])
        n1 = sb("n1", [P, NT])
        n2 = sb("n2", [P, NT])
        rstd2 = sb("rstd2", [P, NT])
        end_b = where[0]
        where[0] = max(end_b, end_a)
        crev = sb("crev", [P, 2, C])
        assert mark_t <= after_a

        rev_ready = sem("rev_ready")
        cT_ps = sem("cT_ps")
        qT_ps = sem("qT_ps")
        cT_done = sem("cT_done")
        qT_done = sem("qT_done")
        s_toep = [sem("s_toep0"), sem("s_toep1")]
        kv_sq = sem("kv_sq")
        kv_ready = sem("kv_ready")
        kvh_ready = sem("kvh_ready")
        kvl_ready = sem("kvl_ready")
        y_ps = sem("y_ps")
        ym_done = sem("ym_done")
        y_done = sem("y_done")
        yT_ps = sem("yT_ps")
        res2 = sem("res2")
        own2 = sem("own2")
        ln2_act = sem("ln2_act")
        g2_ready = sem("g2_ready")
        x2_done = sem("x2_done")

        def conv_out_bank(u):
            return psum[:, u % 8, :]

        with nc.Block() as block:
            @block.sync
            def _(sp):
                def load(h, e, first):
                    if not first:
                        sp.wait_ge(y_ps, h - 1)
                    src = bass.AP(krow.tensor, 1, [[2 * KP, HK], [1, P], [KP, 2], [1, L]])[ds(h, 1)]
                    sp.dma_start(toep[e][:].bitcast(F32), src.rearrange("a p v l -> (a p) v l")).then_inc(s_toep[e], 16)
                for e in range(2):
                    load(e, e, True)
                with sp.Fori(1, HK // 2) as hp:
                    for e in range(2):
                        load(2 * hp + e, e, False)
                if STAGE == 2:
                    sp.wait_ge(x2_done, 1)
                    sp.dma_start(out_tok, xs[:]).then_inc(s_out, 16)
                    sp.wait_ge(s_out, 16)

            @block.gpsimd
            def _(pool):
                pool.wait_ge(cT_done, NT)

                def products(h, e, first):
                    if not first:
                        pool.wait_ge(kvl_ready, h - 1)
                    for s in range(1, I):
                        a = cT[:].rearrange("p k b c -> p (k b) c")
                        ins = nc.gpsimd.tensor_tensor(kv[e][:, :, off[s]:off[s] + I - s], a[:, :, ds(I * h, I - s)],
                                                      a[:, :, ds(I * h + s, I - s)], ALU.mult)
                    ins.then_inc(kv_ready, 1)

                def low_part(h, e, first):
                    pool.wait_ge(kvh_ready, h + 1)
                    if not first:
                        pool.wait_ge(y_ps, h - 1)
                    nc.gpsimd.tensor_tensor(kvl[e][:].rearrange("p k n -> p (k n)"), kv[e][:].rearrange("p a n -> p (a n)"),
                                            kvh[e][:].rearrange("p k n -> p (k n)").bitcast(F32), ALU.subtract).then_inc(kvl_ready, 1)

                products(0, 0, True)
                products(1, 1, True)
                low_part(0, 0, True)
                products(2, 0, False)
                low_part(1, 1, True)
                with pool.Fori(1, HK // 2 - 1) as hp:
                    for e in range(2):
                        products(2 * hp + e + 1, 1 - e, False)
                        low_part(2 * hp + e, e, False)
                products(HK - 1, 1, False)
                low_part(HK - 2, 0, False)
                low_part(HK - 1, 1, False)

            @block.scalar
            def _(act):
                for u in range(NT):
                    b, hc = u // 2, u % 2
                    act.wait_ge(cT_ps, u + 1)
                    nc.scalar.activation(cT[:, :, b, hc * P:(hc + 1) * P], psum[:, (2 * u) % 8, :].rearrange("p (k n) -> p k n", n=P),
                                         ACT.Copy).then_inc(cT_done, 1)
                act.wait_ge(cT_done, NT)

                def squares(h, e, first):
                    if not first:
                        act.wait_ge(kvl_ready, h - 1)
                    a = cT[:].rearrange("p k b c -> p (k b) c")
                    nc.scalar.activation(kv[e][:, :, 0:I], a[:, :, ds(I * h, I)], ACT.Square).then_inc(kv_sq, 1)

                def high_part(h, e, first):
                    act.wait_ge(kv_sq, h + 1)
                    act.wait_ge(kv_ready, h + 1)
                    if not first:
                        act.wait_ge(y_ps, h - 1)
                    nc.scalar.activation(kvh[e][:].rearrange("p k n -> p (k n)"), kv[e][:].rearrange("p a n -> p (a n)"),
                                         ACT.Copy).then_inc(kvh_ready, 1)

                def head(h, e, first):
                    squares(h, e, first)
                    high_part(h, e, first)
                for e in range(2):
                    head(e, e, True)
                with act.Fori(1, HK // 2) as hp:
                    for e in range(2):
                        head(2 * hp + e, e, False)
                act.wait_ge(own2, 3)
                nc.scalar.activation(lnv2[:], ve2[:], ACT.Ln).then_inc(ln2_act, 1)
                act.wait_ge(ln2_act, 1)
                nc.scalar.activation(g2[:], lnv2[:], ACT.Exp, scale=-0.5).then_inc(g2_ready, 1)

            @block.vector
            def _(dve):
                for u in range(NT):
                    b, hc = u // 2, u % 2
                    if u >= 2:
                        dve.wait_ge(cT_ps, u - 1)
                    nc.vector.tensor_copy(crev[:, hc, :].rearrange("p (k l) -> p k l", l=P),
                                          cin[:, u, :].rearrange("p (k l) -> p k l", l=P)[:, :, ::-1]).then_inc(rev_ready, 1)
                    dve.wait_ge(qT_ps, u + 1)
                    nc.vector.tensor_copy(qT[:, :, b, hc * P:(hc + 1) * P],
                                          psum[:, (2 * u + 1) % 8, :].rearrange("p (k n) -> p k n", n=P)).then_inc(qT_done, 1)
                dve.wait_ge(qT_done, NT)

                def scale_by_q(h, e, first):
                    dve.wait_ge(y_ps, h + 1)
                    if not first:
                        dve.wait_ge(y_done, h - 1)
                    flat = prod[e][:].rearrange("p a j i -> p a (j i)")
                    y = psum[:, 4 * e:4 * e + LB, 0:B * PAIRN].rearrange("p k (b n) -> p k b n", n=PAIRN)
                    for s in range(I):
                        ys = y[:, :, :, off[s]:off[s] + I - s]
                        last = (I - s - 1) * (I + 1) + 1
                        for shift, at in ((0, s * I), (s, s))[0:1 + (s > 0)]:
                            o = flat[:, :, at:at + last:I + 1].rearrange("p (k b) n -> p k b n", b=B)
                            ins = nc.vector.tensor_tensor(o, ys, qT[:, :, :, ds(I * h + shift, I - s)], ALU.mult)
                    ins.then_inc(ym_done, 1)

                def sum_over_i(h, e):
                    dve.wait_ge(ym_done, h + 1)
                    nc.vector.tensor_reduce(yT[:].rearrange("p k b c -> p (k b) c")[:, :, ds(I * h, I)], prod[e][:], X, ALU.add)\
                       .then_inc(y_done, 1)

                scale_by_q(0, 0, True)
                scale_by_q(1, 1, True)
                sum_over_i(0, 0)
                with dve.Fori(1, HK // 2) as hp:
                    for e in range(2):
                        scale_by_q(2 * hp + e, e, False)
                        sum_over_i(2 * hp + e - 1, 1 - e)
                sum_over_i(HK - 1, 1)

                for u in range(NT):
                    dve.wait_ge(yT_ps, u + 1)
                    nc.vector.tensor_tensor(xs[:, u, :], xs[:, u, :], conv_out_bank(u), ALU.add).then_inc(res2, 1)
                    if u:
                        dve.wait_ge(res2, u)
                        nc.vector.bn_stats(stats2[:, u - 1, :], xs[:, u - 1, :])
                dve.wait_ge(res2, NT)
                nc.vector.bn_stats(stats2[:, NT - 1, :], xs[:, NT - 1, :]).then_inc(own2, 1)
                dve.wait_ge(own2, 1)
                for u in range(NT):
                    ins = nc.vector.bn_aggr(mv2[:, u, :], stats2[:, u, :])
                ins.then_inc(own2, 1)
                dve.wait_ge(own2, 2)
                nc.vector.tensor_scalar(ve2[:], mv2[:, :, 1], LN_EPS, None, ALU.add).then_inc(own2, 1)
                dve.wait_ge(g2_ready, 1)
                nc.vector.tensor_tensor(n1[:], g2[:], g2[:], ALU.mult).then_inc(own2, 1)
                dve.wait_ge(own2, 4)
                nc.vector.tensor_tensor(n2[:], n1[:], ve2[:], ALU.mult).then_inc(own2, 1)
                dve.wait_ge(own2, 5)
                nc.vector.tensor_scalar(n1[:], n2[:], -0.5, 1.5, ALU.mult, ALU.add).then_inc(own2, 1)
                dve.wait_ge(own2, 6)
                nc.vector.tensor_tensor(rstd2[:], n1[:], g2[:], ALU.mult).then_inc(own2, 1)
                dve.wait_ge(own2, 7)
                for u in range(NT):
                    ins = nc.vector.tensor_scalar(xs[:, u, :], xs[:, u, :], mv2[:, u, 0:1], rstd2[:, u:u + 1], ALU.subtract, ALU.mult)
                ins.then_inc(x2_done, 1)

            @block.tensor
            def _(pe):
                mm = nc.tensor.matmul
                for u in range(NT):
                    if u >= 4:
                        pe.wait_ge(cT_done, u - 3)
                        pe.wait_ge(qT_done, u - 3)
                    for k in range(LB):
                        ins = nc.tensor.transpose(psum[:, (2 * u + 1) % 8, k * P:(k + 1) * P], xs[:, u, k * P:(k + 1) * P], ident[:])
                    ins.then_inc(qT_ps, 1)
                    pe.wait_ge(rev_ready, u + 1)
                    for k in range(LB):
                        ins = nc.tensor.transpose(psum[:, (2 * u) % 8, k * P:(k + 1) * P], crev[:, u % 2, k * P:(k + 1) * P], ident[:])
                    ins.then_inc(cT_ps, 1)
                pe.wait_ge(cT_done, NT)
                pe.wait_ge(qT_done, NT)

                def convolve(h, hp, e, first):
                    pe.wait_ge(s_toep[e], 16 * hp + 16)
                    pe.wait_ge(kvl_ready, h + 1)
                    if not first:
                        pe.wait_ge(ym_done, h - 1)
                    for lb in range(LB):
                        for mb in range(lb + 1):
                            d = slice((lb - mb) * P, (lb - mb + 1) * P)
                            for v, rhs in ((0, kvh), (0, kvl), (1, kvh)):
                                ins = mm(psum[:, 4 * e + lb, 0:B * PAIRN], toep[e][:, v, d], rhs[e][:, mb, :],
                                         start=(mb == 0 and v == 0 and rhs is kvh), stop=(mb == lb and v == 1))
                    ins.then_inc(y_ps, 1)
                for e in range(2):
                    convolve(e, 0, e, True)
                with pe.Fori(1, HK // 2) as hp:
                    for e in range(2):
                        convolve(2 * hp + e, hp, e, False)
                pe.wait_ge(y_done, HK)
                for u in range(NT):
                    b, hc = u // 2, u % 2
                    if u >= 8:
                        pe.wait_ge(res2, u - 7)
                    for k in range(LB):
                        ins = nc.tensor.transpose(conv_out_bank(u)[:, k * P:(k + 1) * P], yT[:, k, b, hc * P:(hc + 1) * P], ident[:])
                    ins.then_inc(yT_ps, 1)

        if STAGE == 2:
            return

        E, _, F = A["wg"].shape
        UNITS = E + A["sg"].shape[1] // F
        FT = [(f, min(P, F - f)) for f in range(0, F, P)]
        NF = len(FT)
        J = 2 * P
        JOBS = NT // 2
        where[0] = mark_b
        xh = sb("xh", [P, KC, NT * P], F32R)
        xl = sb("xl", [P, KC, NT * P], F32R)
        stg = [sb("stg_g", [P, KC, F]), sb("stg_u", [P, KC, F]), sb("stg_d", [P, NF, C])]
        wh = [[sb(f"wh_g{i}", [P, KC, F], F32R), sb(f"wh_u{i}", [P, KC, F], F32R), sb(f"wh_d{i}", [P, NF, C], F32R)] for i in range(2)]
        wl = [[sb(f"wl_g{i}", [P, KC, F], F32R), sb(f"wl_u{i}", [P, KC, F], F32R), sb(f"wl_d{i}", [P, NF, C], F32R)] for i in range(2)]
        sil = sb("sil", [P, NF, J])
        hr = sb("hr", [P, NF, J])
        hh = sb("hh", [P, NF, J], F32R)
        hl = sb("hl", [P, NF, J], F32R)
        rin = sb("rin", [E, C])
        rth = sb("rth", [P, KC, E], F32R)
        rtl = sb("rtl", [P, KC, E], F32R)
        lg = sb("lg", [P, NT, E])
        ex = sb("ex", [P, NT, E])
        gates = sb("gates", [P, NT, E])
        keys = sb("keys", [P, NT, E])
        rest = sb("rest", [P, NT, E])
        one1 = sb("one1", [P, NT, E])
        one2 = sb("one2", [P, NT, E])
        gate = sb("gate", [P, NT, E])
        rank = sb("rank", [P, E])
        t16 = [sb(f"t16_{i}", [P, NT]) for i in range(6)]
        mv3 = sb("mv3", [P, NT, 2])
        stats3 = sb("stats3", [P, NT, 6])
        ve3 = sb("ve3", [P, NT])
        lnv3 = sb("lnv3", [P, NT])
        g3 = sb("g3", [P, NT])
        m1 = sb("m1", [P, NT])
        m2 = sb("m2", [P, NT])
        rstd3 = sb("rstd3", [P, NT])

        xt_ps = sem("xt_ps")
        xh_ready = sem("xh_ready")
        xl_ready = sem("xl_ready")
        s_r = sem("s_r")
        rt_ps = sem("rt_ps")
        rth_ready = sem("rth_ready")
        rt_ready = sem("rt_ready")
        lg_ps = sem("lg_ps")
        rank_ready = sem("rank_ready")
        own3 = sem("own3")
        ex_ready = sem("ex_ready")
        gate_ready = sem("gate_ready")
        s_stg = [sem("s_stg_g"), sem("s_stg_u"), sem("s_stg_d")]
        whi_ready = sem("whi_ready")
        wlo_ready = sem("wlo_ready")
        gu_ps = sem("gu_ps")
        sil_ready = sem("sil_ready")
        hr_ready = sem("hr_ready")
        hh_ready = sem("hh_ready")
        hl_ready = sem("hl_ready")
        dn_ps = sem("dn_ps")
        acc_done = sem("acc_done")
        ln3_act = sem("ln3_act")
        g3_ready = sem("g3_ready")
        x3_done = sem("x3_done")
        DN = 3

        with nc.Block() as block:
            @block.sync
            def _(sp):
                sp.dma_start(rin[:], A["router"]).then_inc(s_r, 16)

                def load(n, first, wg, wu, wd):
                    for i, (w, cut) in enumerate(((wg, None), (wu, None), (wd, None))):
                        if not first:
                            sp.wait_ge(wlo_ready, 3 * (n - 1) + i + 1)
                        if i < 2:
                            sp.dma_start(stg[i][:], w.rearrange("(k p) f -> p k f", p=P)).then_inc(s_stg[i], 16)
                        else:
                            full = F // P
                            sp.dma_start(stg[2][:, 0:full, :], w[0:full * P, :].rearrange("(k p) c -> p k c", p=P)).then_inc(s_stg[2], 16)
                            sp.dma_start(stg[2][0:F - full * P, full, :], w[full * P:F, :]).then_inc(s_stg[2], 16)

                def expert(n, first):
                    row = lambda name: A[name][ds(n, 1)].rearrange("a p f -> (a p) f")
                    load(n, first, row("wg"), row("wu"), row("wd"))
                expert(0, True)
                with sp.Fori(1, E) as n:
                    expert(n, False)
                for u in range(UNITS - E):
                    f = slice(u * F, (u + 1) * F)
                    load(E + u, False, A["sg"][:, f], A["su"][:, f], A["sd"][f, :])
                sp.wait_ge(x3_done, 1)
                sp.dma_start(out_tok, xs[:]).then_inc(s_out, 16)
                sp.wait_ge(s_out, 16)

            def all_units(eng, job, split):
                def unit(n, e, last=False):
                    job(n, e, 0)
                    if split is not None and not last:
                        split(n + 1, 1 - e)
                    with eng.Fori(1, JOBS) as c:
                        job(n, e, c)
                unit(0, 0)
                unit(1, 1)
                with eng.Fori(1, E // 2) as pair:
                    for e in range(2):
                        unit(2 * pair + e, e)
                for n in range(E, UNITS):
                    unit(n, n % 2, last=(n == UNITS - 1))

            @block.gpsimd
            def _(pool):
                for e in range(E):
                    ins = nc.gpsimd.memset(rank[:, e:e + 1], float(E - e))
                ins.then_inc(rank_ready, 1)

            def split_rows(i):
                if i < 2:
                    return [(slice(0, P), slice(0, KC))]
                return [(slice(0, P), slice(0, F // P)), (slice(0, F % P), slice(F // P, NF))]

            @block.scalar
            def _(act):
                for t in range(NT):
                    act.wait_ge(xt_ps, t + 1)
                    nc.scalar.activation(xh[:, :, t * P:(t + 1) * P], psum[:, t % 8, :].rearrange("p (k n) -> p k n", n=P), ACT.Copy)\
                       .then_inc(xh_ready, 1)
                act.wait_ge(rt_ps, 1)
                nc.scalar.activation(rth[:], psum[:, 0, 0:KC * E].rearrange("p (k e) -> p k e", e=E), ACT.Copy).then_inc(rth_ready, 1)
                act.wait_ge(own3, 2)
                nc.scalar.activation(ex[:], lg[:], ACT.Exp).then_inc(ex_ready, 1)

                def high_weights(n, e):
                    for i in range(3):
                        act.wait_ge(s_stg[i], (16 if i < 2 else 32) * (n + 1))
                        if not (isinstance(n, int) and n < 2):
                            act.wait_ge(dn_ps, 2 * JOBS * (n - 1))
                        for r, k in split_rows(i):
                            ins = nc.scalar.activation(wh[e][i][r, k, :], stg[i][r, k, :], ACT.Copy)
                        ins.then_inc(whi_ready, 1)

                def hidden(n, e, c):
                    m = JOBS * n + c
                    for f, (_, w) in enumerate(FT):
                        act.wait_ge(gu_ps, NF * m + f + 1)
                        nc.scalar.activation(sil[0:w, f, :], psum[0:w, f, 0:J], ACT.Silu).then_inc(sil_ready, 1)
                        act.wait_ge(hr_ready, NF * m + f + 1)
                        if not (isinstance(m, int) and m == 0):
                            act.wait_ge(dn_ps, 2 * m)
                        nc.scalar.activation(hh[0:w, f, :], hr[0:w, f, :], ACT.Copy).then_inc(hh_ready, 1)

                high_weights(0, 0)
                all_units(act, hidden, high_weights)
                act.wait_ge(own3, 25)
                nc.scalar.activation(lnv3[:], ve3[:], ACT.Ln).then_inc(ln3_act, 1)
                act.wait_ge(ln3_act, 1)
                nc.scalar.activation(g3[:], lnv3[:], ACT.Exp, scale=-0.5).then_inc(g3_ready, 1)

            @block.vector
            def _(dve):
                chain3 = [0]

                def link(ins):
                    chain3[0] += 1
                    ins.then_inc(own3, 1)
                    dve.wait_ge(own3, chain3[0])

                for t in range(NT):
                    dve.wait_ge(xh_ready, t + 1)
                    nc.vector.tensor_tensor(xl[:, :, t * P:(t + 1) * P], psum[:, t % 8, :].rearrange("p (k n) -> p k n", n=P),
                                            xh[:, :, t * P:(t + 1) * P].bitcast(F32), ALU.subtract).then_inc(xl_ready, 1)
                dve.wait_ge(rth_ready, 1)
                nc.vector.tensor_tensor(rtl[:], psum[:, 0, 0:KC * E].rearrange("p (k e) -> p k e", e=E), rth[:].bitcast(F32),
                                        ALU.subtract).then_inc(rt_ready, 1)
                pl = psum[:, 1, 0:NT * E].rearrange("p (t e) -> p t e", e=E)
                top, tot, rtot, k1, k2, top2 = (t[:] for t in t16)

                def over(a):
                    return a.unsqueeze(2).to_broadcast([P, NT, E])
                dve.wait_ge(lg_ps, 1)
                link(nc.vector.tensor_reduce(top, pl, X, ALU.max))
                link(nc.vector.tensor_tensor(lg[:], pl, over(top), ALU.subtract))
                dve.wait_ge(ex_ready, 1)
                link(nc.vector.tensor_reduce(tot, ex[:], X, ALU.add))
                link(nc.vector.reciprocal(rtot, tot))
                link(nc.vector.tensor_tensor(gates[:], ex[:], over(rtot), ALU.mult))
                dve.wait_ge(rank_ready, 1)
                ranks = rank[:].unsqueeze(1).to_broadcast([P, NT, E])
                link(nc.vector.tensor_reduce(top, gates[:], X, ALU.max))
                link(nc.vector.tensor_tensor(keys[:], gates[:], over(top), ALU.is_equal))
                link(nc.vector.tensor_tensor(keys[:], keys[:], ranks, ALU.mult))
                link(nc.vector.tensor_reduce(k1, keys[:], X, ALU.max))
                link(nc.vector.tensor_tensor(one1[:], keys[:], over(k1), ALU.is_equal))
                link(nc.vector.scalar_tensor_tensor(rest[:].rearrange("p t e -> p (t e)"), one1[:].rearrange("p t e -> p (t e)"), -4.0,
                                                    gates[:].rearrange("p t e -> p (t e)"), ALU.mult, ALU.add))
                link(nc.vector.tensor_reduce(top2, rest[:], X, ALU.max))
                link(nc.vector.tensor_tensor(keys[:], rest[:], over(top2), ALU.is_equal))
                link(nc.vector.tensor_tensor(keys[:], keys[:], ranks, ALU.mult))
                link(nc.vector.tensor_reduce(k2, keys[:], X, ALU.max))
                link(nc.vector.tensor_tensor(one2[:], keys[:], over(k2), ALU.is_equal))
                link(nc.vector.tensor_tensor(one1[:], one1[:], one2[:], ALU.add))
                link(nc.vector.tensor_tensor(gates[:], gates[:], one1[:], ALU.mult))
                link(nc.vector.tensor_reduce(tot, gates[:], X, ALU.add))
                link(nc.vector.tensor_scalar(tot, tot, 1e-20, None, ALU.add))
                link(nc.vector.reciprocal(rtot, tot))
                link(nc.vector.tensor_tensor(gate[:], gates[:], over(rtot), ALU.mult))

                def low_weights(n, e):
                    for i in range(3):
                        dve.wait_ge(whi_ready, 3 * n + i + 1)
                        for r, k in split_rows(i):
                            ins = nc.vector.tensor_tensor(wl[e][i][r, k, :], stg[i][r, k, :], wh[e][i][r, k, :].bitcast(F32), ALU.subtract)
                        ins.then_inc(wlo_ready, 1)

                def hidden(n, e, c):
                    m = JOBS * n + c
                    first = isinstance(m, int) and m == 0
                    for f, (_, w) in enumerate(FT):
                        dve.wait_ge(sil_ready, NF * m + f + 1)
                        if not first:
                            dve.wait_ge(hl_ready, NF * m + f + 1 - NF)
                        nc.vector.tensor_tensor(hr[0:w, f, :], sil[0:w, f, :], psum[0:w, f, J:2 * J], ALU.mult).then_inc(hr_ready, 1)
                        dve.wait_ge(hh_ready, NF * m + f + 1)
                        nc.vector.tensor_tensor(hl[0:w, f, :], hr[0:w, f, :], hh[0:w, f, :].bitcast(F32), ALU.subtract).then_inc(hl_ready, 1)
                    if not first:
                        dve.wait_ge(acc_done, 2 * m)
                    for t in range(2):
                        dve.wait_ge(dn_ps, 2 * m + t + 1)
                        row = xs[:, ds(2 * c + t, 1), :].rearrange("p a c -> p (a c)")
                        if isinstance(n, int) and n >= E:
                            ins = nc.vector.tensor_tensor(row, row, psum[:, DN + t, :], ALU.add)
                        else:
                            g = gate[:].rearrange("p t e -> p (t e)")[:, ds((2 * c + t) * E + n, 1)]
                            ins = nc.vector.scalar_tensor_tensor(row, psum[:, DN + t, :], g, row, ALU.mult, ALU.add)
                        ins.then_inc(acc_done, 1)

                low_weights(0, 0)
                all_units(dve, hidden, low_weights)

                dve.wait_ge(acc_done, 2 * JOBS * UNITS)
                for u in range(NT):
                    ins = nc.vector.bn_stats(stats3[:, u, :], xs[:, u, :])
                link(ins)
                for u in range(NT):
                    ins = nc.vector.bn_aggr(mv3[:, u, :], stats3[:, u, :])
                link(ins)
                link(nc.vector.tensor_scalar(ve3[:], mv3[:, :, 1], LN_EPS, None, ALU.add))
                assert chain3[0] == 25, chain3[0]
                dve.wait_ge(g3_ready, 1)
                link(nc.vector.tensor_tensor(m1[:], g3[:], g3[:], ALU.mult))
                link(nc.vector.tensor_tensor(m2[:], m1[:], ve3[:], ALU.mult))
                link(nc.vector.tensor_scalar(m1[:], m2[:], -0.5, 1.5, ALU.mult, ALU.add))
                link(nc.vector.tensor_tensor(rstd3[:], m1[:], g3[:], ALU.mult))
                for u in range(NT):
                    ins = nc.vector.tensor_scalar(xs[:, u, :], xs[:, u, :], mv3[:, u, 0:1], rstd3[:, u:u + 1], ALU.subtract, ALU.mult)
                ins.then_inc(x3_done, 1)

            @block.tensor
            def _(pe):
                mm = nc.tensor.matmul
                for t in range(NT):
                    if t >= 8:
                        pe.wait_ge(xl_ready, t - 7)
                    for k in range(KC):
                        ins = nc.tensor.transpose(psum[:, t % 8, k * P:(k + 1) * P], xs[:, t, k * P:(k + 1) * P], ident[:])
                    ins.then_inc(xt_ps, 1)
                pe.wait_ge(xl_ready, NT)
                pe.wait_ge(s_r, 16)
                for k in range(KC):
                    ins = nc.tensor.transpose(psum[:, 0, k * E:(k + 1) * E], rin[:, k * P:(k + 1) * P], ident[0:E, 0:E])
                ins.then_inc(rt_ps, 1)
                pe.wait_ge(rt_ready, 1)
                for t in range(NT):
                    for k in range(KC):
                        for xx, rr in ((xh, rth), (xl, rth), (xh, rtl)):
                            ins = mm(psum[:, 1, t * E:(t + 1) * E], xx[:, k, t * P:(t + 1) * P], rr[:, k, :],
                                     start=(k == 0 and xx is xh and rr is rth), stop=(k == KC - 1 and rr is rtl))
                ins.then_inc(lg_ps, 1)
                pe.wait_ge(own3, 2)

                def hidden(n, e, c):
                    m = JOBS * n + c
                    first = isinstance(m, int) and m == 0
                    if isinstance(c, int) and c == 0:
                        pe.wait_ge(wlo_ready, 3 * n + 3)
                    for f, (f0, w) in enumerate(FT):
                        if not first:
                            pe.wait_ge(hr_ready, NF * m + f + 1 - NF)
                        for i in range(2):
                            for k in range(KC):
                                for ww, xx in ((wh, xh), (wh, xl), (wl, xh)):
                                    ins = mm(psum[0:w, f, i * J:(i + 1) * J], ww[e][i][:, k, f0:f0 + w], xx[:, k, ds(J * c, J)],
                                             start=(k == 0 and ww is wh and xx is xh), stop=(k == KC - 1 and ww is wl))
                        ins.then_inc(gu_ps, 1)
                    for f, (f0, w) in enumerate(FT):
                        pe.wait_ge(hl_ready, NF * m + f + 1)
                        for t in range(2):
                            if f == 0 and t == 0 and not first:
                                pe.wait_ge(acc_done, 2 * m)
                            for aa, ww in ((hh, wh), (hl, wh), (hh, wl)):
                                ins = mm(psum[:, DN + t, :], aa[0:w, f, t * P:(t + 1) * P], ww[e][2][0:w, f, :],
                                         start=(f == 0 and aa is hh and ww is wh), stop=(f == NF - 1 and ww is wl))
                            if f == NF - 1:
                                ins.then_inc(dn_ps, 1)

                all_units(pe, hidden, None)


_NAMES = {"x": "x", "ctx": "ctx_2048", "w_qkv": "L0_attn_w_qkv", "w_proj": "L0_attn_w_proj", "ssm": "L0_xattn_ssm_kernel",
          "D": "L0_xattn_D", "router": "L0_ffn_router_w", "wg": "L0_ffn_wg", "wu": "L0_ffn_wu", "wd": "L0_ffn_wd",
          "sg": "L0_ffn_sg", "su": "L0_ffn_su", "sd": "L0_ffn_sd"}


def kernel(**inputs):
    import numpy as _np
    import concourse.bacc as _bacc
    from concourse.bass_utils import run_bass_kernel_spmd as _run

    nc = _bacc.Bacc("TRN2", target_bir_lowering=False, num_devices=1)
    arrays, aps = {}, {}
    for short, name in _NAMES.items():
        a = _np.ascontiguousarray(inputs[name])
        arrays[f"in_{short}"] = a
        aps[short] = nc.dram_tensor(f"in_{short}", a.shape, mybir.dt.from_np(a.dtype), kind="ExternalInput").ap()
    shape = inputs["x"].shape
    aps["out"] = nc.dram_tensor("out", shape, F32, kind="ExternalOutput").ap()
    build(nc, aps)
    r = _run(nc, [arrays], core_ids=[0])
    return r.results[0]["out"]
```

```python
from contextlib import ExitStack

import concourse.bass as bass
from concourse import mybir

STAGE = 3

F32 = mybir.dt.float32
F32R = mybir.dt.float32r
BF16 = mybir.dt.bfloat16
I32 = mybir.dt.int32
ALU = mybir.AluOpType
ACT = mybir.ActivationFunctionType
X = mybir.AxisListType.X
ds = bass.ds

P = 128
MAGIC = 12582912.0
MASKED = -1.0e30
LN_EPS = 1e-05


def build(nc, A):
    B, N, C = A["x"].shape
    H, DH = 16, C // 16
    TB = N // P
    NT = B * TB
    KC = C // P
    OG = 2 * C // P
    HG = P // DH
    NG = H // HG
    PAIRS = H // 2
    WT = 3 * C // P
    WALL = WT + C // P
    WCH = 4
    SCALE = float(DH) ** -0.5
    HK, L = A["ssm"].shape
    KP = P + L
    LB = L // P
    I = N // HK
    E, _, F = A["wg"].shape
    J = 2 * P
    JT = J // P
    RJOBS = (2 * NT * P + E * (J - 1)) // J
    VW = DH + 1

    x_tok = A["x"].rearrange("b (t p) c -> p (b t) c", p=P)
    ctx_tok = A["ctx"].rearrange("b (t p) c -> p (b t) c", p=P)
    out_tok = A["out"].rearrange("b (t p) c -> p (b t) c", p=P)
    wqkv_v = A["w_qkv"].rearrange("(t p) c -> p t c", p=P)
    xg = nc.dram_tensor("xg", (RJOBS, J, C), F32, kind="Internal").ap()
    yg = nc.dram_tensor("yg", (RJOBS, J, C), F32, kind="Internal").ap()
    xg_rows = xg.rearrange("r j c -> (r j) c")
    yg_rows = yg.rearrange("r j c -> (r j) c")
    wproj_v = A["w_proj"].rearrange("(t p) c -> p t c", p=P)

    with ExitStack() as ctx:
        where = [(nc.sbuf_base + 31) // 32 * 32]

        def sb(name, shape, dt=F32):
            size = 4 if dt in (F32, F32R, I32) else 2
            for n in shape[1:]:
                size *= n
            size = (size + 31) // 32 * 32
            where[0] += size
            assert where[0] <= nc.sbuf_usable_end, (name, where[0])
            return nc.alloc_sbuf_tensor_at(name, shape, dt, offset=where[0] - size)

        def sem(name):
            return ctx.enter_context(nc.semaphore(name))

        xs = sb("xs", [P, NT, C])
        ident = sb("ident", [P, P])
        identb = sb("identb", [P, P], BF16)
        ones = sb("ones", [P, P])
        below = sb("below", [P, P])
        rank = sb("rank", [P, E])
        job_no = sb("job_no", [P, RJOBS])
        mhalf = sb("mhalf", [P, NT])
        psum = ctx.enter_context(nc.psum_tensor("psum", [P, 8, 512], F32))

        mark_b = where[0]
        wT = sb("wT", [P, KC, WALL * P], BF16)
        wsum = sb("wsum", [P, WALL])
        wtot = sb("wtot", [P, 2])
        wmean = sb("wmean", [P, 2])
        wscale = sb("wscale", [P, 2])
        mask_st = sb("mask_st", [P, P], BF16)
        mask_s = sb("mask_s", [P, P], BF16)
        xq_t = sb("xq_t", [P, TB, C])
        xq = sb("xq", [P, TB, C], BF16)
        amax = sb("amax", [P, TB])
        inv = sb("inv", [P, TB])
        qs_r = sb("qs_r", [P, TB])
        qs = sb("qs", [P, TB])
        vinv = sb("vinv", [P, TB])
        xqT = sb("xqT", [P, KC, N], BF16)
        rs = sb("rs", [P, N])
        real = sb("real", [P, OG, N])
        hi = sb("hi", [P, OG, N], F32R)
        lo = real[:].bitcast(F32R)
        VPAD = 64
        vx = [sb(f"vx{i}", [P, TB, H * VW + VPAD - VW]) for i in range(2)]
        ot = sb("ot", [P, 2, N])
        orow = sb("orow", [P, 2, 2, TB, P])
        cx = sb("cx", [P, TB, H])
        ct = sb("ct", [H, N], F32R)
        pt = sb("pt", [P, 2, 2, N + P])
        attn = sb("attn", [P, TB, C])
        amax2 = sb("amax2", [P, TB])
        inv2 = sb("inv2", [P, TB])
        qs2_r = sb("qs2_r", [P, TB])
        qs2 = sb("qs2", [P, TB])
        pscale = sb("pscale", [P, 2, TB])
        aq = sb("aq", [P, TB, C], BF16)
        aT = sb("aT", [P, KC, N], BF16)
        resid = sb("resid", [P, TB, C])
        stats = sb("stats", [P, TB, 6])
        mv = sb("mv", [P, TB, 2])
        ve = sb("ve", [P, TB])
        r0 = sb("r0", [P, TB])
        nt1 = sb("nt1", [P, TB])
        nt2 = sb("nt2", [P, TB])
        rstd = sb("rstd", [P, TB])

        cin_at = where[0]
        zero = sb("zero", [P, C])
        kin = sb("kin", [HK, KP])
        dcol = sb("dcol", [HK, 1])
        khl = sb("khl", [HK, 2, KP], F32R)
        krow = nc.dram_tensor("krow", (HK, 2, KP), F32, kind="Internal").ap()
        where[0] = cin_at
        cin = sb("cin", [P, NT, C])
        wraw_at = where[0]
        wraw = sb("wraw", [P, WALL, C])
        wtern = sb("wtern", [P, WALL, C], BF16)
        where[0] = wraw_at
        qst = [sb(f"qst{i}", [P, H, N], F32R) for i in range(2)]
        kst = [sb(f"kst{i}", [P, H, N], F32R) for i in range(2)]
        end_a = where[0]
        KS = 3 * DH
        rec = sb("rec", [P, NG, TB, 2, 2])
        STACK = 16 * 6 * HG

        s_const = sem("s_const")
        s_w = [sem(f"s_w{i}") for i in range(WALL // WCH)]
        s_x = [sem("s_x0"), sem("s_x1")]
        s_dve = sem("s_dve")
        s_wsum = sem("s_wsum")
        s_wtot_ps = sem("s_wtot_ps")
        s_tern = sem("s_tern")
        s_wT_ps = sem("s_wT_ps")
        s_wT = sem("s_wT")
        xq_ready = sem("xq_ready")
        xT_ps = sem("xT_ps")
        xT_sb = sem("xT_sb")
        r_ps = sem("r_ps")
        r_sb = sem("r_sb")
        qk_ps = sem("qk_ps")
        v_ps = sem("v_ps")
        v_sb = sem("v_sb")
        real_ready = sem("real_ready")
        hi_ready = sem("hi_ready")
        lo_ready = sem("lo_ready")
        s_ps = sem("s_ps")
        mx_done = sem("mx_done")
        c_ps = sem("c_ps")
        ct_ready = sem("ct_ready")
        st_ps = sem("st_ps")
        s_stack = [sem("s_stack0"), sem("s_stack1")]
        s_crow = sem("s_crow")
        ones_row = sem("ones_row")
        ot_ready = sem("ot_ready")
        tv_ps = sem("tv_ps")
        orow_ready = sem("orow_ready")
        exp_done = sem("exp_done")
        pv_done = sem("pv_done")
        na_done = sem("na_done")
        aq_ready = sem("aq_ready")
        aT_ps = sem("aT_ps")
        aT_sb = sem("aT_sb")
        proj_ps = sem("proj_ps")
        res_done = sem("res_done")
        var_ready = sem("var_ready")
        r0_ready = sem("r0_ready")
        x1_done = sem("x1_done")
        s_k = sem("s_k")
        k_ready = sem("k_ready")
        k_chain = sem("k_chain")
        s_krow = sem("s_krow")
        s_cin = sem("s_cin")
        s_out = sem("s_out")
        s_zero = sem("s_zero")

        own_sem = {n: sem("own_" + n) for n in (
            'amax', 'clip', 'rec', 'scale', 'round', 'stats', 'aggr', 'nt1', 'nt2', 'nt3', 'nt4', 'srec', 'amax2', 'clip2', 'rec2', 'scale2', 'round2')}
        chain = [0]

        def bankbf(k):
            return psum[:, k, :].bitcast(BF16)

        def stacked(b, e, each):
            return each // 2 * b + each - each // 2 * e

        def all_batches(eng, batch):
            batch(0, 0)
            batch(1, 1)
            with eng.Fori(1, B // 2 - 1) as i:
                for e in range(2):
                    batch(2 * i + e, e)
            batch(B - 2, 0)
            batch(B - 1, 1)

        stage_a = nc.Block()
        block = stage_a.__enter__()

        @block.sync
        def _(sp):
            sp.dma_start(wraw[:, 0:WCH, :], wqkv_v[:, 0:WCH, :]).then_inc(s_w[0], 16)
            sp.dma_start(xs[:, 0:TB, :], x_tok[:, 0:TB, :]).then_inc(s_x[0], 16)
            for i in range(1, WT // WCH):
                sp.dma_start(wraw[:, i * WCH:(i + 1) * WCH, :], wqkv_v[:, i * WCH:(i + 1) * WCH, :]).then_inc(s_w[i], 16)
            sp.dma_start(wraw[:, WT:WALL, :], wproj_v).then_inc(s_w[WT // WCH], 16)
            sp.dma_start(xs[:, TB:NT, :], x_tok[:, TB:NT, :]).then_inc(s_x[1], 16)
            sp.dma_start(kin[:, P:KP], A["ssm"]).then_inc(s_k, 16)
            sp.dma_start(dcol[:], A["D"].rearrange("(h a) -> h a", a=1)).then_inc(s_k, 16)

            def stack(b, e):
                if not (isinstance(b, int) and b < 2):
                    sp.wait_ge(st_ps, PAIRS * (b - 1))
                if isinstance(b, int) and b < 2:
                    sp.wait_ge(s_wT, WALL // 2)
                hif, lof = hi[:].bitcast(F32), real[:]
                for done, ready, n, src, g0, dst, at in (
                        (s_stack, hi_ready, OG // 4, hif, 0, qst, 0), (s_stack, hi_ready, OG // 2, hif, NG, kst, 0),
                        (s_stack, hi_ready, OG // 2, hif, NG, kst, 1), (s_stack, lo_ready, OG // 4, lof, 0, qst, 1),
                        (s_stack, lo_ready, OG // 2, lof, NG, kst, 2), (s_stack, hi_ready, OG // 2, hif, 0, qst, 2)):
                    sp.wait_ge(ready, OG // 2 * b + n)
                    for j in range(HG):
                        to = dst[e][DH * at:DH * (at + 1)].rearrange("p (g j) n -> p g j n", j=HG)[:, :, j, :].bitcast(F32)
                        sp.dma_start(to, src[DH * j:DH * (j + 1), g0:g0 + NG, :]).then_inc(done[e], 16)

            def max_row(b, e):
                sp.wait_ge(ct_ready, b + 1)
                sp.dma_start(qst[e][KS:KS + 1].bitcast(F32), ct[:].bitcast(F32)).then_inc(s_crow, 16)

            def ahead(b, e):
                max_row(b + 1, 1 - e)
                if not (isinstance(b, int) and b + 2 >= B):
                    stack(b + 2, e)
            stack(0, 0)
            max_row(0, 0)
            stack(1, 1)
            ahead(0, 0)
            sp.wait_ge(s_const, 9)
            sp.dma_start(xg_rows.rearrange("(n p) c -> p n c", p=P), zero[:].unsqueeze(1).to_broadcast([P, RJOBS * JT, C])).then_inc(s_zero, 16)
            sp.wait_ge(k_ready, 3)
            sp.dma_start(krow, khl[:].bitcast(F32)).then_inc(s_krow, 16)
            ahead(1, 1)
            sp.wait_ge(s_krow, 16)
            sp.wait_ge(s_zero, 16)
            sp.dma_start(cin[:], ctx_tok).then_inc(s_cin, 16)
            with sp.Fori(1, B // 2 - 1) as i:
                for e in range(2):
                    ahead(2 * i + e, e)
            ahead(B - 2, 0)
            sp.wait_ge(s_cin, 16)
            if STAGE == 1:
                sp.wait_ge(x1_done, B)
                sp.dma_start(out_tok, xs[:]).then_inc(s_out, 16)
                sp.wait_ge(s_out, 16)

        @block.gpsimd
        def _(pool):
            nc.gpsimd.memset(ones[:], 1.0).then_inc(s_const, 1)
            nc.gpsimd.memset(ident[:], 0.0).then_inc(s_const, 1)
            nc.gpsimd.memset(mask_st[:], 0.0).then_inc(s_const, 1)
            nc.gpsimd.memset(mask_s[:], 0.0).then_inc(s_const, 1)
            nc.gpsimd.memset(vx[0][:], 1.0)
            nc.gpsimd.memset(vx[1][:], 1.0).then_inc(s_const, 1)
            nc.gpsimd.memset(cx[:], 0.0).then_inc(s_const, 1)
            nc.gpsimd.memset(zero[:], 0.0).then_inc(s_const, 1)
            nc.gpsimd.memset(below[:], 1.0).then_inc(s_const, 1)
            nc.gpsimd.memset(mhalf[:], -0.5).then_inc(s_const, 1)
            for e in range(E):
                nc.gpsimd.memset(rank[:, e:e + 1], float(E - e))
            for r in range(RJOBS):
                ins = nc.gpsimd.memset(job_no[:, r:r + 1], float(r))
            ins.then_inc(s_const, 1)
            pool.wait_ge(s_const, 10)
            nc.gpsimd.affine_select(out=below[:], in_=below[:], compare_op=ALU.is_gt, fill=0.0, base=0,
                                    pattern=[[1, P]], channel_multiplier=-1).then_inc(s_const, 1)
            nc.gpsimd.affine_select(out=ident[:], in_=ident[:], compare_op=ALU.not_equal, fill=1.0, base=0,
                                    pattern=[[-1, P]], channel_multiplier=1).then_inc(s_const, 1)
            nc.gpsimd.affine_select(out=mask_st[:], in_=mask_st[:], compare_op=ALU.is_ge, fill=MASKED, base=0,
                                    pattern=[[1, P]], channel_multiplier=-1).then_inc(s_const, 1)
            nc.gpsimd.affine_select(out=mask_s[:], in_=mask_s[:], compare_op=ALU.is_ge, fill=MASKED, base=0,
                                    pattern=[[-1, P]], channel_multiplier=1).then_inc(s_const, 1)

            nc.gpsimd.memset(kin[:, 0:P], 0.0).then_inc(k_ready, 1)
            pool.wait_ge(s_k, 32)
            pool.wait_ge(k_ready, 1)
            nc.gpsimd.tensor_tensor(kin[:, P:P + 1], kin[:, P:P + 1], dcol[:], ALU.add).then_inc(k_chain, 1)
            pool.wait_ge(k_chain, 1)
            nc.gpsimd.tensor_copy(khl[:, 0, :], kin[:]).then_inc(k_ready, 1)
            pool.wait_ge(k_ready, 2)
            nc.gpsimd.tensor_tensor(khl[:, 1, :], kin[:], khl[:, 0, :].bitcast(F32), ALU.subtract).then_inc(k_ready, 1)

            def low_parts(b):
                for k in range(OG // 2):
                    pool.wait_ge(hi_ready, OG // 2 * b + k + 1)
                    part = slice(2 * k, 2 * k + 2)
                    nc.gpsimd.tensor_tensor(lo[:, part, :], real[:, part, :], hi[:, part, :].bitcast(F32),
                                            ALU.subtract).then_inc(lo_ready, 1)

            def rstd_guess(b):
                pool.wait_ge(var_ready, b + 1)
                nc.gpsimd.tensor_tensor(r0[:], ve[:], mhalf[:, 0:TB], ALU.pow).then_inc(r0_ready, 1)

            low_parts(0)
            pool.wait_ge(lo_ready, OG // 2)
            pool.wait_ge(s_wT, WALL // 2)
            for e in range(2):
                nc.gpsimd.memset(kst[e][KS:KS + 1].bitcast(F32), 1.0).then_inc(ones_row, 1)
                pool.wait_ge(ones_row, e + 1)
            low_parts(1)

            def batch(b, e):
                if not (isinstance(b, int) and b == 0):
                    rstd_guess(b - 1)
                if not (isinstance(b, int) and b + 2 >= B):
                    low_parts(b + 2)
            all_batches(pool, batch)
            rstd_guess(B - 1)

        @block.scalar
        def _(act):
            for i in range(WALL // 2):
                act.wait_ge(s_wT_ps, i + 1)
                nc.scalar.activation(wT[:, :, 2 * i * P:(2 * i + 2) * P].rearrange("p k (t o) -> p t k o", o=P),
                                     bankbf(i % 8)[:, 0:2 * KC * P].rearrange("p (t k o) -> p t k o", t=2, k=KC),
                                     ACT.Copy).then_inc(s_wT, 1)

            def evacuate_inputs(b, e):
                act.wait_ge(xT_ps, b + 1)
                nc.scalar.activation(xqT[:].rearrange("p k (t n) -> p t k n", n=P),
                                     bankbf(6).rearrange("p (t k n) -> p t k n", t=TB, k=KC), ACT.Copy).then_inc(xT_sb, 1)
                act.wait_ge(r_ps, b + 1)
                nc.scalar.activation(rs[:], psum[:, 7, 0:N], ACT.Copy).then_inc(r_sb, 1)
                for k in range(OG // 2):
                    act.wait_ge(real_ready, OG // 2 * b + k + 1)
                    if k == 0 and not (isinstance(b, int) and b == 0):
                        act.wait_ge(s_stack[1 - e], stacked(b - 1, 1 - e, STACK))
                    nc.scalar.activation(hi[:, 2 * k:2 * k + 2, :], real[:, 2 * k:2 * k + 2, :], ACT.Copy).then_inc(hi_ready, 1)
                for t in range(TB):
                    act.wait_ge(v_ps, TB * b + t + 1)
                    nc.scalar.activation(vx[e][:, t, 0:H * VW].rearrange("p (h v) -> p h v", v=VW)[:, :, 0:DH], psum[:, 6 + t, :].rearrange("p (h d) -> p h d", d=DH),
                                         ACT.Copy, scale=vinv[:, t:t + 1]).then_inc(v_sb, 1)

            def attn_columns(b):
                act.wait_ge(aT_ps, b + 1)
                nc.scalar.activation(aT[:].rearrange("p k (t n) -> p t k n", n=P),
                                     bankbf(6).rearrange("p (t k n) -> p t k n", t=TB, k=KC), ACT.Copy).then_inc(aT_sb, 1)

            def max_columns(b):
                act.wait_ge(c_ps, b + 1)
                if not (isinstance(b, int) and b == 0):
                    act.wait_ge(s_crow, 16 * b)
                nc.scalar.activation(ct[:], psum[0:H, 4, 0:N], ACT.Copy, scale=-1.0).then_inc(ct_ready, 1)

            def values_out(b, p):
                act.wait_ge(pv_done, PAIRS * b + p + 1)
                if not (isinstance(b, int) and b == 0 and p < 2):
                    if p % 2:
                        act.wait_ge(tv_ps, NG * b + p // 2)
                nc.scalar.activation(ot[:, p % 2], psum[:, 4, 0:N], ACT.Copy).then_inc(ot_ready, 1)

            def rows_out(b, g):
                act.wait_ge(tv_ps, NG * b + g + 1)
                if not (isinstance(b, int) and b == 0 and g < 2):
                    act.wait_ge(na_done, NG * b + g - 1)
                nc.scalar.activation(orow[:, g % 2].rearrange("p a t v -> p (a t v)"), psum[:, 5, :], ACT.Copy).then_inc(orow_ready, 1)

            def softmax(b):
                for p in range(PAIRS):
                    n = PAIRS * b + p
                    act.wait_ge(st_ps, n + 1)
                    if not (isinstance(b, int) and n < 2):
                        act.wait_ge(pv_done, n - 1)
                    s = 2 * (p % 2)
                    nc.scalar.activation(pt[:, p % 2], psum[:, s:s + 2, 0:N + P], ACT.Exp, scale=SCALE).then_inc(exp_done, 1)
                    if p:
                        values_out(b, p - 1)
                    if p >= 3 and p % 2:
                        rows_out(b, (p - 3) // 2)
                values_out(b, PAIRS - 1)
                rows_out(b, NG - 1)

            def batch(b, e):
                softmax(b)
                if not (isinstance(b, int) and b == B - 1):
                    max_columns(b + 1)
                if not (isinstance(b, int) and b + 2 >= B):
                    evacuate_inputs(b + 2, e)
                attn_columns(b)

            evacuate_inputs(0, 0)
            max_columns(0)
            evacuate_inputs(1, 1)
            all_batches(act, batch)

        @block.vector
        def _(dve):
            def link(ins):
                chain[0] += 1
                ins.then_inc(s_dve, 1)
                dve.wait_ge(s_dve, chain[0])

            dve.wait_ge(s_const, 14)
            link(nc.vector.tensor_copy(identb[:], ident[:]))
            for i in range(WALL // WCH):
                dve.wait_ge(s_w[i], 16)
                ins = nc.vector.tensor_reduce(wsum[:, i * WCH:(i + 1) * WCH], wraw[:, i * WCH:(i + 1) * WCH, :], X, ALU.add,
                                              apply_absolute_value=True)
            link(ins)
            nc.vector.tensor_reduce(wtot[:, 0:1], wsum[:, 0:WT], X, ALU.add)
            nc.vector.tensor_reduce(wtot[:, 1:2], wsum[:, WT:WALL], X, ALU.add).then_inc(s_wsum, 1)
            dve.wait_ge(s_wtot_ps, 1)
            nc.vector.tensor_scalar(wmean[:, 0:1], psum[:, 0, 0:1], 1.0 / (3 * C * C), 1e-05, ALU.mult, ALU.max)
            link(nc.vector.tensor_scalar(wmean[:, 1:2], psum[:, 0, 1:2], 1.0 / (C * C), 1e-05, ALU.mult, ALU.max))
            link(nc.vector.reciprocal(wscale[:], wmean[:]))
            for i in range(WALL // WCH):
                part = slice(i * WCH, (i + 1) * WCH)
                w = 0 if i < WT // WCH else 1
                link(nc.vector.tensor_scalar(wraw[:, part, :], wraw[:, part, :], wscale[:, w:w + 1], MAGIC, ALU.mult, ALU.add))
                link(nc.vector.tensor_scalar(wraw[:, part, :], wraw[:, part, :], MAGIC, 1.0, ALU.subtract, ALU.min))
                nc.vector.tensor_scalar(wtern[:, part, :], wraw[:, part, :], -1.0, None, ALU.max).then_inc(s_tern, 1)

            def step(b, name, ins):
                ins.then_inc(own_sem[name], 1)
                dve.wait_ge(own_sem[name], b + 1)

            def quantize(b):
                x_in = xs[:, ds(TB * b, TB), :]
                if isinstance(b, int):
                    dve.wait_ge(s_x[min(b, 1)], 16)
                if not (isinstance(b, int) and b == 0):
                    dve.wait_ge(v_sb, TB * b)
                step(b, "amax", nc.vector.tensor_reduce(amax[:], x_in, X, ALU.max, apply_absolute_value=True))
                step(b, "clip", nc.vector.tensor_scalar(amax[:], amax[:], 1e-05, None, ALU.max))
                nc.vector.tensor_scalar(inv[:], amax[:], 1.0 / 127.0, None, ALU.mult)
                step(b, "rec", nc.vector.reciprocal(qs_r[:], amax[:]))
                nc.vector.tensor_scalar(vinv[:], inv[:], wmean[:, 0:1], None, ALU.mult)
                step(b, "scale", nc.vector.tensor_scalar(qs[:], qs_r[:], 127.0, None, ALU.mult))
                for t in range(TB):
                    ins = nc.vector.tensor_scalar(xq_t[:, t, :], xs[:, ds(TB * b + t, 1), :].rearrange("p a c -> p (a c)"),
                                                  qs[:, t:t + 1], MAGIC, ALU.mult, ALU.add)
                step(b, "round", ins)

            def quantize_out(b):
                nc.vector.tensor_scalar(xq[:], xq_t[:], MAGIC, 127.0, ALU.subtract, ALU.min).then_inc(xq_ready, 1)

            def scale_qk(b, e):
                dve.wait_ge(r_sb, b + 1)
                if not (isinstance(b, int) and b == 0):
                    dve.wait_ge(s_stack[1 - e], stacked(b - 1, 1 - e, STACK))
                for k in range(OG // 2):
                    dve.wait_ge(qk_ps, OG // 2 * b + k + 1)
                    nc.vector.tensor_tensor(real[:, 2 * k:2 * k + 2, :], psum[:, k, :].rearrange("p (a n) -> p a n", n=N),
                                            rs[:].unsqueeze(1).to_broadcast([P, 2, N]), ALU.mult).then_inc(real_ready, 1)

            def row_max(b, pairs):
                for p in pairs:
                    dve.wait_ge(s_ps, PAIRS * b + p + 1)
                    if p == 0 and not (isinstance(b, int) and b == 0):
                        dve.wait_ge(c_ps, b)
                    nc.vector.tensor_reduce(cx[:, 1, 2 * p:2 * p + 2], psum[:, 6:8, 0:N], X, ALU.max)
                    nc.vector.tensor_reduce(cx[:, 0, 2 * p:2 * p + 2], psum[:, 6:8, N:N + P], X, ALU.max).then_inc(mx_done, 1)

            def residual(b):
                if not (isinstance(b, int) and b == 0):
                    dve.wait_ge(x1_done, b)
                for t in range(TB):
                    dve.wait_ge(proj_ps, TB * b + t + 1)
                    row = xs[:, ds(TB * b + t, 1), :].rearrange("p a c -> p (a c)")
                    ins = nc.vector.scalar_tensor_tensor(resid[:, t, :], psum[:, 7 - t, :], pscale[:, 1, t:t + 1], row, ALU.mult, ALU.add)
                    ins.then_inc(res_done, 1)

            def statistics(b):
                for t in range(TB):
                    dve.wait_ge(res_done, TB * b + t + 1)
                    ins = nc.vector.bn_stats(stats[:, t, :], resid[:, t, :])
                ins.then_inc(own_sem["stats"], 1)
                dve.wait_ge(own_sem["stats"], b + 1)

            def variance(b):
                for t in range(TB):
                    ins = nc.vector.bn_aggr(mv[:, t, :], stats[:, t, :])
                step(b, "aggr", ins)
                nc.vector.tensor_scalar(ve[:], mv[:, :, 1], LN_EPS, None, ALU.add).then_inc(var_ready, 1)

            def normalise(b):
                dve.wait_ge(r0_ready, b + 1)
                step(b, "nt1", nc.vector.tensor_tensor(nt1[:], r0[:], r0[:], ALU.mult))
                step(b, "nt2", nc.vector.tensor_tensor(nt2[:], nt1[:], ve[:], ALU.mult))
                step(b, "nt3", nc.vector.tensor_scalar(nt1[:], nt2[:], -0.5, 1.5, ALU.mult, ALU.add))
                step(b, "nt4", nc.vector.tensor_tensor(rstd[:], nt1[:], r0[:], ALU.mult))
                for t in range(TB):
                    row = xs[:, ds(TB * b + t, 1), :].rearrange("p a c -> p (a c)")
                    ins = nc.vector.tensor_scalar(row, resid[:, t, :], mv[:, t, 0:1], rstd[:, t:t + 1], ALU.subtract, ALU.mult)
                ins.then_inc(x1_done, 1)

            def attention_rows(b, g):
                dve.wait_ge(orow_ready, NG * b + g + 1)
                o = orow[:, g % 2].rearrange("p a t (x v) -> p t a x v", v=VPAD)
                ins = nc.vector.reciprocal(rec[:, g], o[:, :, :, :, DH])
                ins.then_inc(own_sem["srec"], 1)
                dve.wait_ge(own_sem["srec"], NG * b + g + 1)
                for t in range(TB):
                    ins = nc.vector.tensor_tensor(
                        attn[:, t, g * P:(g + 1) * P].rearrange("p (a x d) -> p a x d", a=2, d=DH), o[:, t, :, :, 0:DH],
                        rec[:, g, t].unsqueeze(3).to_broadcast([P, 2, 2, DH]), ALU.mult)
                ins.then_inc(na_done, 1)

            def quantize_rows(b):
                dve.wait_ge(na_done, NG * b + NG)
                step(b, "amax2", nc.vector.tensor_reduce(amax2[:], attn[:], X, ALU.max, apply_absolute_value=True))
                step(b, "clip2", nc.vector.tensor_scalar(amax2[:], amax2[:], 1e-05, None, ALU.max))
                nc.vector.tensor_scalar(inv2[:], amax2[:], 1.0 / 127.0, None, ALU.mult)
                step(b, "rec2", nc.vector.reciprocal(qs2_r[:], amax2[:]))
                nc.vector.tensor_scalar(pscale[:, 1, :], inv2[:], wmean[:, 1:2], None, ALU.mult)
                step(b, "scale2", nc.vector.tensor_scalar(qs2[:], qs2_r[:], 127.0, None, ALU.mult))
                for t in range(TB):
                    ins = nc.vector.tensor_scalar(attn[:, t, :], attn[:, t, :], qs2[:, t:t + 1], MAGIC, ALU.mult, ALU.add)
                step(b, "round2", ins)
                nc.vector.tensor_scalar(aq[:], attn[:], MAGIC, 127.0, ALU.subtract, ALU.min).then_inc(aq_ready, 1)
                dve.wait_ge(aq_ready, b + 1)

            def batch(b, e):
                fixed = isinstance(b, int)
                first, final = fixed and b == 0, fixed and b == B - 1
                project_next = not (fixed and b + 2 >= B)
                if not first:
                    statistics(b - 1)
                if project_next:
                    quantize(b + 2)
                attention_rows(b, 0)
                if project_next:
                    quantize_out(b + 2)
                if not first:
                    variance(b - 1)
                    normalise(b - 1)
                if not final:
                    row_max(b + 1, range(0, 4))
                attention_rows(b, 1)
                if not final:
                    row_max(b + 1, range(4, PAIRS))
                attention_rows(b, 2)
                attention_rows(b, 3)
                quantize_rows(b)
                if project_next:
                    scale_qk(b + 2, e)
                residual(b)

            quantize(0)
            quantize_out(0)
            scale_qk(0, 0)
            row_max(0, range(PAIRS))
            quantize(1)
            quantize_out(1)
            scale_qk(1, 1)
            all_batches(dve, batch)
            statistics(B - 1)
            nc.vector.tensor_scalar(nt1[:], stats[:, :, 0], 1.0, None, ALU.mult)
            variance(B - 1)
            normalise(B - 1)

        @block.tensor
        def _(pe):
            mm = nc.tensor.matmul
            pe.wait_ge(s_wsum, 1)
            mm(psum[:, 0, 0:2], ones[:], wtot[:], start=True, stop=True).then_inc(s_wtot_ps, 1)
            for i in range(WALL // 2):
                pe.wait_ge(s_tern, 2 * i // WCH + 1)
                if i >= 8:
                    pe.wait_ge(s_wT, i - 7)
                for t in range(2):
                    for k in range(KC):
                        at = (t * KC + k) * P
                        ins = nc.tensor.transpose(bankbf(i % 8)[:, at:at + P], wtern[:, 2 * i + t, k * P:(k + 1) * P], identb[:])
                ins.then_inc(s_wT_ps, 1)
            pe.wait_ge(s_wT, WALL // 2)

            def qkv(b):
                pe.wait_ge(xq_ready, b + 1)
                if not (isinstance(b, int) and b == 0):
                    pe.wait_ge(v_sb, TB * b)
                    pe.wait_ge(mx_done, PAIRS * b)
                for t in range(TB):
                    for k in range(KC):
                        at = (t * KC + k) * P
                        ins = nc.tensor.transpose(bankbf(6)[:, at:at + P], xq[:, t, k * P:(k + 1) * P], identb[:])
                ins.then_inc(xT_ps, 1)
                for t in range(TB):
                    ins = mm(psum[:, 7, t * P:(t + 1) * P], vinv[:, t:t + 1].to_broadcast([P, P]), ident[:], start=True, stop=True)
                ins.then_inc(r_ps, 1)
                pe.wait_ge(xT_sb, b + 1)
                if isinstance(b, int) and b == 1:
                    pe.wait_ge(real_ready, OG // 2)
                elif not (isinstance(b, int) and b == 0):
                    pe.wait_ge(exp_done, PAIRS * (b - 1))
                for o in range(OG):
                    for k in range(KC):
                        ins = mm(psum[:, o // 2, (o % 2) * N:(o % 2 + 1) * N], wT[:, k, o * P:(o + 1) * P], xqT[:, k, :],
                                 start=(k == 0), stop=(k == KC - 1))
                    if o % 2:
                        ins.then_inc(qk_ps, 1)
                pe.wait_ge(r_sb, b + 1)
                for t in range(TB):
                    for k in range(KC):
                        ins = mm(psum[:, 6 + t, :], xqT[:, k, t * P:(t + 1) * P], wT[:, k, OG * P:OG * P + C],
                                 start=(k == 0), stop=(k == KC - 1))
                    ins.then_inc(v_ps, 1)

            def scores_for_max(b, e, pairs):
                for p in pairs:
                    if p == 0:
                        pe.wait_ge(s_stack[e], stacked(b, e, STACK))
                        pe.wait_ge(v_sb, TB * (b + 1))
                        if not (isinstance(b, int) and b < 2):
                            pe.wait_ge(res_done, TB * (b - 1))
                    else:
                        pe.wait_ge(mx_done, PAIRS * b + p)
                    for x in range(2):
                        bank = 6 + x
                        mm(psum[:, bank, P:2 * P], identb[:], mask_s[:], start=True, stop=False, skip_group_check=True)
                        mm(psum[:, bank, N:N + P], identb[:], mask_s[:], start=False, stop=False, skip_group_check=True)
                    for x in range(2):
                        bank = 6 + x
                        h = 2 * p + x
                        mm(psum[:, bank, 0:N], qst[e][0:KS, h, P:N], kst[e][0:KS, h, :], start=False, stop=False, skip_group_check=True)
                        ins = mm(psum[:, bank, N:N + P], qst[e][0:KS, h, 0:P], kst[e][0:KS, h, 0:P], start=False, stop=True,
                                 skip_group_check=True)
                    ins.then_inc(s_ps, 1)

            def turn_max(b):
                pe.wait_ge(mx_done, PAIRS * (b + 1))
                if not (isinstance(b, int) and b == 0):
                    pe.wait_ge(ot_ready, PAIRS * b)
                for t in range(TB):
                    ins = nc.tensor.transpose(psum[0:H, 4, t * P:(t + 1) * P], cx[:, t, :], ident[:])
                ins.then_inc(c_ps, 1)

            def project(b):
                pe.wait_ge(aq_ready, b + 1)
                for t in range(TB):
                    for k in range(KC):
                        at = (t * KC + k) * P
                        ins = nc.tensor.transpose(bankbf(6)[:, at:at + P], aq[:, t, k * P:(k + 1) * P], identb[:])
                ins.then_inc(aT_ps, 1)
                pe.wait_ge(aT_sb, b + 1)
                for t in range(TB):
                    for k in range(KC):
                        ins = mm(psum[:, 7 - t, :], aT[:, k, t * P:(t + 1) * P], wT[:, k, WT * P:WALL * P],
                                 start=(k == 0), stop=(k == KC - 1))
                    ins.then_inc(proj_ps, 1)

            def scores(b, e, p):
                if p >= 2:
                    pe.wait_ge(exp_done, PAIRS * b + p - 1)
                for x in range(2):
                    bank = 2 * (p % 2) + x
                    mm(psum[:, bank, 0:P], identb[:], mask_st[:], start=True, stop=False, skip_group_check=True)
                    mm(psum[:, bank, N:N + P], identb[:], mask_st[:], start=False, stop=False, skip_group_check=True)
                for x in range(2):
                    bank = 2 * (p % 2) + x
                    h = 2 * p + x
                    mm(psum[:, bank, 0:N], kst[e][0:KS + 1, h, 0:P], qst[e][0:KS + 1, h, :], start=False, stop=False, skip_group_check=True)
                    ins = mm(psum[:, bank, N:N + P], kst[e][0:KS + 1, h, P:N], qst[e][0:KS + 1, h, P:N], start=False, stop=True,
                             skip_group_check=True)
                ins.then_inc(st_ps, 1)

            def values(b, e, p):
                pe.wait_ge(exp_done, PAIRS * b + p + 1)
                if not (isinstance(b, int) and b == 0 and p == 0):
                    pe.wait_ge(ot_ready, PAIRS * b + p)
                for x in range(2):
                    at = (2 * p + x) * VW
                    r = slice(VPAD * x, VPAD * (x + 1))
                    mm(psum[r, 4, 0:N], vx[e][:, 0, at:at + VPAD], pt[:, p % 2, x, 0:N], start=True, stop=False, skip_group_check=True)
                    ins = mm(psum[r, 4, P:N], vx[e][:, 1, at:at + VPAD], pt[:, p % 2, x, N:N + P], start=False, stop=True,
                             skip_group_check=True)
                ins.then_inc(pv_done, 1)

            def turn_values(b, p):
                pe.wait_ge(ot_ready, PAIRS * b + p + 1)
                if p % 2 == 0 and not (isinstance(b, int) and b == 0 and p == 0):
                    pe.wait_ge(orow_ready, NG * b + p // 2)
                for t in range(TB):
                    at = (p % 2 * TB + t) * P
                    ins = nc.tensor.transpose(psum[:, 5, at:at + P], ot[:, p % 2, t * P:(t + 1) * P], ident[:])
                if p % 2:
                    ins.then_inc(tv_ps, 1)

            def batch(b, e):
                fixed = isinstance(b, int)
                final = fixed and b == B - 1
                if not final:
                    pe.wait_ge(real_ready, OG // 2 * (b + 2))
                if not (fixed and b == 0):
                    pe.wait_ge(exp_done, PAIRS * b)
                pe.wait_ge(v_sb, TB * (b + 1))
                pe.wait_ge(s_crow, 16 * (b + 1))
                pe.wait_ge(s_stack[e], stacked(b, e, STACK))
                for p in range(PAIRS):
                    scores(b, e, p)
                    late = 2 * (p - PAIRS // 2)
                    if late >= 0 and not final:
                        scores_for_max(b + 1, 1 - e, [late])
                    if p:
                        values(b, e, p - 1)
                    if late >= 0 and not final:
                        scores_for_max(b + 1, 1 - e, [late + 1])
                    if p >= 2:
                        turn_values(b, p - 2)
                values(b, e, PAIRS - 1)
                turn_values(b, PAIRS - 2)
                turn_values(b, PAIRS - 1)
                if not final:
                    turn_max(b + 1)
                if not (fixed and b + 2 >= B):
                    qkv(b + 2)
                    pe.wait_ge(v_sb, TB * (b + 3))
                elif not final:
                    pe.wait_ge(mx_done, PAIRS * (b + 2))
                project(b)

            qkv(0)
            scores_for_max(0, 0, range(PAIRS))
            turn_max(0)
            qkv(1)
            pe.wait_ge(ones_row, 2)
            all_batches(pe, batch)

        stage_a.__exit__(None, None, None)
        if STAGE == 1:
            return

        PAIRN = I * (I + 1) // 2
        off = [sum(I - r for r in range(s)) for s in range(I)]
        where[0] = mark_b
        cT = sb("cT", [P, LB, B, N])
        qT = sb("qT", [P, LB, B, N])
        mark_t = where[0]
        yT = sb("yT", [P, LB, B, N])
        kv = [sb(f"kv{i}", [P, LB * B, PAIRN]) for i in range(2)]
        kvh = [sb(f"kvh{i}", [P, LB, B * PAIRN], F32R) for i in range(2)]
        kvl = [sb(f"kvl{i}", [P, LB, B * PAIRN], F32R) for i in range(2)]
        prod = [sb(f"prod{i}", [P, LB * B, I, I]) for i in range(2)]
        toep = [sb(f"toep{i}", [P, 2, L], F32R) for i in range(2)]
        stats2 = sb("stats2", [P, NT, 6])
        mv2 = sb("mv2", [P, NT, 2])
        ve2 = sb("ve2", [P, NT])
        lnv2 = sb("lnv2", [P, NT])
        g2 = sb("g2", [P, NT])
        n1 = sb("n1", [P, NT])
        n2 = sb("n2", [P, NT])
        rstd2 = sb("rstd2", [P, NT])
        end_b = where[0]
        where[0] = max(end_b, wraw_at)
        crev = sb("crev", [P, 2, C])
        assert mark_t <= cin_at

        rev_ready = sem("rev_ready")
        cT_ps = sem("cT_ps")
        qT_ps = sem("qT_ps")
        cT_done = sem("cT_done")
        qT_done = sem("qT_done")
        s_toep = [sem("s_toep0"), sem("s_toep1")]
        kv_sq = sem("kv_sq")
        kv_ready = sem("kv_ready")
        kvh_ready = sem("kvh_ready")
        kvl_ready = sem("kvl_ready")
        y_ps = sem("y_ps")
        ym_done = sem("ym_done")
        y_done = sem("y_done")
        yT_ps = sem("yT_ps")
        res2 = sem("res2")
        own2 = sem("own2")
        ln2_act = sem("ln2_act")
        g2_ready = sem("g2_ready")
        x2_done = sem("x2_done")

        def conv_out_bank(u):
            return psum[:, u % 8, :]

        with nc.Block() as block:
            @block.sync
            def _(sp):
                def load(h, e, first):
                    if not first:
                        sp.wait_ge(y_ps, h - 1)
                    src = bass.AP(krow.tensor, 1, [[2 * KP, HK], [1, P], [KP, 2], [1, L]])[ds(h, 1)]
                    sp.dma_start(toep[e][:].bitcast(F32), src.rearrange("a p v l -> (a p) v l")).then_inc(s_toep[e], 16)
                for e in range(2):
                    load(e, e, True)
                with sp.Fori(1, HK // 2) as hp:
                    for e in range(2):
                        load(2 * hp + e, e, False)
                if STAGE == 2:
                    sp.wait_ge(x2_done, 1)
                    sp.dma_start(out_tok, xs[:]).then_inc(s_out, 16)
                    sp.wait_ge(s_out, 16)

            @block.gpsimd
            def _(pool):
                pool.wait_ge(cT_done, NT)

                def products(h, e, first):
                    if not first:
                        pool.wait_ge(kvl_ready, h - 1)
                    for s in range(1, I):
                        a = cT[:].rearrange("p k b c -> p (k b) c")
                        ins = nc.gpsimd.tensor_tensor(kv[e][:, :, off[s]:off[s] + I - s], a[:, :, ds(I * h, I - s)],
                                                      a[:, :, ds(I * h + s, I - s)], ALU.mult)
                    ins.then_inc(kv_ready, 1)

                def low_part(h, e, first):
                    pool.wait_ge(kvh_ready, h + 1)
                    if not first:
                        pool.wait_ge(y_ps, h - 1)
                    nc.gpsimd.tensor_tensor(kvl[e][:].rearrange("p k n -> p (k n)"), kv[e][:].rearrange("p a n -> p (a n)"),
                                            kvh[e][:].rearrange("p k n -> p (k n)").bitcast(F32), ALU.subtract).then_inc(kvl_ready, 1)

                products(0, 0, True)
                products(1, 1, True)
                low_part(0, 0, True)
                products(2, 0, False)
                low_part(1, 1, True)
                with pool.Fori(1, HK // 2 - 1) as hp:
                    for e in range(2):
                        products(2 * hp + e + 1, 1 - e, False)
                        low_part(2 * hp + e, e, False)
                products(HK - 1, 1, False)
                low_part(HK - 2, 0, False)
                low_part(HK - 1, 1, False)

            @block.scalar
            def _(act):
                for u in range(NT):
                    b, hc = u // 2, u % 2
                    act.wait_ge(cT_ps, u + 1)
                    nc.scalar.activation(cT[:, :, b, hc * P:(hc + 1) * P], psum[:, (2 * u) % 8, :].rearrange("p (k n) -> p k n", n=P),
                                         ACT.Copy).then_inc(cT_done, 1)
                act.wait_ge(cT_done, NT)

                def squares(h, e, first):
                    if not first:
                        act.wait_ge(kvl_ready, h - 1)
                    a = cT[:].rearrange("p k b c -> p (k b) c")
                    nc.scalar.activation(kv[e][:, :, 0:I], a[:, :, ds(I * h, I)], ACT.Square).then_inc(kv_sq, 1)

                def high_part(h, e, first):
                    act.wait_ge(kv_sq, h + 1)
                    act.wait_ge(kv_ready, h + 1)
                    if not first:
                        act.wait_ge(y_ps, h - 1)
                    nc.scalar.activation(kvh[e][:].rearrange("p k n -> p (k n)"), kv[e][:].rearrange("p a n -> p (a n)"),
                                         ACT.Copy).then_inc(kvh_ready, 1)

                def head(h, e, first):
                    squares(h, e, first)
                    high_part(h, e, first)
                for e in range(2):
                    head(e, e, True)
                with act.Fori(1, HK // 2) as hp:
                    for e in range(2):
                        head(2 * hp + e, e, False)
                act.wait_ge(own2, 3)
                nc.scalar.activation(lnv2[:], ve2[:], ACT.Ln).then_inc(ln2_act, 1)
                act.wait_ge(ln2_act, 1)
                nc.scalar.activation(g2[:], lnv2[:], ACT.Exp, scale=-0.5).then_inc(g2_ready, 1)

            @block.vector
            def _(dve):
                for u in range(NT):
                    b, hc = u // 2, u % 2
                    if u >= 2:
                        dve.wait_ge(cT_ps, u - 1)
                    nc.vector.tensor_copy(crev[:, hc, :].rearrange("p (k l) -> p k l", l=P),
                                          cin[:, u, :].rearrange("p (k l) -> p k l", l=P)[:, :, ::-1]).then_inc(rev_ready, 1)
                    dve.wait_ge(qT_ps, u + 1)
                    nc.vector.tensor_copy(qT[:, :, b, hc * P:(hc + 1) * P],
                                          psum[:, (2 * u + 1) % 8, :].rearrange("p (k n) -> p k n", n=P)).then_inc(qT_done, 1)
                dve.wait_ge(qT_done, NT)

                def scale_by_q(h, e, first):
                    dve.wait_ge(y_ps, h + 1)
                    if not first:
                        dve.wait_ge(y_done, h - 1)
                    flat = prod[e][:].rearrange("p a j i -> p a (j i)")
                    y = psum[:, 4 * e:4 * e + LB, 0:B * PAIRN].rearrange("p k (b n) -> p k b n", n=PAIRN)
                    for s in range(I):
                        ys = y[:, :, :, off[s]:off[s] + I - s]
                        last = (I - s - 1) * (I + 1) + 1
                        for shift, at in ((0, s * I), (s, s))[0:1 + (s > 0)]:
                            o = flat[:, :, at:at + last:I + 1].rearrange("p (k b) n -> p k b n", b=B)
                            ins = nc.vector.tensor_tensor(o, ys, qT[:, :, :, ds(I * h + shift, I - s)], ALU.mult)
                    ins.then_inc(ym_done, 1)

                def sum_over_i(h, e):
                    dve.wait_ge(ym_done, h + 1)
                    nc.vector.tensor_reduce(yT[:].rearrange("p k b c -> p (k b) c")[:, :, ds(I * h, I)], prod[e][:], X, ALU.add)\
                       .then_inc(y_done, 1)

                scale_by_q(0, 0, True)
                scale_by_q(1, 1, True)
                sum_over_i(0, 0)
                with dve.Fori(1, HK // 2) as hp:
                    for e in range(2):
                        scale_by_q(2 * hp + e, e, False)
                        sum_over_i(2 * hp + e - 1, 1 - e)
                sum_over_i(HK - 1, 1)

                for u in range(NT):
                    dve.wait_ge(yT_ps, u + 1)
                    nc.vector.tensor_tensor(xs[:, u, :], xs[:, u, :], conv_out_bank(u), ALU.add).then_inc(res2, 1)
                    if u:
                        dve.wait_ge(res2, u)
                        nc.vector.bn_stats(stats2[:, u - 1, :], xs[:, u - 1, :])
                dve.wait_ge(res2, NT)
                nc.vector.bn_stats(stats2[:, NT - 1, :], xs[:, NT - 1, :]).then_inc(own2, 1)
                dve.wait_ge(own2, 1)
                for u in range(NT):
                    ins = nc.vector.bn_aggr(mv2[:, u, :], stats2[:, u, :])
                ins.then_inc(own2, 1)
                dve.wait_ge(own2, 2)
                nc.vector.tensor_scalar(ve2[:], mv2[:, :, 1], LN_EPS, None, ALU.add).then_inc(own2, 1)
                dve.wait_ge(g2_ready, 1)
                nc.vector.tensor_tensor(n1[:], g2[:], g2[:], ALU.mult).then_inc(own2, 1)
                dve.wait_ge(own2, 4)
                nc.vector.tensor_tensor(n2[:], n1[:], ve2[:], ALU.mult).then_inc(own2, 1)
                dve.wait_ge(own2, 5)
                nc.vector.tensor_scalar(n1[:], n2[:], -0.5, 1.5, ALU.mult, ALU.add).then_inc(own2, 1)
                dve.wait_ge(own2, 6)
                nc.vector.tensor_tensor(rstd2[:], n1[:], g2[:], ALU.mult).then_inc(own2, 1)
                dve.wait_ge(own2, 7)
                for u in range(NT):
                    ins = nc.vector.tensor_scalar(xs[:, u, :], xs[:, u, :], mv2[:, u, 0:1], rstd2[:, u:u + 1], ALU.subtract, ALU.mult)
                ins.then_inc(x2_done, 1)

            @block.tensor
            def _(pe):
                mm = nc.tensor.matmul
                for u in range(NT):
                    if u >= 4:
                        pe.wait_ge(cT_done, u - 3)
                        pe.wait_ge(qT_done, u - 3)
                    for k in range(LB):
                        ins = nc.tensor.transpose(psum[:, (2 * u + 1) % 8, k * P:(k + 1) * P], xs[:, u, k * P:(k + 1) * P], ident[:])
                    ins.then_inc(qT_ps, 1)
                    pe.wait_ge(rev_ready, u + 1)
                    for k in range(LB):
                        ins = nc.tensor.transpose(psum[:, (2 * u) % 8, k * P:(k + 1) * P], crev[:, u % 2, k * P:(k + 1) * P], ident[:])
                    ins.then_inc(cT_ps, 1)
                pe.wait_ge(cT_done, NT)
                pe.wait_ge(qT_done, NT)

                def convolve(h, hp, e, first):
                    pe.wait_ge(s_toep[e], 16 * hp + 16)
                    pe.wait_ge(kvl_ready, h + 1)
                    if not first:
                        pe.wait_ge(ym_done, h - 1)
                    for lb in range(LB):
                        for mb in range(lb + 1):
                            d = slice((lb - mb) * P, (lb - mb + 1) * P)
                            for v, rhs in ((0, kvh), (0, kvl), (1, kvh)):
                                ins = mm(psum[:, 4 * e + lb, 0:B * PAIRN], toep[e][:, v, d], rhs[e][:, mb, :],
                                         start=(mb == 0 and v == 0 and rhs is kvh), stop=(mb == lb and v == 1))
                    ins.then_inc(y_ps, 1)
                for e in range(2):
                    convolve(e, 0, e, True)
                with pe.Fori(1, HK // 2) as hp:
                    for e in range(2):
                        convolve(2 * hp + e, hp, e, False)
                pe.wait_ge(y_done, HK)
                for u in range(NT):
                    b, hc = u // 2, u % 2
                    if u >= 8:
                        pe.wait_ge(res2, u - 7)
                    for k in range(LB):
                        ins = nc.tensor.transpose(conv_out_bank(u)[:, k * P:(k + 1) * P], yT[:, k, b, hc * P:(hc + 1) * P], ident[:])
                    ins.then_inc(yT_ps, 1)

        if STAGE == 2:
            return

        UNITS = E + A["sg"].shape[1] // F
        assert UNITS == E + 2
        FT = [(f, min(P, F - f)) for f in range(0, F, P)]
        NF = len(FT)
        where[0] = mark_b
        stg = [sb("stg_g", [P, KC, F]), sb("stg_u", [P, KC, F]), sb("stg_d", [P, NF, C])]
        over_sets, wh, wl = where[0], [], []
        for i in range(2):
            wh.append([sb(f"wh_g{i}", [P, KC, F], F32R), sb(f"wh_u{i}", [P, KC, F], F32R), sb(f"wh_d{i}", [P, NF, C], F32R)])
            wl.append([sb(f"wl_g{i}", [P, KC, F], F32R), sb(f"wl_u{i}", [P, KC, F], F32R), sb(f"wl_d{i}", [P, NF, C], F32R)])
            if i == 0:
                end_set = where[0]
        end_sets, where[0] = where[0], over_sets
        got = [sb(f"got{i}", [P, JT, 2, C]) for i in range(2)]
        fin = [sb(f"fin{i}", [P, JT, C]) for i in range(2)]
        assert where[0] <= end_set
        where[0] = end_sets
        sil = sb("sil", [P, NF, J])
        hr = sb("hr", [P, NF, J])
        hh = [sb(f"hh{i}", [P, NF, J], F32R) for i in range(2)]
        hl = [sb(f"hl{i}", [P, NF, J], F32R) for i in range(2)]
        xrow = [sb(f"xrow{i}", [P, JT, C]) for i in range(2)]
        xh = [sb(f"xh{i}", [P, KC, J], F32R) for i in range(2)]
        xl = [sb(f"xl{i}", [P, KC, J], F32R) for i in range(2)]
        yout = sb("yout", [P, JT, C])
        acc = sb("acc", [P, NT, C])
        rin = sb("rin", [E, C])
        rth = sb("rth", [P, KC, E], F32R)
        lgt = sb("lgt", [E, J])
        rtl = sb("rtl", [P, KC, E], F32R)
        lg = sb("lg", [P, NT, E])
        ex = sb("ex", [P, NT, E])
        gates = sb("gates", [P, NT, E])
        keys = sb("keys", [P, NT, E])
        rest = sb("rest", [P, NT, E])
        one1 = sb("one1", [P, NT, E])
        one2 = sb("one2", [P, NT, E])
        both = sb("both", [P, NT, E])
        slots = sb("slots", [P, NT, E])
        before_t = sb("before_t", [P, NT, E])
        count = sb("count", [P, E])
        jobs_e = sb("jobs_e", [P, E])
        end_e = sb("end_e", [P, E])
        base_e = sb("base_e", [P, E])
        le = sb("le", [P, RJOBS, E])
        exp_of = sb("exp_of", [P, RJOBS])
        exp_i = sb("exp_i", [P, RJOBS], I32)
        slot_f = sb("slot_f", [P, 2, NT])
        slot_i = sb("slot_i", [P, 2, NT], I32)
        gate = sb("gate", [P, 2, NT])
        t16 = [sb(f"t16_{i}", [P, NT]) for i in range(6)]
        stats3 = sb("stats3", [P, JT, 6])
        mv3 = [sb(f"mv3{i}", [P, JT, 2]) for i in range(2)]
        ve3 = [sb(f"ve3{i}", [P, JT]) for i in range(2)]
        g3 = sb("g3", [P, JT])
        m1 = sb("m1", [P, JT])
        m2 = sb("m2", [P, JT])
        rstd3 = [sb(f"rstd3{i}", [P, JT]) for i in range(2)]
        shift3 = [sb(f"shift3{i}", [P, JT]) for i in range(2)]

        NA = NT // JT
        NE = 6
        FIRST_R = NA + NE
        FIRST_B = FIRST_R + RJOBS
        NJ = FIRST_B + NA - NE
        LAST_SET = RJOBS + 2
        TR, LG, DN = 5, 7, 3

        s_r = sem("s_r")
        rt_ps = sem("rt_ps")
        rth_ready = sem("rth_ready")
        rt_ready = sem("rt_ready")
        lg_ps = sem("lg_ps")
        lgt_ps = sem("lgt_ps")
        lgt_ready = sem("lgt_ready")
        own3 = sem("own3")
        lg_ready = sem("lg_ready")
        ex_ready = sem("ex_ready")
        both_ready = sem("both_ready")
        pre_ps = sem("pre_ps")
        slot_ready = sem("slot_ready")
        s_scat = sem("s_scat")
        s_stg = [sem("s_stg_g"), sem("s_stg_u"), sem("s_stg_d")]
        s_row = [sem("s_row0"), sem("s_row1")]
        xt_ps = sem("xt_ps")
        xh_ready = sem("xh_ready")
        xl_ready = sem("xl_ready")
        whi_gu = sem("whi_gu")
        wlo_gu = sem("wlo_gu")
        whi_d = sem("whi_d")
        wlo_d = sem("wlo_d")
        gu_ps = sem("gu_ps")
        sil_ready = sem("sil_ready")
        hr_ready = sem("hr_ready")
        hh_ready = sem("hh_ready")
        hl_ready = sem("hl_ready")
        dn_ps = sem("dn_ps")
        down_out = sem("down_out")
        y_copied = sem("y_copied")
        s_y = sem("s_y")
        s_got = [sem("s_got0"), sem("s_got1")]
        got_used = sem("got_used")
        own_f = {n: sem("own_f_" + n) for n in ("sum", "stats", "aggr", "m1", "m2", "m3", "m4")}
        ve3_ready = sem("ve3_ready")
        g3_ready = sem("g3_ready")
        shift_ready = sem("shift_ready")
        fin_ready = sem("fin_ready")

        with nc.Block() as block:
            class Job:
                def __init__(self, kind, c, m, e, wset, wp, own_d=False, next_gu=False):
                    self.kind, self.c, self.m, self.e, self.wset, self.wp = kind, c, m, e, wset, wp
                    self.own_d, self.next_gu = own_d, next_gu

            def job_a(c, e):
                return Job("a", c, c, e, 0, 0, next_gu=isinstance(c, int) and c == NA - 1)

            def job_s(c, e):
                fixed = isinstance(c, int)
                return Job("s", c, c + NA, (NA + e) % 2, 1, 1, own_d=fixed and c == 0, next_gu=fixed and c == NE - 1)

            def job_r(c, e):
                return Job("r", c, c + FIRST_R, (FIRST_R + e) % 2, c + 2, e, own_d=True, next_gu=True)

            def job_b(c):
                return Job("b", c, FIRST_B + c - NE, (FIRST_B + c - NE) % 2, LAST_SET, LAST_SET % 2, own_d=(c == NE))

            def passes(eng, job, after_a=None, after_s=None, before_last=None):
                job(job_a(0, 0), None)
                job(job_a(1, 1), job_a(0, 0))
                with eng.Fori(1, NA // 2 - 1) as i:
                    for e in range(2):
                        job(job_a(2 * i + e, e), job_a(2 * i + e - 1, 1 - e))
                job(job_a(NA - 2, 0), job_a(NA - 3, 1))
                job(job_a(NA - 1, 1), job_a(NA - 2, 0))
                if after_a is not None:
                    after_a()
                job(job_s(0, 0), job_a(NA - 1, 1))
                if after_s is not None:
                    after_s()
                with eng.Fori(0, (NE - 2) // 2) as i:
                    for e in range(2):
                        job(job_s(2 * i + 1 + e, 1 - e), job_s(2 * i + e, e))
                job(job_s(NE - 1, 1), job_s(NE - 2, 0))
                job(job_r(0, 0), job_s(NE - 1, 1))
                job(job_r(1, 1), job_r(0, 0))
                with eng.Fori(1, RJOBS // 2) as i:
                    for e in range(2):
                        job(job_r(2 * i + e, e), job_r(2 * i + e - 1, 1 - e))
                job(job_r(RJOBS - 1, 0), job_r(RJOBS - 2, 1))
                job(job_b(NE), job_r(RJOBS - 1, 0))
                for c in range(NE + 1, NA):
                    job(job_b(c), job_b(c - 1))
                job(None, job_b(NA - 1))

            def last(j):
                return isinstance(j.m, int) and j.m == NJ - 1

            def split_rows(i):
                if i < 2:
                    return [(slice(0, P), slice(0, KC))]
                return [(slice(0, P), slice(0, F // P)), (slice(0, F % P), slice(F // P, NF))]

            @block.sync
            def _(sp):
                sp.dma_start(rin[:], A["router"]).then_inc(s_r, 16)

                def gate_up(n, wg, wu):
                    for i, w in enumerate((wg, wu)):
                        if not (isinstance(n, int) and n == 0):
                            sp.wait_ge(wlo_gu, 2 * (n - 1) + i + 1)
                        sp.dma_start(stg[i][:], w.rearrange("(k p) f -> p k f", p=P)).then_inc(s_stg[i], 16)

                def down_weights(n, wd):
                    if not (isinstance(n, int) and n == 0):
                        sp.wait_ge(wlo_d, n)
                    full = F // P
                    sp.dma_start(stg[2][:, 0:full, :], wd[0:full * P, :].rearrange("(k p) c -> p k c", p=P)).then_inc(s_stg[2], 16)
                    sp.dma_start(stg[2][0:F - full * P, full, :], wd[full * P:F, :]).then_inc(s_stg[2], 16)

                def expert(r):
                    return sp.value_load(exp_i[0:1, ds(r, 1)], min_val=0, max_val=E - 1)

                def part(name, e):
                    return A[name][ds(e, 1)].rearrange("a p f -> (a p) f")

                def routed_gate_up(r):
                    e = expert(r)
                    gate_up(r + 2, part("wg", e), part("wu", e))

                def routed_down(r):
                    down_weights(r + 2, part("wd", expert(r)))

                def shared_gate_up(n, u):
                    gate_up(n, A["sg"][:, u * F:(u + 1) * F], A["su"][:, u * F:(u + 1) * F])

                def shared_down(n, u):
                    down_weights(n, A["sd"][u * F:(u + 1) * F, :])

                def rows_of_tokens(m, e, c):
                    if not (isinstance(m, int) and m < 2):
                        sp.wait_ge(xt_ps, m - 1)
                    sp.dma_start(xrow[e][:], xs[:, ds(JT * c, JT), :]).then_inc(s_row[e], 16)

                def rows_of_slots(r, e):
                    sp.wait_ge(xt_ps, r + FIRST_R - 1)
                    buf = (FIRST_R + e) % 2
                    sp.dma_start(xrow[buf][:], xg[ds(r, 1)].rearrange("a (t p) c -> p (a t) c", p=P)).then_inc(s_row[buf], 16)

                def store(r):
                    sp.wait_ge(y_copied, r + 1)
                    sp.dma_start(yg[ds(r, 1)].rearrange("a (t p) c -> p (a t) c", p=P), yout[:]).then_inc(s_y, 16)

                shared_gate_up(0, 0)
                rows_of_tokens(0, 0, 0)
                shared_down(0, 0)
                rows_of_tokens(1, 1, 1)
                shared_gate_up(1, 1)
                shared_down(1, 1)
                with sp.Fori(1, NA // 2) as i:
                    for e in range(2):
                        rows_of_tokens(2 * i + e, e, 2 * i + e)
                with sp.Fori(0, NE // 2) as i:
                    for e in range(2):
                        rows_of_tokens(2 * i + NA + e, (NA + e) % 2, 2 * i + e)
                sp.wait_ge(slot_ready, 1)
                routed_gate_up(0)
                routed_down(0)
                sp.wait_ge(s_scat, 16 * 2 * NT)
                for r in range(3):
                    rows_of_slots(r, r % 2)
                routed_gate_up(1)

                def beside(r, e):
                    fixed = isinstance(r, int)
                    if not fixed or r + 3 < RJOBS:
                        rows_of_slots(r + 3, 1 - e)
                    elif r + 3 - RJOBS < NA - NE:
                        m = FIRST_R + r + 3
                        rows_of_tokens(m, m % 2, NE + r + 3 - RJOBS)
                    if not fixed or r + 2 < RJOBS:
                        routed_gate_up(r + 2)
                    elif r + 2 == RJOBS:
                        shared_gate_up(LAST_SET, 1)
                    if not fixed or r + 1 < RJOBS:
                        routed_down(r + 1)
                    else:
                        shared_down(LAST_SET, 1)
                    if not (fixed and r == 0):
                        store(r - 1)
                beside(0, 0)
                with sp.Fori(0, (RJOBS - 4) // 2) as i:
                    for e in range(2):
                        beside(2 * i + 1 + e, 1 - e)
                for r in range(2 * ((RJOBS - 4) // 2) + 1, RJOBS):
                    beside(r, r % 2)
                store(RJOBS - 1)
                for c in range(NA):
                    sp.wait_ge(fin_ready, c + 1)
                    sp.dma_start(out_tok[:, JT * c:JT * (c + 1), :], xs[:, JT * c:JT * (c + 1), :]).then_inc(s_out, 16)
                sp.wait_ge(s_out, 16 * NA)

            @block.gpsimd
            def _(pool):
                pool.wait_ge(slot_ready, 1)
                for t in range(NT):
                    for w in range(2):
                        nc.gpsimd.indirect_dma_start(out=xg_rows, out_offset=bass.IndirectOffsetOnAxis(slot_i[:, w, t:t + 1], 0),
                                                     in_=xs[:, t, :], in_offset=None).then_inc(s_scat, 16)
                pool.wait_ge(s_y, 16 * RJOBS)

                def fetch(c):
                    for t in range(JT):
                        for w in range(2):
                            nc.gpsimd.indirect_dma_start(out=got[c % 2][:, t, w, :], out_offset=None, in_=yg_rows,
                                                         in_offset=bass.IndirectOffsetOnAxis(slot_i[:, w, JT * c + t:JT * c + t + 1], 0))\
                              .then_inc(s_got[c % 2], 16)
                fetch(0)
                fetch(1)
                for c in range(NA):
                    pool.wait_ge(ve3_ready, c + 1)
                    if c:
                        pool.wait_ge(own_f["m4"], c)
                    nc.gpsimd.tensor_tensor(g3[:], ve3[c % 2][:], mhalf[:, 0:JT], ALU.pow).then_inc(g3_ready, 1)
                    if c + 2 < NA:
                        pool.wait_ge(got_used, c + 1)
                        fetch(c + 2)

            @block.scalar
            def _(act):
                act.wait_ge(rt_ps, 1)
                nc.scalar.activation(rth[:], psum[:, LG, 0:KC * E].rearrange("p (k e) -> p k e", e=E), ACT.Copy).then_inc(rth_ready, 1)

                def exponentials():
                    act.wait_ge(lg_ready, 1)
                    nc.scalar.activation(ex[:], lg[:], ACT.Exp).then_inc(ex_ready, 1)

                def high_part(n, e, i):
                    act.wait_ge(s_stg[i], (16 if i < 2 else 32) * (n + 1))
                    for r, k in split_rows(i):
                        ins = nc.scalar.activation(wh[e][i][r, k, :], stg[i][r, k, :], ACT.Copy)
                    ins.then_inc(whi_gu if i < 2 else whi_d, 1)

                def high_rows(m, e):
                    act.wait_ge(xt_ps, m + 1)
                    nc.scalar.activation(xh[e][:].rearrange("p k (t n) -> p t k n", n=P),
                                         psum[:, TR:TR + JT, :].rearrange("p t (k n) -> p t k n", n=P), ACT.Copy).then_inc(xh_ready, 1)

                def job(j, prev):
                    for f, (_, w) in enumerate(FT if j else ()):
                        act.wait_ge(gu_ps, NF * j.m + f + 1)
                        nc.scalar.activation(sil[0:w, f, :], psum[0:w, f, 0:J], ACT.Silu).then_inc(sil_ready, 1)
                        act.wait_ge(hr_ready, NF * j.m + f + 1)
                        if not (isinstance(j.m, int) and j.m < 2):
                            act.wait_ge(dn_ps, JT * (j.m - 1))
                        nc.scalar.activation(hh[j.e][0:w, f, :], hr[0:w, f, :], ACT.Copy).then_inc(hh_ready, 1)
                        if f == 0 and not last(j):
                            high_rows(j.m + 1, 1 - j.e)
                        if f == 1 and j.kind == "a":
                            act.wait_ge(lgt_ps, j.c + 1)
                            if not (isinstance(j.m, int) and j.m == 0):
                                act.wait_ge(lg_ps, j.c)
                            nc.scalar.activation(lgt[:], psum[0:E, LG, J:2 * J], ACT.Copy).then_inc(lgt_ready, 1)
                        if f < 2 and j.next_gu:
                            high_part(j.wset + 1, 1 - j.wp, f)
                        if f == 2 and j.own_d:
                            high_part(j.wset, j.wp, 2)
                    if prev and prev.kind == "r":
                        act.wait_ge(dn_ps, JT * prev.m + JT)
                        if not (isinstance(prev.c, int) and prev.c == 0):
                            act.wait_ge(s_y, 16 * prev.c)
                        nc.scalar.activation(yout[:], psum[:, DN:DN + JT, :], ACT.Copy).then_inc(y_copied, 1)

                for i in range(3):
                    high_part(0, 0, i)
                high_rows(0, 0)
                passes(act, job, after_a=exponentials)
                for c in range(NA):
                    act.wait_ge(shift_ready, c + 1)
                    for t in range(JT):
                        ins = nc.scalar.activation(xs[:, JT * c + t, :], fin[c % 2][:, t, :], ACT.Identity, bias=shift3[c % 2][:, t:t + 1], scale=rstd3[c % 2][:, t:t + 1])
                    ins.then_inc(fin_ready, 1)

            @block.vector
            def _(dve):
                chain3 = [0]

                def link(ins):
                    chain3[0] += 1
                    ins.then_inc(own3, 1)
                    dve.wait_ge(own3, chain3[0])

                dve.wait_ge(rth_ready, 1)
                nc.vector.tensor_tensor(rtl[:], psum[:, LG, 0:KC * E].rearrange("p (k e) -> p k e", e=E), rth[:].bitcast(F32),
                                        ALU.subtract).then_inc(rt_ready, 1)
                def over(a):
                    return a.unsqueeze(2).to_broadcast([P, NT, E])

                def per_expert(a):
                    return a.unsqueeze(1).to_broadcast([P, NT, E])

                def flat(a):
                    return a[:].rearrange("p t e -> p (t e)")

                tt, tr, tsc = nc.vector.tensor_tensor, nc.vector.tensor_reduce, nc.vector.tensor_scalar
                top, tot, rtot, k1, k2, top2 = (t[:] for t in t16)

                def choose():
                    pl = psum[:, LG, 0:NT * E].rearrange("p (t e) -> p t e", e=E)
                    dve.wait_ge(lg_ps, NA)
                    link(tr(top, pl, X, ALU.max))
                    tt(lg[:], pl, over(top), ALU.subtract).then_inc(lg_ready, 1)
                    dve.wait_ge(ex_ready, 1)
                    link(tr(tot, ex[:], X, ALU.add))
                    link(nc.vector.reciprocal(rtot, tot))
                    link(tt(gates[:], ex[:], over(rtot), ALU.mult))
                    ranks = per_expert(rank[:])
                    link(tr(top, gates[:], X, ALU.max))
                    link(tt(keys[:], gates[:], over(top), ALU.is_equal))
                    link(tt(keys[:], keys[:], ranks, ALU.mult))
                    link(tr(k1, keys[:], X, ALU.max))
                    link(tt(one1[:], keys[:], over(k1), ALU.is_equal))
                    link(nc.vector.scalar_tensor_tensor(flat(rest), flat(one1), -4.0, flat(gates), ALU.mult, ALU.add))
                    link(tr(top2, rest[:], X, ALU.max))
                    link(tt(keys[:], rest[:], over(top2), ALU.is_equal))
                    link(tt(keys[:], keys[:], ranks, ALU.mult))
                    link(tr(k2, keys[:], X, ALU.max))
                    link(tt(one2[:], keys[:], over(k2), ALU.is_equal))
                    tt(both[:], one1[:], one2[:], ALU.add).then_inc(both_ready, 1)
                    link(tt(tot, top, top2, ALU.add))
                    link(tsc(tot, tot, 1e-20, None, ALU.add))
                    link(nc.vector.reciprocal(rtot, tot))
                    tt(gate[:, 0, :], top, rtot, ALU.mult)
                    link(tt(gate[:, 1, :], top2, rtot, ALU.mult))

                def place():
                    within = psum[:, LG, NT * E:2 * NT * E].rearrange("p (t e) -> p t e", e=E)
                    total = psum[:, LG, 2 * NT * E:3 * NT * E].rearrange("p (t e) -> p t e", e=E)
                    link(nc.vector.memset(before_t[:, 0, :], 0.0))
                    dve.wait_ge(pre_ps, 1)
                    for t in range(1, NT):
                        link(tt(before_t[:, t, :], before_t[:, t - 1, :], total[:, t - 1, :], ALU.add))
                    link(tt(count[:], before_t[:, NT - 1, :], total[:, NT - 1, :], ALU.add))
                    link(tsc(jobs_e[:], count[:], J / 2.0 - 0.5, 1.0 / J, ALU.add, ALU.mult))
                    link(tsc(jobs_e[:], jobs_e[:], MAGIC, None, ALU.add))
                    link(tsc(jobs_e[:], jobs_e[:], MAGIC, None, ALU.subtract))
                    link(nc.vector.tensor_copy(end_e[:, 0:1], jobs_e[:, 0:1]))
                    for x in range(1, E):
                        link(tt(end_e[:, x:x + 1], end_e[:, x - 1:x], jobs_e[:, x:x + 1], ALU.add))
                    link(tt(base_e[:], end_e[:], jobs_e[:], ALU.subtract))
                    link(tt(le[:], end_e[:].unsqueeze(1).to_broadcast([P, RJOBS, E]), job_no[:].unsqueeze(2).to_broadcast([P, RJOBS, E]),
                            ALU.is_le))
                    link(tr(exp_of[:], le[:], X, ALU.add))
                    link(tsc(exp_i[:], exp_of[:], float(E - 1), None, ALU.min))
                    link(tsc(base_e[:], base_e[:], float(J), None, ALU.mult))
                    link(tt(slots[:], before_t[:], within, ALU.add))
                    link(tt(slots[:], slots[:], per_expert(base_e[:]), ALU.add))
                    link(tt(keys[:], slots[:], one1[:], ALU.mult))
                    link(tr(slot_f[:, 0, :], keys[:], X, ALU.add))
                    link(tt(keys[:], slots[:], one2[:], ALU.mult))
                    link(tr(slot_f[:, 1, :], keys[:], X, ALU.add))
                    nc.vector.tensor_copy(slot_i[:], slot_f[:]).then_inc(slot_ready, 1)

                def low_part(n, e, i):
                    dve.wait_ge(whi_gu if i < 2 else whi_d, 2 * n + i + 1 if i < 2 else n + 1)
                    for r, k in split_rows(i):
                        ins = nc.vector.tensor_tensor(wl[e][i][r, k, :], stg[i][r, k, :], wh[e][i][r, k, :].bitcast(F32), ALU.subtract)
                    ins.then_inc(wlo_gu if i < 2 else wlo_d, 1)

                def low_rows(m, e):
                    dve.wait_ge(xh_ready, m + 1)
                    for t in range(JT):
                        part = slice(t * P, (t + 1) * P)
                        ins = nc.vector.tensor_tensor(xl[e][:, :, part], psum[:, TR + t, :].rearrange("p (k n) -> p k n", n=P),
                                                      xh[e][:, :, part].bitcast(F32), ALU.subtract)
                    ins.then_inc(xl_ready, 1)

                def row(a, t):
                    return a[:, ds(t, 1), :].rearrange("p a c -> p (a c)")

                def hidden(j):
                    for f, (_, w) in enumerate(FT):
                        dve.wait_ge(sil_ready, NF * j.m + f + 1)
                        if not (isinstance(j.m, int) and j.m == 0):
                            dve.wait_ge(hl_ready, NF * j.m + f + 1 - NF)
                        nc.vector.tensor_tensor(hr[0:w, f, :], sil[0:w, f, :], psum[0:w, f, J:2 * J], ALU.mult).then_inc(hr_ready, 1)
                        dve.wait_ge(hh_ready, NF * j.m + f + 1)
                        nc.vector.tensor_tensor(hl[j.e][0:w, f, :], hr[0:w, f, :], hh[j.e][0:w, f, :].bitcast(F32), ALU.subtract)\
                          .then_inc(hl_ready, 1)
                        if f == 0 and not last(j):
                            low_rows(j.m + 1, 1 - j.e)
                        if f < 2 and j.next_gu:
                            low_part(j.wset + 1, 1 - j.wp, f)
                        if f == 2 and j.own_d:
                            low_part(j.wset, j.wp, 2)

                def down_into_acc(prev):
                    dve.wait_ge(dn_ps, JT * prev.m + JT)
                    for t in range(JT):
                        so_far = xs if prev.kind == "a" else acc
                        ins = nc.vector.tensor_tensor(row(acc, JT * prev.c + t), row(so_far, JT * prev.c + t), psum[:, DN + t, :], ALU.add)
                    ins.then_inc(down_out, 1)

                def job(j, prev):
                    if j:
                        hidden(j)
                    if j and last(j):
                        gather_rows(0, 0)
                        gather_rows(1, 1)
                    if prev and prev.kind != "r":
                        down_into_acc(prev)

                def gather_rows(c, e):
                    f = fin[e]
                    fixed = isinstance(c, int)
                    nth = 8 * JT * c * 2 + (32 * JT if e == 0 else 16 * JT)
                    dve.wait_ge(s_got[e], nth)
                    if not (fixed and c < 2):
                        dve.wait_ge(fin_ready, c - 1)
                    for t in range(JT):
                        g = gate[:, 0, :][:, ds(JT * c + t, 1)]
                        ins = nc.vector.scalar_tensor_tensor(f[:, t, :], got[e][:, t, 0, :], g, row(acc, JT * c + t), ALU.mult, ALU.add)
                    ins.then_inc(own_f["sum"], 1)
                    dve.wait_ge(own_f["sum"], c + 1)
                    for t in range(JT):
                        g = gate[:, 1, :][:, ds(JT * c + t, 1)]
                        ins = nc.vector.scalar_tensor_tensor(f[:, t, :], got[e][:, t, 1, :], g, f[:, t, :], ALU.mult, ALU.add)
                    ins.then_inc(got_used, 1)
                    dve.wait_ge(got_used, c + 1)
                    for t in range(JT):
                        ins = nc.vector.bn_stats(stats3[:, t, :], f[:, t, :])
                    ins.then_inc(own_f["stats"], 1)
                    dve.wait_ge(own_f["stats"], c + 1)
                    if not (fixed and c == 0):
                        scales(c - 1, 1 - e)
                    for t in range(JT):
                        ins = nc.vector.bn_aggr(mv3[e][:, t, :], stats3[:, t, :])
                    ins.then_inc(own_f["aggr"], 1)
                    dve.wait_ge(own_f["aggr"], c + 1)
                    nc.vector.tensor_scalar(ve3[e][:], mv3[e][:, :, 1], LN_EPS, None, ALU.add).then_inc(ve3_ready, 1)

                def scales(c, e):
                    dve.wait_ge(g3_ready, c + 1)
                    nc.vector.tensor_tensor(m1[:], g3[:], g3[:], ALU.mult).then_inc(own_f["m1"], 1)
                    dve.wait_ge(own_f["m1"], c + 1)
                    nc.vector.tensor_tensor(m2[:], m1[:], ve3[e][:], ALU.mult).then_inc(own_f["m2"], 1)
                    dve.wait_ge(own_f["m2"], c + 1)
                    nc.vector.tensor_scalar(m1[:], m2[:], -0.5, 1.5, ALU.mult, ALU.add).then_inc(own_f["m3"], 1)
                    dve.wait_ge(own_f["m3"], c + 1)
                    nc.vector.tensor_tensor(rstd3[e][:], m1[:], g3[:], ALU.mult).then_inc(own_f["m4"], 1)
                    dve.wait_ge(own_f["m4"], c + 1)
                    nc.vector.scalar_tensor_tensor(shift3[e][:], mv3[e][:, :, 0], -1.0, rstd3[e][:], ALU.mult, ALU.mult).then_inc(shift_ready, 1)

                for i in range(3):
                    low_part(0, 0, i)
                low_rows(0, 0)
                passes(dve, job, after_a=choose, after_s=place)
                with dve.Fori(1, NA // 2) as i:
                    for e in range(2):
                        gather_rows(2 * i + e, e)
                scales(NA - 1, (NA - 1) % 2)

            @block.tensor
            def _(pe):
                mm = nc.tensor.matmul
                pe.wait_ge(s_r, 16)
                for k in range(KC):
                    ins = nc.tensor.transpose(psum[:, LG, k * E:(k + 1) * E], rin[:, k * P:(k + 1) * P], ident[0:E, 0:E])
                ins.then_inc(rt_ps, 1)
                pe.wait_ge(rt_ready, 1)

                def logits(c, e):
                    for k in range(KC):
                        for xx, rr in ((xh, rth), (xl, rth), (xh, rtl)):
                            ins = mm(psum[0:E, LG, J:2 * J], rr[:, k, :], xx[e][:, k, :],
                                     start=(k == 0 and xx is xh and rr is rth), stop=(k == KC - 1 and rr is rtl))
                    ins.then_inc(lgt_ps, 1)

                def turn_logits(c):
                    pe.wait_ge(lgt_ready, c + 1)
                    for t in range(JT):
                        ins = mm(psum[:, LG, ds((JT * c + t) * E, E)], lgt[:, t * P:(t + 1) * P], ident[0:E, 0:E], start=True, stop=True)
                    ins.then_inc(lg_ps, 1)

                def prefix():
                    pe.wait_ge(both_ready, 1)
                    mm(psum[:, LG, NT * E:2 * NT * E], below[:], both[:].rearrange("p t e -> p (t e)"), start=True, stop=True)
                    mm(psum[:, LG, 2 * NT * E:3 * NT * E], ones[:], both[:].rearrange("p t e -> p (t e)"), start=True, stop=True)\
                        .then_inc(pre_ps, 1)

                def turn_rows(m, e):
                    pe.wait_ge(s_row[e], 8 * m + 16 - 8 * e)
                    for t in range(JT):
                        for k in range(KC):
                            ins = nc.tensor.transpose(psum[:, TR + t, k * P:(k + 1) * P], xrow[e][:, t, k * P:(k + 1) * P], ident[:])
                    ins.then_inc(xt_ps, 1)

                def down_banks_free(j):
                    if j.kind == "r":
                        if isinstance(j.c, int) and j.c == 0:
                            pe.wait_ge(down_out, FIRST_R)
                        else:
                            pe.wait_ge(y_copied, j.c)
                    elif j.kind == "b" and j.c == NE:
                        pe.wait_ge(y_copied, RJOBS)
                    elif j.kind == "a":
                        if not (isinstance(j.c, int) and j.c == 0):
                            pe.wait_ge(down_out, j.c)
                    else:
                        pe.wait_ge(down_out, j.c + NA)

                def gate_and_up(j):
                    pe.wait_ge(xl_ready, j.m + 1)
                    pe.wait_ge(wlo_gu, 2 * j.wset + 2)
                    for f, (f0, w) in enumerate(FT):
                        if not (isinstance(j.m, int) and j.m == 0):
                            pe.wait_ge(hr_ready, NF * j.m + f + 1 - NF)
                        for i in range(2):
                            for k in range(KC):
                                for ww, xx in ((wh, xh), (wh, xl), (wl, xh)):
                                    ins = mm(psum[0:w, f, i * J:(i + 1) * J], ww[j.wp][i][:, k, f0:f0 + w], xx[j.e][:, k, :],
                                             start=(k == 0 and ww is wh and xx is xh), stop=(k == KC - 1 and ww is wl))
                        ins.then_inc(gu_ps, 1)
                        if f == 0 and not last(j):
                            turn_rows(j.m + 1, 1 - j.e)
                        if f == 1 and j.kind == "a":
                            logits(j.c, j.e)
                        if f == 0 and (j.kind == "a" or j.kind == "s" and isinstance(j.c, int) and j.c == 0):
                            if not (isinstance(j.m, int) and j.m == 0):
                                turn_logits(j.m - 1)

                def down(j):
                    pe.wait_ge(wlo_d, j.wset + 1)
                    down_banks_free(j)
                    for f, (f0, w) in enumerate(FT):
                        pe.wait_ge(hl_ready, NF * j.m + f + 1)
                        for t in range(JT):
                            for aa, ww in ((hh, wh), (hl, wh), (hh, wl)):
                                ins = mm(psum[:, DN + t, :], aa[j.e][0:w, f, t * P:(t + 1) * P], ww[j.wp][2][0:w, f, :],
                                         start=(f == 0 and aa is hh and ww is wh), stop=(f == NF - 1 and ww is wl))
                            if f == NF - 1:
                                ins.then_inc(dn_ps, 1)

                def job(j, prev):
                    if j:
                        gate_and_up(j)
                    if prev:
                        down(prev)

                turn_rows(0, 0)
                passes(pe, job, after_s=prefix)


_NAMES = {"x": "x", "ctx": "ctx_2048", "w_qkv": "L0_attn_w_qkv", "w_proj": "L0_attn_w_proj", "ssm": "L0_xattn_ssm_kernel",
          "D": "L0_xattn_D", "router": "L0_ffn_router_w", "wg": "L0_ffn_wg", "wu": "L0_ffn_wu", "wd": "L0_ffn_wd",
          "sg": "L0_ffn_sg", "su": "L0_ffn_su", "sd": "L0_ffn_sd"}


def kernel(**inputs):
    import numpy as _np
    import concourse.bacc as _bacc
    from concourse.bass_utils import run_bass_kernel_spmd as _run

    nc = _bacc.Bacc("TRN2", target_bir_lowering=False, num_devices=1)
    arrays, aps = {}, {}
    for short, name in _NAMES.items():
        a = _np.ascontiguousarray(inputs[name])
        arrays[f"in_{short}"] = a
        aps[short] = nc.dram_tensor(f"in_{short}", a.shape, mybir.dt.from_np(a.dtype), kind="ExternalInput").ap()
    shape = inputs["x"].shape
    aps["out"] = nc.dram_tensor("out", shape, F32, kind="ExternalOutput").ap()
    build(nc, aps)
    r = _run(nc, [arrays], core_ids=[0])
    return r.results[0]["out"]
```

```python
from contextlib import ExitStack

import concourse.bass as bass
from concourse import mybir

STAGE = 3

F32 = mybir.dt.float32
F32R = mybir.dt.float32r
BF16 = mybir.dt.bfloat16
I32 = mybir.dt.int32
ALU = mybir.AluOpType
ACT = mybir.ActivationFunctionType
X = mybir.AxisListType.X
ds = bass.ds

P = 128
MAGIC = 12582912.0
MASKED = -1.0e30
LN_EPS = 1e-05


def build(nc, A):
    B, N, C = A["x"].shape
    H, DH = 16, C // 16
    TB = N // P
    NT = B * TB
    KC = C // P
    OG = 2 * C // P
    HG = P // DH
    NG = H // HG
    PAIRS = H // 2
    WT = 3 * C // P
    WALL = WT + C // P
    WCH = 4
    SCALE = float(DH) ** -0.5
    HK, L = A["ssm"].shape
    KP = P + L
    LB = L // P
    I = N // HK
    E, _, F = A["wg"].shape
    J = 2 * P
    JT = J // P
    RJOBS = (2 * NT * P + E * (J - 1)) // J
    VW = DH + 1

    x_tok = A["x"].rearrange("b (t p) c -> p (b t) c", p=P)
    ctx_tok = A["ctx"].rearrange("b (t p) c -> p (b t) c", p=P)
    out_tok = A["out"].rearrange("b (t p) c -> p (b t) c", p=P)
    wqkv_v = A["w_qkv"].rearrange("(t p) c -> p t c", p=P)
    xg = nc.dram_tensor("xg", (RJOBS, J, C), F32, kind="Internal").ap()
    yg = nc.dram_tensor("yg", (RJOBS, J, C), F32, kind="Internal").ap()
    xg_rows = xg.rearrange("r j c -> (r j) c")
    yg_rows = yg.rearrange("r j c -> (r j) c")
    wproj_v = A["w_proj"].rearrange("(t p) c -> p t c", p=P)

    with ExitStack() as ctx:
        where = [(nc.sbuf_base + 31) // 32 * 32]

        def sb(name, shape, dt=F32):
            size = 4 if dt in (F32, F32R, I32) else 2
            for n in shape[1:]:
                size *= n
            size = (size + 31) // 32 * 32
            where[0] += size
            assert where[0] <= nc.sbuf_usable_end, (name, where[0])
            return nc.alloc_sbuf_tensor_at(name, shape, dt, offset=where[0] - size)

        def sem(name):
            return ctx.enter_context(nc.semaphore(name))

        xs = sb("xs", [P, NT, C])
        ident = sb("ident", [P, P])
        identb = sb("identb", [P, P], BF16)
        ones = sb("ones", [P, P])
        rank = sb("rank", [P, E])
        job_no = sb("job_no", [P, RJOBS])
        mhalf = sb("mhalf", [P, NT])
        psum = ctx.enter_context(nc.psum_tensor("psum", [P, 8, 512], F32))

        mark_b = where[0]
        wT = sb("wT", [P, KC, WALL * P], BF16)
        wmean = sb("wmean", [P, 2])
        mask_st = sb("mask_st", [P, P], BF16)
        mask_s = sb("mask_s", [P, P], BF16)
        xq_t = sb("xq_t", [P, TB, C])
        xq = sb("xq", [P, TB, C], BF16)
        amax = sb("amax", [P, TB])
        qs_r = sb("qs_r", [P, TB])
        qs = sb("qs", [P, TB])
        vinv = sb("vinv", [P, TB])
        xqT = sb("xqT", [P, KC, N], BF16)
        rs = sb("rs", [P, N])
        real = sb("real", [P, OG, N])
        hi = sb("hi", [P, OG, N], F32R)
        lo = real[:].bitcast(F32R)
        VPAD = 64
        vx = [sb(f"vx{i}", [P, TB, H * VW + VPAD - VW]) for i in range(2)]
        ot = sb("ot", [P, 2, N])
        orow = sb("orow", [P, 2, 2, TB, P])
        cx = sb("cx", [P, TB, H])
        ct = sb("ct", [H, N], F32R)
        pt = sb("pt", [P, 2, 2, N + P])
        attn = sb("attn", [P, TB, C])
        amax2 = sb("amax2", [P, TB])
        qs2_r = sb("qs2_r", [P, TB])
        qs2 = sb("qs2", [P, TB])
        pscale = sb("pscale", [P, 2, TB])
        aq = sb("aq", [P, TB, C], BF16)
        aT = sb("aT", [P, KC, N], BF16)
        resid = sb("resid", [P, TB, C])
        stats = sb("stats", [P, TB, 6])
        mv = sb("mv", [P, TB, 2])
        ve = sb("ve", [P, TB])
        r0 = sb("r0", [P, TB])
        nt1 = sb("nt1", [P, TB])
        nt2 = sb("nt2", [P, TB])
        rstd = sb("rstd", [P, TB])

        cin_at = where[0]
        zero = sb("zero", [P, C])
        kin = sb("kin", [HK, KP])
        dcol = sb("dcol", [HK, 1])
        krow = nc.dram_tensor("krow", (HK, KP), F32, kind="Internal").ap()
        where[0] = cin_at
        cin = sb("cin", [P, NT + 1, C])
        wraw_at = where[0]
        wraw = sb("wraw", [P, WALL, C])
        wtern = sb("wtern", [P, WALL, C], BF16)
        wsum = sb("wsum", [P, WALL])
        wtot = sb("wtot", [P, 2])
        wscale = sb("wscale", [P, 2])
        where[0] = wraw_at
        qst = [sb(f"qst{i}", [P, H, N], F32R) for i in range(2)]
        kst = [sb(f"kst{i}", [P, H, N], F32R) for i in range(2)]
        end_a = where[0]
        KS = 3 * DH
        rec = sb("rec", [P, NG, TB, 2, 2])
        STACK = 16 * (6 * HG - 4)

        s_const = sem("s_const")
        s_w = [sem(f"s_w{i}") for i in range(WALL // WCH)]
        s_x = [sem("s_x0"), sem("s_x1")]
        s_dve = sem("s_dve")
        s_wsum = sem("s_wsum")
        s_wtot_ps = sem("s_wtot_ps")
        s_tern = sem("s_tern")
        s_wT_ps = sem("s_wT_ps")
        s_wT = sem("s_wT")
        xq_ready = sem("xq_ready")
        xT_ps = sem("xT_ps")
        xT_sb = sem("xT_sb")
        r_ps = sem("r_ps")
        r_sb = sem("r_sb")
        qk_ps = sem("qk_ps")
        v_ps = sem("v_ps")
        v_sb = sem("v_sb")
        real_ready = sem("real_ready")
        hi_ready = sem("hi_ready")
        lo_ready = sem("lo_ready")
        s_ps = sem("s_ps")
        mx_done = sem("mx_done")
        c_ps = sem("c_ps")
        ct_ready = sem("ct_ready")
        st_ps = sem("st_ps")
        s_stack = [sem("s_stack0"), sem("s_stack1")]
        stack_copy = sem("stack_copy")
        s_crow = sem("s_crow")
        ones_row = sem("ones_row")
        ot_ready = sem("ot_ready")
        rev_ready = sem("rev_ready")
        tv_ps = sem("tv_ps")
        orow_ready = sem("orow_ready")
        exp_done = sem("exp_done")
        pv_done = sem("pv_done")
        na_done = sem("na_done")
        aq_ready = sem("aq_ready")
        aT_ps = sem("aT_ps")
        aT_sb = sem("aT_sb")
        proj_ps = sem("proj_ps")
        res_done = sem("res_done")
        var_ready = sem("var_ready")
        r0_ready = sem("r0_ready")
        x1_done = sem("x1_done")
        s_k = sem("s_k")
        k_ready = sem("k_ready")
        s_krow = sem("s_krow")
        s_cin = sem("s_cin")
        s_out = sem("s_out")
        s_zero = sem("s_zero")

        own_sem = {n: sem("own_" + n) for n in (
            'amax', 'clip', 'rec', 'scale', 'round', 'stats', 'aggr', 'nt1', 'nt2', 'nt3', 'nt4', 'srec', 'amax2', 'clip2', 'rec2', 'scale2', 'round2')}
        chain = [0]

        def bankbf(k):
            return psum[:, k, :].bitcast(BF16)

        def stacked(b, e, each):
            return each // 2 * b + each - each // 2 * e

        def all_batches(eng, batch):
            batch(0, 0)
            batch(1, 1)
            with eng.Fori(1, B // 2 - 1) as i:
                for e in range(2):
                    batch(2 * i + e, e)
            batch(B - 2, 0)
            batch(B - 1, 1)

        stage_a = nc.Block()
        block = stage_a.__enter__()

        @block.sync
        def _(sp):
            sp.dma_start(wraw[:, 0:WCH, :], wqkv_v[:, 0:WCH, :]).then_inc(s_w[0], 16)
            sp.dma_start(xs[:, 0:TB, :], x_tok[:, 0:TB, :]).then_inc(s_x[0], 16)
            for i in range(1, WT // WCH):
                sp.dma_start(wraw[:, i * WCH:(i + 1) * WCH, :], wqkv_v[:, i * WCH:(i + 1) * WCH, :]).then_inc(s_w[i], 16)
            sp.dma_start(wraw[:, WT:WALL, :], wproj_v).then_inc(s_w[WT // WCH], 16)
            sp.dma_start(xs[:, TB:NT, :], x_tok[:, TB:NT, :]).then_inc(s_x[1], 16)
            sp.dma_start(kin[:, P:KP], A["ssm"]).then_inc(s_k, 16)
            sp.dma_start(dcol[:], A["D"].rearrange("(h a) -> h a", a=1)).then_inc(s_k, 16)

            def stack(b, e):
                if not (isinstance(b, int) and b < 2):
                    sp.wait_ge(st_ps, PAIRS * (b - 1))
                if isinstance(b, int) and b < 2:
                    sp.wait_ge(s_wT, WALL // 2)
                hif, lof = hi[:].bitcast(F32), real[:]
                for done, ready, n, src, g0, dst, at in (
                        (s_stack, hi_ready, OG // 4, hif, 0, qst, 0), (s_stack, hi_ready, OG // 2, hif, NG, kst, 0),
                        (s_stack, hi_ready, OG // 2, hif, NG, kst, 1), (s_stack, lo_ready, OG // 4, lof, 0, qst, 1),
                        (s_stack, lo_ready, OG // 2, lof, NG, kst, 2), (s_stack, hi_ready, OG // 2, hif, 0, qst, 2)):
                    sp.wait_ge(ready, OG // 2 * b + n)
                    for j in range(HG):
                        if src is hif and j == at:
                            continue
                        to = dst[e][DH * at:DH * (at + 1)].rearrange("p (g j) n -> p g j n", j=HG)[:, :, j, :].bitcast(F32)
                        sp.dma_start(to, src[DH * j:DH * (j + 1), g0:g0 + NG, :]).then_inc(done[e], 16)

            def max_row(b, e):
                sp.wait_ge(ct_ready, b + 1)
                sp.dma_start(qst[e][KS:KS + 1].bitcast(F32), ct[:].bitcast(F32)).then_inc(s_crow, 16)

            def ahead(b, e):
                max_row(b + 1, 1 - e)
                if not (isinstance(b, int) and b + 2 >= B):
                    stack(b + 2, e)
            stack(0, 0)
            stack(1, 1)
            max_row(0, 0)
            ahead(0, 0)
            sp.wait_ge(s_const, 9)
            sp.dma_start(xg_rows.rearrange("(n p) c -> p n c", p=P), zero[:].unsqueeze(1).to_broadcast([P, RJOBS * JT, C])).then_inc(s_zero, 16)
            sp.wait_ge(k_ready, 2)
            sp.dma_start(krow, kin[:]).then_inc(s_krow, 16)
            ahead(1, 1)
            sp.wait_ge(s_krow, 16)
            sp.wait_ge(s_zero, 16)
            sp.dma_start(cin[:, 1:NT + 1, :], ctx_tok).then_inc(s_cin, 16)
            with sp.Fori(1, B // 2 - 1) as i:
                for e in range(2):
                    ahead(2 * i + e, e)
            ahead(B - 2, 0)
            sp.wait_ge(s_cin, 16)
            if STAGE == 1:
                sp.wait_ge(x1_done, B)
                sp.dma_start(out_tok, xs[:]).then_inc(s_out, 16)
                sp.wait_ge(s_out, 16)

        @block.gpsimd
        def _(pool):
            nc.gpsimd.memset(ones[:], 1.0).then_inc(s_const, 1)
            nc.gpsimd.memset(ident[:], 0.0).then_inc(s_const, 1)
            nc.gpsimd.memset(mask_st[:], 0.0).then_inc(s_const, 1)
            nc.gpsimd.memset(mask_s[:], 0.0).then_inc(s_const, 1)
            nc.gpsimd.memset(vx[0][:], 1.0)
            nc.gpsimd.memset(vx[1][:], 1.0).then_inc(s_const, 1)
            nc.gpsimd.memset(cx[:], 0.0).then_inc(s_const, 1)
            nc.gpsimd.memset(zero[:], 0.0).then_inc(s_const, 1)
            nc.gpsimd.memset(mhalf[:], -0.5).then_inc(s_const, 1)
            for e in range(E):
                nc.gpsimd.memset(rank[:, e:e + 1], float(E - e))
            for r in range(RJOBS):
                ins = nc.gpsimd.memset(job_no[:, r:r + 1], float(r))
            ins.then_inc(s_const, 1)
            pool.wait_ge(s_const, 9)
            nc.gpsimd.affine_select(out=ident[:], in_=ident[:], compare_op=ALU.not_equal, fill=1.0, base=0,
                                    pattern=[[-1, P]], channel_multiplier=1).then_inc(s_const, 1)
            nc.gpsimd.affine_select(out=mask_st[:], in_=mask_st[:], compare_op=ALU.is_ge, fill=MASKED, base=0,
                                    pattern=[[1, P]], channel_multiplier=-1).then_inc(s_const, 1)
            nc.gpsimd.affine_select(out=mask_s[:], in_=mask_s[:], compare_op=ALU.is_ge, fill=MASKED, base=0,
                                    pattern=[[-1, P]], channel_multiplier=1).then_inc(s_const, 1)

            nc.gpsimd.memset(kin[:, 0:P], 0.0).then_inc(k_ready, 1)
            pool.wait_ge(s_k, 32)
            pool.wait_ge(k_ready, 1)
            nc.gpsimd.tensor_tensor(kin[:, P:P + 1], kin[:, P:P + 1], dcol[:], ALU.add).then_inc(k_ready, 1)

            def low_parts(b):
                for k in range(OG // 2):
                    pool.wait_ge(hi_ready, OG // 2 * b + k + 1)
                    part = slice(2 * k, 2 * k + 2)
                    nc.gpsimd.tensor_tensor(lo[:, part, :], real[:, part, :], hi[:, part, :].bitcast(F32),
                                            ALU.subtract).then_inc(lo_ready, 1)

            def rstd_guess(b):
                pool.wait_ge(var_ready, b + 1)
                nc.gpsimd.tensor_tensor(r0[:], ve[:], mhalf[:, 0:TB], ALU.pow).then_inc(r0_ready, 1)

            def reverse(tiles):
                for u in tiles:
                    if u:
                        pool.wait_ge(rev_ready, u)
                    nc.gpsimd.tensor_copy(cin[:, u, :].rearrange("p (k l) -> p k l", l=P),
                                          cin[:, u + 1, :].rearrange("p (k l) -> p k l", l=P)[:, :, ::-1]).then_inc(rev_ready, 1)

            low_parts(0)
            pool.wait_ge(lo_ready, OG // 2)
            pool.wait_ge(s_wT, WALL // 2)
            for e in range(2):
                nc.gpsimd.memset(kst[e][KS:KS + 1].bitcast(F32), 1.0).then_inc(ones_row, 1)
                pool.wait_ge(ones_row, e + 1)
            low_parts(1)

            def batch(b, e):
                if not (isinstance(b, int) and b == 0):
                    rstd_guess(b - 1)
                if not (isinstance(b, int) and b + 2 >= B):
                    low_parts(b + 2)
                elif b == B - 2:
                    pool.wait_ge(s_cin, 16)
                    reverse(range(0, 10))
                else:
                    reverse(range(10, NT))
            all_batches(pool, batch)
            rstd_guess(B - 1)

        @block.scalar
        def _(act):
            for i in range(WALL // 2):
                act.wait_ge(s_wT_ps, i + 1)
                nc.scalar.activation(wT[:, :, 2 * i * P:(2 * i + 2) * P].rearrange("p k (t o) -> p t k o", o=P),
                                     bankbf(i % 8)[:, 0:2 * KC * P].rearrange("p (t k o) -> p t k o", t=2, k=KC),
                                     ACT.Copy).then_inc(s_wT, 1)

            def evacuate_inputs(b, e):
                act.wait_ge(xT_ps, b + 1)
                nc.scalar.activation(xqT[:].rearrange("p k (t n) -> p t k n", n=P),
                                     bankbf(6).rearrange("p (t k n) -> p t k n", t=TB, k=KC), ACT.Copy).then_inc(xT_sb, 1)
                act.wait_ge(r_ps, b + 1)
                nc.scalar.activation(rs[:], psum[:, 7, 0:N], ACT.Copy).then_inc(r_sb, 1)
                for k in range(OG // 2):
                    act.wait_ge(real_ready, OG // 2 * b + k + 1)
                    if k == 0 and not (isinstance(b, int) and b == 0):
                        act.wait_ge(s_stack[1 - e], stacked(b - 1, 1 - e, STACK))
                    nc.scalar.activation(hi[:, 2 * k:2 * k + 2, :], real[:, 2 * k:2 * k + 2, :], ACT.Copy).then_inc(hi_ready, 1)
                for t in range(TB):
                    act.wait_ge(v_ps, TB * b + t + 1)
                    nc.scalar.activation(vx[e][:, t, 0:H * VW].rearrange("p (h v) -> p h v", v=VW)[:, :, 0:DH], psum[:, 6 + t, :].rearrange("p (h d) -> p h d", d=DH),
                                         ACT.Copy, scale=vinv[:, t:t + 1]).then_inc(v_sb, 1)

            def copy_piece(b, e, i):
                dst, g0, at = ((qst, 0, 0), (kst, NG, 0), (kst, NG, 1), (qst, 0, 2))[i]
                rows = slice(DH * at, DH * (at + 1))
                if i == 0:
                    act.wait_ge(hi_ready, OG // 2 * (b + 1))
                nc.scalar.activation(dst[e][rows].rearrange("p (g j) n -> p g j n", j=HG)[:, :, at, :],
                                     hi[rows, g0:g0 + NG, :].bitcast(F32), ACT.Copy).then_inc(stack_copy, 1)

            def attn_columns(b):
                act.wait_ge(aT_ps, b + 1)
                nc.scalar.activation(aT[:].rearrange("p k (t n) -> p t k n", n=P),
                                     bankbf(6).rearrange("p (t k n) -> p t k n", t=TB, k=KC), ACT.Copy).then_inc(aT_sb, 1)

            def max_columns(b):
                act.wait_ge(c_ps, b + 1)
                if not (isinstance(b, int) and b == 0):
                    act.wait_ge(s_crow, 16 * b)
                nc.scalar.activation(ct[:], psum[0:H, 4, 0:N], ACT.Copy, scale=-1.0).then_inc(ct_ready, 1)

            def values_out(b, p):
                act.wait_ge(pv_done, PAIRS * b + p + 1)
                if not (isinstance(b, int) and b == 0 and p < 2):
                    if p % 2:
                        act.wait_ge(tv_ps, NG * b + p // 2)
                nc.scalar.activation(ot[:, p % 2], psum[:, 4, 0:N], ACT.Copy).then_inc(ot_ready, 1)

            def rows_out(b, g):
                act.wait_ge(tv_ps, NG * b + g + 1)
                if not (isinstance(b, int) and b == 0 and g < 2):
                    act.wait_ge(na_done, NG * b + g - 1)
                nc.scalar.activation(orow[:, g % 2].rearrange("p a t v -> p (a t v)"), psum[:, 5, :], ACT.Copy).then_inc(orow_ready, 1)

            def softmax(b, e):
                for p in range(PAIRS):
                    n = PAIRS * b + p
                    act.wait_ge(st_ps, n + 1)
                    if not (isinstance(b, int) and n < 2):
                        act.wait_ge(pv_done, n - 1)
                    s = 2 * (p % 2)
                    nc.scalar.activation(pt[:, p % 2], psum[:, s:s + 2, 0:N + P], ACT.Exp, scale=SCALE).then_inc(exp_done, 1)
                    if p:
                        values_out(b, p - 1)
                    if p < 4 and not (isinstance(b, int) and (b == 0 or b == B - 1)):
                        copy_piece(b + 1, 1 - e, p)
                    if p >= 3 and p % 2:
                        rows_out(b, (p - 3) // 2)
                    if p == 2 and not (isinstance(b, int) and b == 0):
                        attn_columns(b - 1)
                values_out(b, PAIRS - 1)
                rows_out(b, NG - 1)

            def batch(b, e):
                softmax(b, e)
                if not (isinstance(b, int) and b == B - 1):
                    max_columns(b + 1)
                if not (isinstance(b, int) and b + 2 >= B):
                    evacuate_inputs(b + 2, e)

            evacuate_inputs(0, 0)
            act.wait_ge(s_wT, WALL // 2)
            for i in range(4):
                copy_piece(0, 0, i)
            act.wait_ge(stack_copy, 4)
            evacuate_inputs(1, 1)
            for i in range(4):
                copy_piece(1, 1, i)
            max_columns(0)
            all_batches(act, batch)
            attn_columns(B - 1)

        @block.vector
        def _(dve):
            def link(ins):
                chain[0] += 1
                ins.then_inc(s_dve, 1)
                dve.wait_ge(s_dve, chain[0])

            dve.wait_ge(s_const, 12)
            link(nc.vector.tensor_copy(identb[:], ident[:]))
            for i in range(WALL // WCH):
                dve.wait_ge(s_w[i], 16)
                ins = nc.vector.tensor_reduce(wsum[:, i * WCH:(i + 1) * WCH], wraw[:, i * WCH:(i + 1) * WCH, :], X, ALU.add,
                                              apply_absolute_value=True)
            link(ins)
            nc.vector.tensor_reduce(wtot[:, 0:1], wsum[:, 0:WT], X, ALU.add)
            nc.vector.tensor_reduce(wtot[:, 1:2], wsum[:, WT:WALL], X, ALU.add).then_inc(s_wsum, 1)
            dve.wait_ge(s_wtot_ps, 1)
            nc.vector.tensor_scalar(wmean[:, 0:1], psum[:, 0, 0:1], 1.0 / (3 * C * C), 1e-05, ALU.mult, ALU.max)
            link(nc.vector.tensor_scalar(wmean[:, 1:2], psum[:, 0, 1:2], 1.0 / (C * C), 1e-05, ALU.mult, ALU.max))
            link(nc.vector.reciprocal(wscale[:], wmean[:]))
            for i in range(WALL // WCH):
                part = slice(i * WCH, (i + 1) * WCH)
                w = 0 if i < WT // WCH else 1
                link(nc.vector.tensor_scalar(wraw[:, part, :], wraw[:, part, :], wscale[:, w:w + 1], MAGIC, ALU.mult, ALU.add))
                link(nc.vector.tensor_scalar(wraw[:, part, :], wraw[:, part, :], MAGIC, 1.0, ALU.subtract, ALU.min))
                nc.vector.tensor_scalar(wtern[:, part, :], wraw[:, part, :], -1.0, None, ALU.max).then_inc(s_tern, 1)

            def step(b, name, ins):
                ins.then_inc(own_sem[name], 1)
                dve.wait_ge(own_sem[name], b + 1)

            def quantize(b):
                x_in = xs[:, ds(TB * b, TB), :]
                if isinstance(b, int):
                    dve.wait_ge(s_x[min(b, 1)], 16)
                if not (isinstance(b, int) and b == 0):
                    dve.wait_ge(v_sb, TB * b)
                step(b, "amax", nc.vector.tensor_reduce(amax[:], x_in, X, ALU.max, apply_absolute_value=True))
                step(b, "clip", nc.vector.tensor_scalar(amax[:], amax[:], 1e-05, None, ALU.max))
                step(b, "rec", nc.vector.reciprocal(qs_r[:], amax[:]))
                nc.vector.tensor_scalar(vinv[:], amax[:], 1.0 / 127.0, wmean[:, 0:1], ALU.mult, ALU.mult)
                step(b, "scale", nc.vector.tensor_scalar(qs[:], qs_r[:], 127.0, None, ALU.mult))
                for t in range(TB):
                    ins = nc.vector.tensor_scalar(xq_t[:, t, :], xs[:, ds(TB * b + t, 1), :].rearrange("p a c -> p (a c)"),
                                                  qs[:, t:t + 1], MAGIC, ALU.mult, ALU.add)
                step(b, "round", ins)

            def quantize_out(b):
                nc.vector.tensor_scalar(xq[:], xq_t[:], MAGIC, 127.0, ALU.subtract, ALU.min).then_inc(xq_ready, 1)

            def scale_qk(b, e):
                dve.wait_ge(r_sb, b + 1)
                if not (isinstance(b, int) and b == 0):
                    dve.wait_ge(s_stack[1 - e], stacked(b - 1, 1 - e, STACK))
                for k in range(OG // 2):
                    dve.wait_ge(qk_ps, OG // 2 * b + k + 1)
                    nc.vector.tensor_tensor(real[:, 2 * k:2 * k + 2, :], psum[:, k, :].rearrange("p (a n) -> p a n", n=N),
                                            rs[:].unsqueeze(1).to_broadcast([P, 2, N]), ALU.mult).then_inc(real_ready, 1)

            def row_max(b, pairs):
                for h in range(2 * pairs[0], 2 * pairs[-1] + 2):
                    dve.wait_ge(s_ps, H * b + h + 1)
                    if h == 0 and not (isinstance(b, int) and b == 0):
                        dve.wait_ge(c_ps, b)
                    nc.vector.tensor_reduce(cx[:, 1, h:h + 1], psum[:, 6 + h % 2, 0:N], X, ALU.max)
                    nc.vector.tensor_reduce(cx[:, 0, h:h + 1], psum[:, 6 + h % 2, N:N + P], X, ALU.max).then_inc(mx_done, 1)

            def residual(b):
                if not (isinstance(b, int) and b == 0):
                    dve.wait_ge(x1_done, b)
                for t in range(TB):
                    dve.wait_ge(proj_ps, TB * b + t + 1)
                    row = xs[:, ds(TB * b + t, 1), :].rearrange("p a c -> p (a c)")
                    ins = nc.vector.scalar_tensor_tensor(resid[:, t, :], psum[:, 7 - t, :], pscale[:, 1, t:t + 1], row, ALU.mult, ALU.add)
                    ins.then_inc(res_done, 1)

            def statistics(b):
                for t in range(TB):
                    dve.wait_ge(res_done, TB * b + t + 1)
                    ins = nc.vector.bn_stats(stats[:, t, :], resid[:, t, :])
                ins.then_inc(own_sem["stats"], 1)
                dve.wait_ge(own_sem["stats"], b + 1)

            def variance(b):
                for t in range(TB):
                    ins = nc.vector.bn_aggr(mv[:, t, :], stats[:, t, :])
                step(b, "aggr", ins)
                nc.vector.tensor_scalar(ve[:], mv[:, :, 1], LN_EPS, None, ALU.add).then_inc(var_ready, 1)

            def normalise(b):
                dve.wait_ge(r0_ready, b + 1)
                step(b, "nt1", nc.vector.tensor_tensor(nt1[:], r0[:], r0[:], ALU.mult))
                step(b, "nt2", nc.vector.tensor_tensor(nt2[:], nt1[:], ve[:], ALU.mult))
                step(b, "nt3", nc.vector.tensor_scalar(nt1[:], nt2[:], -0.5, 1.5, ALU.mult, ALU.add))
                step(b, "nt4", nc.vector.tensor_tensor(rstd[:], nt1[:], r0[:], ALU.mult))
                for t in range(TB):
                    row = xs[:, ds(TB * b + t, 1), :].rearrange("p a c -> p (a c)")
                    ins = nc.vector.tensor_scalar(row, resid[:, t, :], mv[:, t, 0:1], rstd[:, t:t + 1], ALU.subtract, ALU.mult)
                ins.then_inc(x1_done, 1)

            def attention_rows(b, g):
                dve.wait_ge(orow_ready, NG * b + g + 1)
                o = orow[:, g % 2].rearrange("p a t (x v) -> p t a x v", v=VPAD)
                ins = nc.vector.reciprocal(rec[:, g], o[:, :, :, :, DH])
                ins.then_inc(own_sem["srec"], 1)
                dve.wait_ge(own_sem["srec"], NG * b + g + 1)
                for t in range(TB):
                    ins = nc.vector.tensor_tensor(
                        attn[:, t, g * P:(g + 1) * P].rearrange("p (a x d) -> p a x d", a=2, d=DH), o[:, t, :, :, 0:DH],
                        rec[:, g, t].unsqueeze(3).to_broadcast([P, 2, 2, DH]), ALU.mult)
                ins.then_inc(na_done, 1)

            def quantize_rows(b):
                dve.wait_ge(na_done, NG * b + NG)
                step(b, "amax2", nc.vector.tensor_reduce(amax2[:], attn[:], X, ALU.max, apply_absolute_value=True))
                step(b, "clip2", nc.vector.tensor_scalar(amax2[:], amax2[:], 1e-05, None, ALU.max))
                step(b, "rec2", nc.vector.reciprocal(qs2_r[:], amax2[:]))
                nc.vector.tensor_scalar(pscale[:, 1, :], amax2[:], 1.0 / 127.0, wmean[:, 1:2], ALU.mult, ALU.mult)
                step(b, "scale2", nc.vector.tensor_scalar(qs2[:], qs2_r[:], 127.0, None, ALU.mult))
                for t in range(TB):
                    ins = nc.vector.tensor_scalar(attn[:, t, :], attn[:, t, :], qs2[:, t:t + 1], MAGIC, ALU.mult, ALU.add)
                step(b, "round2", ins)
                nc.vector.tensor_scalar(aq[:], attn[:], MAGIC, 127.0, ALU.subtract, ALU.min).then_inc(aq_ready, 1)
                dve.wait_ge(aq_ready, b + 1)

            def batch(b, e):
                fixed = isinstance(b, int)
                first, final = fixed and b == 0, fixed and b == B - 1
                project_next = not (fixed and b + 2 >= B)
                if project_next:
                    quantize(b + 2)
                attention_rows(b, 0)
                if not first:
                    residual(b - 1)
                if project_next:
                    quantize_out(b + 2)
                if not first:
                    statistics(b - 1)
                if not final:
                    row_max(b + 1, range(0, 4))
                attention_rows(b, 1)
                if not first:
                    variance(b - 1)
                if not final:
                    row_max(b + 1, range(4, PAIRS))
                attention_rows(b, 2)
                if not first:
                    normalise(b - 1)
                attention_rows(b, 3)
                if project_next:
                    scale_qk(b + 2, e)
                quantize_rows(b)

            quantize(0)
            quantize_out(0)
            scale_qk(0, 0)
            quantize(1)
            quantize_out(1)
            scale_qk(1, 1)
            row_max(0, range(PAIRS))
            all_batches(dve, batch)
            residual(B - 1)
            statistics(B - 1)
            nc.vector.tensor_scalar(nt1[:], stats[:, :, 0], 1.0, None, ALU.mult)
            variance(B - 1)
            normalise(B - 1)

        @block.tensor
        def _(pe):
            mm = nc.tensor.matmul
            pe.wait_ge(s_wsum, 1)
            mm(psum[:, 0, 0:2], ones[:], wtot[:], start=True, stop=True).then_inc(s_wtot_ps, 1)
            for i in range(WALL // 2):
                pe.wait_ge(s_tern, 2 * i // WCH + 1)
                if i >= 8:
                    pe.wait_ge(s_wT, i - 7)
                for t in range(2):
                    for k in range(KC):
                        at = (t * KC + k) * P
                        ins = nc.tensor.transpose(bankbf(i % 8)[:, at:at + P], wtern[:, 2 * i + t, k * P:(k + 1) * P], identb[:])
                ins.then_inc(s_wT_ps, 1)
            pe.wait_ge(s_wT, WALL // 2)

            def qkv(b):
                pe.wait_ge(xq_ready, b + 1)
                if not (isinstance(b, int) and b == 0):
                    pe.wait_ge(v_sb, TB * b)
                if not (isinstance(b, int) and b < 2):
                    pe.wait_ge(mx_done, H * b)
                for t in range(TB):
                    for k in range(KC):
                        at = (t * KC + k) * P
                        ins = nc.tensor.transpose(bankbf(6)[:, at:at + P], xq[:, t, k * P:(k + 1) * P], identb[:])
                ins.then_inc(xT_ps, 1)
                for t in range(TB):
                    ins = mm(psum[:, 7, t * P:(t + 1) * P], vinv[:, t:t + 1].to_broadcast([P, P]), ident[:], start=True, stop=True)
                ins.then_inc(r_ps, 1)
                pe.wait_ge(xT_sb, b + 1)
                if isinstance(b, int) and b == 1:
                    pe.wait_ge(real_ready, OG // 2)
                elif not (isinstance(b, int) and b == 0):
                    pe.wait_ge(exp_done, PAIRS * (b - 1))
                for o in range(OG):
                    for k in range(KC):
                        ins = mm(psum[:, o // 2, (o % 2) * N:(o % 2 + 1) * N], wT[:, k, o * P:(o + 1) * P], xqT[:, k, :],
                                 start=(k == 0), stop=(k == KC - 1))
                    if o % 2:
                        ins.then_inc(qk_ps, 1)
                pe.wait_ge(r_sb, b + 1)
                for t in range(TB):
                    for k in range(KC):
                        ins = mm(psum[:, 6 + t, :], xqT[:, k, t * P:(t + 1) * P], wT[:, k, OG * P:OG * P + C],
                                 start=(k == 0), stop=(k == KC - 1))
                    ins.then_inc(v_ps, 1)

            def scores_for_max(b, e, pairs):
                for h in range(2 * pairs[0], 2 * pairs[-1] + 2):
                    if h == 0:
                        pe.wait_ge(s_stack[e], stacked(b, e, STACK))
                        pe.wait_ge(stack_copy, 4 * (b + 1))
                        pe.wait_ge(v_sb, TB * (b + 1) if not (isinstance(b, int) and b == 0) else 2 * TB)
                        if not (isinstance(b, int) and b < 2):
                            pe.wait_ge(res_done, TB * (b - 1))
                    elif h >= 2:
                        pe.wait_ge(mx_done, H * b + h - 1)
                    o = psum[:, 6 + h % 2, :]
                    mm(o[:, P:2 * P], identb[:], mask_s[:], start=True, stop=False, skip_group_check=True)
                    mm(o[:, N:N + P], identb[:], mask_s[:], start=False, stop=False, skip_group_check=True)
                    mm(o[:, 0:N], qst[e][0:KS, h, P:N], kst[e][0:KS, h, :], start=False, stop=False, skip_group_check=True)
                    mm(o[:, N:N + P], qst[e][0:KS, h, 0:P], kst[e][0:KS, h, 0:P], start=False, stop=True,
                       skip_group_check=True).then_inc(s_ps, 1)

            def turn_max(b):
                pe.wait_ge(mx_done, H * (b + 1))
                if not (isinstance(b, int) and b == 0):
                    pe.wait_ge(ot_ready, PAIRS * b)
                for t in range(TB):
                    ins = nc.tensor.transpose(psum[0:H, 4, t * P:(t + 1) * P], cx[:, t, :], ident[:])
                ins.then_inc(c_ps, 1)

            def turn_rows(b):
                pe.wait_ge(aq_ready, b + 1)
                for t in range(TB):
                    for k in range(KC):
                        at = (t * KC + k) * P
                        ins = nc.tensor.transpose(bankbf(6)[:, at:at + P], aq[:, t, k * P:(k + 1) * P], identb[:])
                ins.then_inc(aT_ps, 1)

            def project(b):
                pe.wait_ge(aT_sb, b + 1)
                for t in range(TB):
                    for k in range(KC):
                        ins = mm(psum[:, 7 - t, :], aT[:, k, t * P:(t + 1) * P], wT[:, k, WT * P:WALL * P],
                                 start=(k == 0), stop=(k == KC - 1))
                    ins.then_inc(proj_ps, 1)

            def scores(b, e, p):
                if p >= 2:
                    pe.wait_ge(exp_done, PAIRS * b + p - 1)
                for x in range(2):
                    bank = 2 * (p % 2) + x
                    mm(psum[:, bank, 0:P], identb[:], mask_st[:], start=True, stop=False, skip_group_check=True)
                    mm(psum[:, bank, N:N + P], identb[:], mask_st[:], start=False, stop=False, skip_group_check=True)
                for x in range(2):
                    bank = 2 * (p % 2) + x
                    h = 2 * p + x
                    mm(psum[:, bank, 0:N], kst[e][0:KS + 1, h, 0:P], qst[e][0:KS + 1, h, :], start=False, stop=False, skip_group_check=True)
                    ins = mm(psum[:, bank, N:N + P], kst[e][0:KS + 1, h, P:N], qst[e][0:KS + 1, h, P:N], start=False, stop=True,
                             skip_group_check=True)
                ins.then_inc(st_ps, 1)

            def values(b, e, p):
                pe.wait_ge(exp_done, PAIRS * b + p + 1)
                if not (isinstance(b, int) and b == 0 and p == 0):
                    pe.wait_ge(ot_ready, PAIRS * b + p)
                for x in range(2):
                    at = (2 * p + x) * VW
                    r = slice(VPAD * x, VPAD * (x + 1))
                    mm(psum[r, 4, 0:N], vx[e][:, 0, at:at + VPAD], pt[:, p % 2, x, 0:N], start=True, stop=False, skip_group_check=True)
                    ins = mm(psum[r, 4, P:N], vx[e][:, 1, at:at + VPAD], pt[:, p % 2, x, N:N + P], start=False, stop=True,
                             skip_group_check=True)
                ins.then_inc(pv_done, 1)

            def turn_values(b, p):
                pe.wait_ge(ot_ready, PAIRS * b + p + 1)
                if p % 2 == 0 and not (isinstance(b, int) and b == 0 and p == 0):
                    pe.wait_ge(orow_ready, NG * b + p // 2)
                for t in range(TB):
                    at = (p % 2 * TB + t) * P
                    ins = nc.tensor.transpose(psum[:, 5, at:at + P], ot[:, p % 2, t * P:(t + 1) * P], ident[:])
                if p % 2:
                    ins.then_inc(tv_ps, 1)

            def batch(b, e):
                fixed = isinstance(b, int)
                final = fixed and b == B - 1
                if not final:
                    pe.wait_ge(real_ready, OG // 2 * (b + 2))
                if not (fixed and b == 0):
                    pe.wait_ge(exp_done, PAIRS * b)
                pe.wait_ge(v_sb, TB * (b + 1) if final else TB * (b + 2))
                if fixed and b >= B - 2:
                    pe.wait_ge(mx_done, H * (b + 1))
                pe.wait_ge(s_crow, 16 * (b + 1))
                pe.wait_ge(s_stack[e], stacked(b, e, STACK))
                for p in range(PAIRS):
                    scores(b, e, p)
                    late = 2 * (p - PAIRS // 2)
                    if late >= 0 and not final:
                        scores_for_max(b + 1, 1 - e, [late])
                    if p:
                        values(b, e, p - 1)
                    if late >= 0 and not final:
                        scores_for_max(b + 1, 1 - e, [late + 1])
                    if p >= 2:
                        turn_values(b, p - 2)
                    if p == 2 and not (fixed and b == 0):
                        turn_rows(b - 1)
                    if p == 3 and not (fixed and b == 0):
                        project(b - 1)
                values(b, e, PAIRS - 1)
                turn_values(b, PAIRS - 2)
                turn_values(b, PAIRS - 1)
                if not final:
                    turn_max(b + 1)
                if not (fixed and b + 2 >= B):
                    qkv(b + 2)

            qkv(0)
            qkv(1)
            scores_for_max(0, 0, range(PAIRS))
            turn_max(0)
            pe.wait_ge(ones_row, 2)
            all_batches(pe, batch)
            turn_rows(B - 1)
            project(B - 1)

        stage_a.__exit__(None, None, None)
        if STAGE == 1:
            return

        PAIRN = I * (I + 1) // 2
        off = [sum(I - r for r in range(s)) for s in range(I)]
        where[0] = mark_b
        cT = sb("cT", [P, LB, B, N])
        qT = sb("qT", [P, LB, B, N])
        mark_t = where[0]
        yT = sb("yT", [P, LB, B, N])
        prod = [sb(f"prod{i}", [P, LB * B, I, I]) for i in range(2)]
        assert where[0] >= wraw_at
        kv = [sb(f"kv{i}", [P, LB * B, PAIRN]) for i in range(2)]
        toep = [sb(f"toep{i}", [P, L]) for i in range(2)]
        POOL_SUMS = 10
        half = sb("half", [P, POOL_SUMS, I, I // 2])
        quarter = sb("quarter", [P, POOL_SUMS, I, I // 4])
        stats2 = sb("stats2", [P, NT, 6])
        mv2 = sb("mv2", [P, NT, 2])
        ve2 = sb("ve2", [P, NT])
        shift2 = sb("shift2", [P, NT])
        g2 = sb("g2", [P, NT])
        n1 = sb("n1", [P, NT])
        n2 = sb("n2", [P, NT])
        rstd2 = sb("rstd2", [P, NT])
        end_b = where[0]
        E, _, F = A["wg"].shape
        FT = [(f, min(P, F - f)) for f in range(0, F, P)]
        NF = len(FT)
        top = nc.sbuf_usable_end // 32 * 32 - 4 * (2 * KC * F + NF * C + C + P)
        assert end_b <= top
        where[0] = top
        stg = [sb("stg_g", [P, KC, F]), sb("stg_u", [P, KC, F]), sb("stg_d", [P, NF, C])]
        rin = sb("rin", [E, C])
        below = sb("below", [P, P])
        below_ready = sem("below_ready")
        s_r = sem("s_r")
        s_stg = [sem("s_stg_g"), sem("s_stg_u"), sem("s_stg_d")]
        assert mark_t <= cin_at

        cT_ps = sem("cT_ps")
        qT_ps = sem("qT_ps")
        cT_done = sem("cT_done")
        qT_done = sem("qT_done")
        s_toep = [sem("s_toep0"), sem("s_toep1")]
        kv_sq = sem("kv_sq")
        kv_ready = sem("kv_ready")
        half_ready = sem("half_ready")
        quarter_ready = sem("quarter_ready")
        yp_done = sem("yp_done")
        y_ps = sem("y_ps")
        ym_done = sem("ym_done")
        y_done = sem("y_done")
        yT_ps = sem("yT_ps")
        res2 = sem("res2")
        own2 = sem("own2")
        ve2_ready = sem("ve2_ready")
        shift2_ready = sem("shift2_ready")
        g2_ready = sem("g2_ready")
        x2_done = sem("x2_done")

        by_half = list(range(0, NT, 2)) + list(range(1, NT, 2))
        LG2 = 4

        def conv_out_bank(u):
            return psum[:, u % 8, :]

        with nc.Block() as block:
            @block.sync
            def _(sp):
                def load(h, e, first):
                    if not first:
                        sp.wait_ge(y_ps, h - 1)
                    src = bass.AP(krow.tensor, 1, [[KP, HK], [1, P], [1, L]])[ds(h, 1)]
                    sp.dma_start(toep[e][:], src.rearrange("a p l -> (a p) l")).then_inc(s_toep[e], 16)
                for e in range(2):
                    load(e, e, True)
                with sp.Fori(1, HK // 2) as hp:
                    for e in range(2):
                        load(2 * hp + e, e, False)
                sp.dma_start(stg[0][:], A["sg"][:, 0:F].rearrange("(k p) f -> p k f", p=P)).then_inc(s_stg[0], 16)
                sp.dma_start(stg[1][:], A["su"][:, 0:F].rearrange("(k p) f -> p k f", p=P)).then_inc(s_stg[1], 16)
                full = F // P
                sp.dma_start(stg[2][:, 0:full, :], A["sd"][0:full * P, :].rearrange("(k p) c -> p k c", p=P)).then_inc(s_stg[2], 16)
                sp.dma_start(stg[2][0:F - full * P, full, :], A["sd"][full * P:F, :]).then_inc(s_stg[2], 16)
                sp.dma_start(rin[:], A["router"]).then_inc(s_r, 16)
                for at in s_stg[0:2] + [s_r]:
                    sp.wait_ge(at, 16)
                sp.wait_ge(s_stg[2], 32)
                if STAGE == 2:
                    sp.wait_ge(x2_done, 1)
                    sp.dma_start(out_tok, xs[:]).then_inc(s_out, 16)
                    sp.wait_ge(s_out, 16)

            @block.gpsimd
            def _(pool):
                nc.gpsimd.memset(below[:], 1.0).then_inc(below_ready, 1)
                pool.wait_ge(below_ready, 1)
                nc.gpsimd.affine_select(out=below[:], in_=below[:], compare_op=ALU.is_gt, fill=0.0, base=0,
                                        pattern=[[1, P]], channel_multiplier=-1).then_inc(below_ready, 1)
                pool.wait_ge(below_ready, 2)
                pool.wait_ge(cT_done, NT // 2)

                def products(h, e, first):
                    if not first:
                        pool.wait_ge(y_ps, h - 1)
                    for s in range(1, I):
                        a = cT[:].rearrange("p k b c -> p (k b) c")
                        ins = nc.gpsimd.tensor_tensor(kv[e][:, :, off[s]:off[s] + I - s], a[:, :, ds(I * h, I - s)],
                                                      a[:, :, ds(I * h + s, I - s)], ALU.mult)
                    ins.then_inc(kv_ready, 1)

                def sum_over_i(h, e, first=False):
                    mine = prod[e][:, LB * B - POOL_SUMS:LB * B]
                    pool.wait_ge(ym_done, h + 1)
                    if not first:
                        pool.wait_ge(yp_done, h)
                    nc.gpsimd.tensor_tensor(half[:], mine[:, :, :, 0:I // 2], mine[:, :, :, I // 2:I], ALU.add).then_inc(half_ready, 1)
                    pool.wait_ge(half_ready, h + 1)
                    nc.gpsimd.tensor_tensor(quarter[:], half[:, :, :, 0:I // 4], half[:, :, :, I // 4:I // 2], ALU.add).then_inc(quarter_ready, 1)
                    pool.wait_ge(quarter_ready, h + 1)
                    nc.gpsimd.tensor_tensor(yT[:].rearrange("p k b c -> p (k b) c")[:, LB * B - POOL_SUMS:LB * B, ds(I * h, I)],
                                            quarter[:, :, :, 0], quarter[:, :, :, 1], ALU.add).then_inc(yp_done, 1)

                products(0, 0, True)
                products(1, 1, True)
                products(2, 0, False)
                sum_over_i(0, 0, True)
                pool.wait_ge(cT_done, NT)
                products(3, 1, False)
                sum_over_i(1, 1)
                with pool.Fori(1, HK // 2 - 1) as hp:
                    for e in range(2):
                        products(2 * hp + e + 2, e, False)
                        sum_over_i(2 * hp + e, e)
                sum_over_i(HK - 2, 0)
                sum_over_i(HK - 1, 1)
                for g in range(NT // LG2):
                    part = slice(LG2 * g, LG2 * (g + 1))
                    pool.wait_ge(ve2_ready, g + 1)
                    nc.gpsimd.tensor_tensor(g2[:, part], ve2[:, part], mhalf[:, part], ALU.pow).then_inc(g2_ready, 1)

            @block.scalar
            def _(act):
                def ctx_columns(n):
                    b, hc = by_half[n] // 2, by_half[n] % 2
                    act.wait_ge(cT_ps, n + 1)
                    nc.scalar.activation(cT[:, :, b, hc * P:(hc + 1) * P], psum[:, (2 * n) % 8, :].rearrange("p (k n) -> p k n", n=P),
                                         ACT.Copy).then_inc(cT_done, 1)

                def squares(h, e, first):
                    if not first:
                        act.wait_ge(y_ps, h - 1)
                    a = cT[:].rearrange("p k b c -> p (k b) c")
                    nc.scalar.activation(kv[e][:, :, 0:I], a[:, :, ds(I * h, I)], ACT.Square).then_inc(kv_sq, 1)

                for n in range(NT // 2):
                    ctx_columns(n)
                act.wait_ge(cT_done, NT // 2)
                squares(0, 0, True)
                squares(1, 1, True)
                for n in range(NT // 2, NT):
                    ctx_columns(n)
                act.wait_ge(cT_done, NT)
                with act.Fori(1, HK // 2) as hp:
                    for e in range(2):
                        squares(2 * hp + e, e, False)
                for g in range(NT // LG2):
                    act.wait_ge(shift2_ready, g + 1)
                    for u in range(LG2 * g, LG2 * (g + 1)):
                        ins = nc.scalar.activation(xs[:, u, :], xs[:, u, :], ACT.Identity, bias=shift2[:, u:u + 1], scale=rstd2[:, u:u + 1])
                ins.then_inc(x2_done, 1)

            @block.vector
            def _(dve):
                for n, u in enumerate(by_half):
                    b, hc = u // 2, u % 2
                    dve.wait_ge(qT_ps, n + 1)
                    nc.vector.tensor_copy(qT[:, :, b, hc * P:(hc + 1) * P],
                                          psum[:, (2 * n + 1) % 8, :].rearrange("p (k n) -> p k n", n=P)).then_inc(qT_done, 1)
                dve.wait_ge(qT_done, NT)

                def scale_by_q(h, e, first):
                    dve.wait_ge(y_ps, h + 1)
                    if not first:
                        dve.wait_ge(y_done, h - 1)
                        dve.wait_ge(yp_done, h - 1)
                    flat = prod[e][:].rearrange("p a j i -> p a (j i)")
                    y = psum[:, 4 * e:4 * e + LB, 0:B * PAIRN].rearrange("p k (b n) -> p k b n", n=PAIRN)
                    for s in range(I):
                        ys = y[:, :, :, off[s]:off[s] + I - s]
                        last = (I - s - 1) * (I + 1) + 1
                        for shift, at in ((0, s * I), (s, s))[0:1 + (s > 0)]:
                            o = flat[:, :, at:at + last:I + 1].rearrange("p (k b) n -> p k b n", b=B)
                            ins = nc.vector.tensor_tensor(o, ys, qT[:, :, :, ds(I * h + shift, I - s)], ALU.mult)
                    ins.then_inc(ym_done, 1)

                def sum_over_i(h, e):
                    dve.wait_ge(ym_done, h + 1)
                    nc.vector.tensor_reduce(yT[:].rearrange("p k b c -> p (k b) c")[:, 0:LB * B - POOL_SUMS, ds(I * h, I)],
                                            prod[e][:, 0:LB * B - POOL_SUMS], X, ALU.add)\
                       .then_inc(y_done, 1)

                scale_by_q(0, 0, True)
                scale_by_q(1, 1, True)
                sum_over_i(0, 0)
                with dve.Fori(1, HK // 2) as hp:
                    for e in range(2):
                        scale_by_q(2 * hp + e, e, False)
                        sum_over_i(2 * hp + e - 1, 1 - e)
                sum_over_i(HK - 1, 1)

                links = [0]

                def link(ins):
                    links[0] += 1
                    ins.then_inc(own2, 1)
                    dve.wait_ge(own2, links[0])

                def scales(g):
                    part = slice(LG2 * g, LG2 * (g + 1))
                    dve.wait_ge(g2_ready, g + 1)
                    link(nc.vector.tensor_tensor(n1[:, part], g2[:, part], g2[:, part], ALU.mult))
                    link(nc.vector.tensor_tensor(n2[:, part], n1[:, part], ve2[:, part], ALU.mult))
                    link(nc.vector.tensor_scalar(n1[:, part], n2[:, part], -0.5, 1.5, ALU.mult, ALU.add))
                    link(nc.vector.tensor_tensor(rstd2[:, part], n1[:, part], g2[:, part], ALU.mult))
                    nc.vector.scalar_tensor_tensor(shift2[:, part], mv2[:, part, 0], -1.0, rstd2[:, part], ALU.mult, ALU.mult)\
                        .then_inc(shift2_ready, 1)

                for g in range(NT // LG2):
                    tiles = range(LG2 * g, LG2 * (g + 1))
                    for u in tiles:
                        dve.wait_ge(yT_ps, u + 1)
                        nc.vector.tensor_tensor(xs[:, u, :], xs[:, u, :], conv_out_bank(u), ALU.add).then_inc(res2, 1)
                    for u in tiles:
                        dve.wait_ge(res2, u + 1)
                        ins = nc.vector.bn_stats(stats2[:, u, :], xs[:, u, :])
                    link(ins)
                    for u in tiles:
                        ins = nc.vector.bn_aggr(mv2[:, u, :], stats2[:, u, :])
                    link(ins)
                    part = slice(LG2 * g, LG2 * (g + 1))
                    nc.vector.tensor_scalar(ve2[:, part], mv2[:, part, 1], LN_EPS, None, ALU.add).then_inc(ve2_ready, 1)
                    if g:
                        scales(g - 1)
                scales(NT // LG2 - 1)

            @block.tensor
            def _(pe):
                mm = nc.tensor.matmul
                for n, u in enumerate(by_half):
                    if n >= 4:
                        pe.wait_ge(cT_done, n - 3)
                        pe.wait_ge(qT_done, n - 3)
                    for k in range(LB):
                        ins = nc.tensor.transpose(psum[:, (2 * n) % 8, k * P:(k + 1) * P], cin[:, u, k * P:(k + 1) * P], ident[:])
                    ins.then_inc(cT_ps, 1)
                    for k in range(LB):
                        ins = nc.tensor.transpose(psum[:, (2 * n + 1) % 8, k * P:(k + 1) * P], xs[:, u, k * P:(k + 1) * P], ident[:])
                    ins.then_inc(qT_ps, 1)
                pe.wait_ge(cT_done, NT)
                pe.wait_ge(qT_done, NT)

                def convolve(h, hp, e, first):
                    pe.wait_ge(s_toep[e], 16 * hp + 16)
                    pe.wait_ge(kv_sq, h + 1)
                    pe.wait_ge(kv_ready, h + 1)
                    if not first:
                        pe.wait_ge(ym_done, h - 1)
                    for lb in range(LB):
                        for mb in range(lb + 1):
                            d = slice((lb - mb) * P, (lb - mb + 1) * P)
                            ins = mm(psum[:, 4 * e + lb, 0:B * PAIRN], toep[e][:, d], kv[e][:, mb * B:(mb + 1) * B, :],
                                     start=(mb == 0), stop=(mb == lb))
                    ins.then_inc(y_ps, 1)
                for e in range(2):
                    convolve(e, 0, e, True)
                with pe.Fori(1, HK // 2) as hp:
                    for e in range(2):
                        convolve(2 * hp + e, hp, e, False)
                pe.wait_ge(y_done, HK)
                pe.wait_ge(yp_done, HK)
                for u in range(NT):
                    b, hc = u // 2, u % 2
                    if u >= 8:
                        pe.wait_ge(res2, u - 7)
                    for k in range(LB):
                        ins = nc.tensor.transpose(conv_out_bank(u)[:, k * P:(k + 1) * P], yT[:, k, b, hc * P:(hc + 1) * P], ident[:])
                    ins.then_inc(yT_ps, 1)

        if STAGE == 2:
            return

        UNITS = E + A["sg"].shape[1] // F
        assert UNITS == E + 2
        where[0] = mark_b
        over_sets, wh, wl = where[0], [], []
        for i in range(2):
            wh.append([sb(f"wh_g{i}", [P, KC, F], F32R), sb(f"wh_u{i}", [P, KC, F], F32R), sb(f"wh_d{i}", [P, NF, C], F32R)])
            wl.append([sb(f"wl_g{i}", [P, KC, F], F32R), sb(f"wl_u{i}", [P, KC, F], F32R), sb(f"wl_d{i}", [P, NF, C], F32R)])
            if i == 0:
                end_set = where[0]
        end_sets, where[0] = where[0], over_sets
        got = [sb(f"got{i}", [P, JT, 2, C]) for i in range(2)]
        fin = [sb(f"fin{i}", [P, JT, C]) for i in range(2)]
        assert where[0] <= end_set
        where[0] = end_sets
        sil = sb("sil", [P, NF, J])
        hr = sb("hr", [P, NF, J])
        hh = [sb(f"hh{i}", [P, NF, J], F32R) for i in range(2)]
        hl = [sb(f"hl{i}", [P, NF, J], F32R) for i in range(2)]
        xrow = [sb(f"xrow{i}", [P, JT, C]) for i in range(2)]
        xh = [sb(f"xh{i}", [P, KC, J], F32R) for i in range(2)]
        xl = [sb(f"xl{i}", [P, KC, J], F32R) for i in range(2)]
        yout = sb("yout", [P, JT, C])
        acc = sb("acc", [P, NT, C])
        rth = sb("rth", [P, KC, E], F32R)
        lgt = sb("lgt", [E, J])
        rtl = sb("rtl", [P, KC, E], F32R)
        lg = sb("lg", [P, NT, E])
        ex = sb("ex", [P, NT, E])
        gates = sb("gates", [P, NT, E])
        keys = sb("keys", [P, NT, E])
        rest = sb("rest", [P, NT, E])
        one1 = sb("one1", [P, NT, E])
        one2 = sb("one2", [P, NT, E])
        both = sb("both", [P, NT, E])
        slots = sb("slots", [P, NT, E])
        before_t = sb("before_t", [P, NT, E])
        count = sb("count", [P, E])
        jobs_e = sb("jobs_e", [P, E])
        end_e = sb("end_e", [P, E])
        base_e = sb("base_e", [P, E])
        le = sb("le", [P, RJOBS, E])
        exp_of = sb("exp_of", [P, RJOBS])
        exp_i = sb("exp_i", [P, RJOBS], I32)
        slot_f = sb("slot_f", [P, 2, NT])
        slot_i = sb("slot_i", [P, 2, NT], I32)
        gate = sb("gate", [P, 2, NT])
        t16 = [sb(f"t16_{i}", [P, NT]) for i in range(6)]
        stats3 = sb("stats3", [P, JT, 6])
        mv3 = [sb(f"mv3{i}", [P, JT, 2]) for i in range(2)]
        ve3 = [sb(f"ve3{i}", [P, JT]) for i in range(2)]
        g3 = sb("g3", [P, JT])
        m1 = sb("m1", [P, JT])
        m2 = sb("m2", [P, JT])
        rstd3 = [sb(f"rstd3{i}", [P, JT]) for i in range(2)]
        shift3 = [sb(f"shift3{i}", [P, JT]) for i in range(2)]
        assert where[0] <= top

        NA = NT // JT
        NE = 6
        FIRST_R = NA + NE
        FIRST_B = FIRST_R + RJOBS
        NJ = FIRST_B + NA - NE
        LAST_SET = RJOBS + 2
        TR, LG, DN = 5, 7, 3

        rt_ps = sem("rt_ps")
        rth_ready = sem("rth_ready")
        rt_ready = sem("rt_ready")
        lg_ps = sem("lg_ps")
        lgt_ps = sem("lgt_ps")
        lgt_ready = sem("lgt_ready")
        own3 = sem("own3")
        lg_ready = sem("lg_ready")
        ex_ready = sem("ex_ready")
        both_ready = sem("both_ready")
        pre_ps = sem("pre_ps")
        slot_ready = sem("slot_ready")
        s_scat = sem("s_scat")
        s_row = [sem("s_row0"), sem("s_row1")]
        xt_ps = sem("xt_ps")
        xh_ready = sem("xh_ready")
        xl_ready = sem("xl_ready")
        whi_gu = sem("whi_gu")
        wlo_gu = sem("wlo_gu")
        whi_d = sem("whi_d")
        wlo_d = sem("wlo_d")
        gu_ps = sem("gu_ps")
        sil_ready = sem("sil_ready")
        hr_ready = sem("hr_ready")
        hh_ready = sem("hh_ready")
        hl_ready = sem("hl_ready")
        dn_ps = sem("dn_ps")
        down_out = sem("down_out")
        y_copied = sem("y_copied")
        s_y = sem("s_y")
        s_got = [sem("s_got0"), sem("s_got1")]
        got_used = sem("got_used")
        own_f = {n: sem("own_f_" + n) for n in ("sum", "stats", "aggr", "m1", "m2", "m3", "m4")}
        ve3_ready = sem("ve3_ready")
        g3_ready = sem("g3_ready")
        shift_ready = sem("shift_ready")
        fin_ready = sem("fin_ready")

        with nc.Block() as block:
            class Job:
                def __init__(self, kind, c, m, e, wset, wp, own_d=False, next_gu=False):
                    self.kind, self.c, self.m, self.e, self.wset, self.wp = kind, c, m, e, wset, wp
                    self.own_d, self.next_gu = own_d, next_gu

            def job_a(c, e):
                return Job("a", c, c, e, 0, 0, next_gu=isinstance(c, int) and c == NA - 1)

            def job_s(c, e):
                fixed = isinstance(c, int)
                return Job("s", c, c + NA, (NA + e) % 2, 1, 1, own_d=fixed and c == 0, next_gu=fixed and c == NE - 1)

            def job_r(c, e):
                return Job("r", c, c + FIRST_R, (FIRST_R + e) % 2, c + 2, e, own_d=True, next_gu=True)

            def job_b(c):
                return Job("b", c, FIRST_B + c - NE, (FIRST_B + c - NE) % 2, LAST_SET, LAST_SET % 2, own_d=(c == NE))

            def passes(eng, job, after_a=None, after_s=None, before_last=None):
                job(job_a(0, 0), None)
                job(job_a(1, 1), job_a(0, 0))
                with eng.Fori(1, NA // 2 - 1) as i:
                    for e in range(2):
                        job(job_a(2 * i + e, e), job_a(2 * i + e - 1, 1 - e))
                job(job_a(NA - 2, 0), job_a(NA - 3, 1))
                job(job_a(NA - 1, 1), job_a(NA - 2, 0))
                if after_a is not None:
                    after_a()
                job(job_s(0, 0), job_a(NA - 1, 1))
                if after_s is not None:
                    after_s()
                with eng.Fori(0, (NE - 2) // 2) as i:
                    for e in range(2):
                        job(job_s(2 * i + 1 + e, 1 - e), job_s(2 * i + e, e))
                job(job_s(NE - 1, 1), job_s(NE - 2, 0))
                job(job_r(0, 0), job_s(NE - 1, 1))
                job(job_r(1, 1), job_r(0, 0))
                with eng.Fori(1, RJOBS // 2) as i:
                    for e in range(2):
                        job(job_r(2 * i + e, e), job_r(2 * i + e - 1, 1 - e))
                job(job_r(RJOBS - 1, 0), job_r(RJOBS - 2, 1))
                job(job_b(NE), job_r(RJOBS - 1, 0))
                for c in range(NE + 1, NA):
                    job(job_b(c), job_b(c - 1))
                job(None, job_b(NA - 1))

            def last(j):
                return isinstance(j.m, int) and j.m == NJ - 1

            def split_rows(i):
                if i < 2:
                    return [(slice(0, P), slice(0, KC))]
                return [(slice(0, P), slice(0, F // P)), (slice(0, F % P), slice(F // P, NF))]

            @block.sync
            def _(sp):
                def gate_up(n, wg, wu):
                    for i, w in enumerate((wg, wu)):
                        sp.wait_ge(wlo_gu, 2 * (n - 1) + i + 1)
                        sp.dma_start(stg[i][:], w.rearrange("(k p) f -> p k f", p=P)).then_inc(s_stg[i], 16)

                def down_weights(n, wd):
                    sp.wait_ge(wlo_d, n)
                    full = F // P
                    sp.dma_start(stg[2][:, 0:full, :], wd[0:full * P, :].rearrange("(k p) c -> p k c", p=P)).then_inc(s_stg[2], 16)
                    sp.dma_start(stg[2][0:F - full * P, full, :], wd[full * P:F, :]).then_inc(s_stg[2], 16)

                def expert(r):
                    return sp.value_load(exp_i[0:1, ds(r, 1)], min_val=0, max_val=E - 1)

                def part(name, e):
                    return A[name][ds(e, 1)].rearrange("a p f -> (a p) f")

                def routed_gate_up(r):
                    e = expert(r)
                    gate_up(r + 2, part("wg", e), part("wu", e))

                def routed_down(r):
                    down_weights(r + 2, part("wd", expert(r)))

                def shared_gate_up(n, u):
                    gate_up(n, A["sg"][:, u * F:(u + 1) * F], A["su"][:, u * F:(u + 1) * F])

                def shared_down(n, u):
                    down_weights(n, A["sd"][u * F:(u + 1) * F, :])

                def rows_of_tokens(m, e, c):
                    if not (isinstance(m, int) and m < 2):
                        sp.wait_ge(xt_ps, m - 1)
                    sp.dma_start(xrow[e][:], xs[:, ds(JT * c, JT), :]).then_inc(s_row[e], 16)

                def rows_of_slots(r, e):
                    sp.wait_ge(xt_ps, r + FIRST_R - 1)
                    buf = (FIRST_R + e) % 2
                    sp.dma_start(xrow[buf][:], xg[ds(r, 1)].rearrange("a (t p) c -> p (a t) c", p=P)).then_inc(s_row[buf], 16)

                def store(r):
                    sp.wait_ge(y_copied, r + 1)
                    sp.dma_start(yg[ds(r, 1)].rearrange("a (t p) c -> p (a t) c", p=P), yout[:]).then_inc(s_y, 16)

                rows_of_tokens(0, 0, 0)
                rows_of_tokens(1, 1, 1)
                shared_gate_up(1, 1)
                shared_down(1, 1)
                with sp.Fori(1, NA // 2) as i:
                    for e in range(2):
                        rows_of_tokens(2 * i + e, e, 2 * i + e)
                with sp.Fori(0, NE // 2) as i:
                    for e in range(2):
                        rows_of_tokens(2 * i + NA + e, (NA + e) % 2, 2 * i + e)
                sp.wait_ge(slot_ready, 1)
                routed_gate_up(0)
                routed_down(0)
                sp.wait_ge(s_scat, 16 * 2 * NT)
                for r in range(3):
                    rows_of_slots(r, r % 2)
                routed_gate_up(1)

                def beside(r, e):
                    fixed = isinstance(r, int)
                    if not fixed or r + 3 < RJOBS:
                        rows_of_slots(r + 3, 1 - e)
                    elif r + 3 - RJOBS < NA - NE:
                        m = FIRST_R + r + 3
                        rows_of_tokens(m, m % 2, NE + r + 3 - RJOBS)
                    if not fixed or r + 2 < RJOBS:
                        routed_gate_up(r + 2)
                    elif r + 2 == RJOBS:
                        shared_gate_up(LAST_SET, 1)
                    if not fixed or r + 1 < RJOBS:
                        routed_down(r + 1)
                    else:
                        shared_down(LAST_SET, 1)
                    if not (fixed and r == 0):
                        store(r - 1)
                beside(0, 0)
                with sp.Fori(0, (RJOBS - 4) // 2) as i:
                    for e in range(2):
                        beside(2 * i + 1 + e, 1 - e)
                for r in range(2 * ((RJOBS - 4) // 2) + 1, RJOBS):
                    beside(r, r % 2)
                store(RJOBS - 1)
                for c in range(NA):
                    sp.wait_ge(fin_ready, c + 1)
                    sp.dma_start(out_tok[:, JT * c:JT * (c + 1), :], xs[:, JT * c:JT * (c + 1), :]).then_inc(s_out, 16)
                sp.wait_ge(s_out, 16 * NA)

            @block.gpsimd
            def _(pool):
                pool.wait_ge(slot_ready, 1)
                for t in range(NT):
                    for w in range(2):
                        nc.gpsimd.indirect_dma_start(out=xg_rows, out_offset=bass.IndirectOffsetOnAxis(slot_i[:, w, t:t + 1], 0),
                                                     in_=xs[:, t, :], in_offset=None).then_inc(s_scat, 16)
                pool.wait_ge(s_y, 16 * RJOBS)

                def fetch(c):
                    for t in range(JT):
                        for w in range(2):
                            nc.gpsimd.indirect_dma_start(out=got[c % 2][:, t, w, :], out_offset=None, in_=yg_rows,
                                                         in_offset=bass.IndirectOffsetOnAxis(slot_i[:, w, JT * c + t:JT * c + t + 1], 0))\
                              .then_inc(s_got[c % 2], 16)
                fetch(0)
                fetch(1)
                for c in range(NA):
                    if c + 2 < NA:
                        pool.wait_ge(got_used, c + 1)
                        fetch(c + 2)
                    pool.wait_ge(ve3_ready, c + 1)
                    if c:
                        pool.wait_ge(own_f["m4"], c)
                    nc.gpsimd.tensor_tensor(g3[:], ve3[c % 2][:], mhalf[:, 0:JT], ALU.pow).then_inc(g3_ready, 1)

            @block.scalar
            def _(act):
                act.wait_ge(rt_ps, 1)
                nc.scalar.activation(rth[:], psum[:, LG, 0:KC * E].rearrange("p (k e) -> p k e", e=E), ACT.Copy).then_inc(rth_ready, 1)

                def exponentials():
                    act.wait_ge(lg_ready, 1)
                    nc.scalar.activation(ex[:], lg[:], ACT.Exp).then_inc(ex_ready, 1)

                def high_part(n, e, i):
                    act.wait_ge(s_stg[i], (16 if i < 2 else 32) * (n + 1))
                    for r, k in split_rows(i):
                        ins = nc.scalar.activation(wh[e][i][r, k, :], stg[i][r, k, :], ACT.Copy)
                    ins.then_inc(whi_gu if i < 2 else whi_d, 1)

                def high_rows(m, e):
                    act.wait_ge(xt_ps, m + 1)
                    nc.scalar.activation(xh[e][:].rearrange("p k (t n) -> p t k n", n=P),
                                         psum[:, TR:TR + JT, :].rearrange("p t (k n) -> p t k n", n=P), ACT.Copy).then_inc(xh_ready, 1)

                def job(j, prev):
                    for f, (_, w) in enumerate(FT if j else ()):
                        act.wait_ge(gu_ps, NF * j.m + f + 1)
                        nc.scalar.activation(sil[0:w, f, :], psum[0:w, f, 0:J], ACT.Silu).then_inc(sil_ready, 1)
                        act.wait_ge(hr_ready, NF * j.m + f + 1)
                        if not (isinstance(j.m, int) and j.m < 2):
                            act.wait_ge(dn_ps, JT * (j.m - 1))
                        nc.scalar.activation(hh[j.e][0:w, f, :], hr[0:w, f, :], ACT.Copy).then_inc(hh_ready, 1)
                        if f == 0 and not last(j):
                            high_rows(j.m + 1, 1 - j.e)
                        if f == 1 and j.kind == "a":
                            act.wait_ge(lgt_ps, j.c + 1)
                            if not (isinstance(j.m, int) and j.m == 0):
                                act.wait_ge(lg_ps, j.c)
                            nc.scalar.activation(lgt[:], psum[0:E, LG, J:2 * J], ACT.Copy).then_inc(lgt_ready, 1)
                        if f < 2 and j.next_gu:
                            high_part(j.wset + 1, 1 - j.wp, f)
                        if f == 2 and j.own_d:
                            high_part(j.wset, j.wp, 2)
                    if prev and prev.kind == "r":
                        act.wait_ge(dn_ps, JT * prev.m + JT)
                        if not (isinstance(prev.c, int) and prev.c == 0):
                            act.wait_ge(s_y, 16 * prev.c)
                        nc.scalar.activation(yout[:], psum[:, DN:DN + JT, :], ACT.Copy).then_inc(y_copied, 1)

                high_rows(0, 0)
                for i in range(3):
                    high_part(0, 0, i)
                passes(act, job, after_a=exponentials)
                for c in range(NA):
                    act.wait_ge(shift_ready, c + 1)
                    for t in range(JT):
                        ins = nc.scalar.activation(xs[:, JT * c + t, :], fin[c % 2][:, t, :], ACT.Identity, bias=shift3[c % 2][:, t:t + 1], scale=rstd3[c % 2][:, t:t + 1])
                    ins.then_inc(fin_ready, 1)

            @block.vector
            def _(dve):
                chain3 = [0]

                def link(ins):
                    chain3[0] += 1
                    ins.then_inc(own3, 1)
                    dve.wait_ge(own3, chain3[0])

                dve.wait_ge(rth_ready, 1)
                nc.vector.tensor_tensor(rtl[:], psum[:, LG, 0:KC * E].rearrange("p (k e) -> p k e", e=E), rth[:].bitcast(F32),
                                        ALU.subtract).then_inc(rt_ready, 1)
                def over(a):
                    return a.unsqueeze(2).to_broadcast([P, NT, E])

                def per_expert(a):
                    return a.unsqueeze(1).to_broadcast([P, NT, E])

                def flat(a):
                    return a[:].rearrange("p t e -> p (t e)")

                tt, tr, tsc = nc.vector.tensor_tensor, nc.vector.tensor_reduce, nc.vector.tensor_scalar
                top, tot, rtot, k1, k2, top2 = (t[:] for t in t16)

                def choose():
                    pl = psum[:, LG, 0:NT * E].rearrange("p (t e) -> p t e", e=E)
                    dve.wait_ge(lg_ps, NA)
                    link(tr(top, pl, X, ALU.max))
                    tt(lg[:], pl, over(top), ALU.subtract).then_inc(lg_ready, 1)
                    dve.wait_ge(ex_ready, 1)
                    link(tr(tot, ex[:], X, ALU.add))
                    link(nc.vector.reciprocal(rtot, tot))
                    link(tt(gates[:], ex[:], over(rtot), ALU.mult))
                    ranks = per_expert(rank[:])
                    link(tr(top, gates[:], X, ALU.max))
                    link(tt(keys[:], gates[:], over(top), ALU.is_equal))
                    link(tt(keys[:], keys[:], ranks, ALU.mult))
                    link(tr(k1, keys[:], X, ALU.max))
                    link(tt(one1[:], keys[:], over(k1), ALU.is_equal))
                    link(nc.vector.scalar_tensor_tensor(flat(rest), flat(one1), -4.0, flat(gates), ALU.mult, ALU.add))
                    link(tr(top2, rest[:], X, ALU.max))
                    link(tt(keys[:], rest[:], over(top2), ALU.is_equal))
                    link(tt(keys[:], keys[:], ranks, ALU.mult))
                    link(tr(k2, keys[:], X, ALU.max))
                    link(tt(one2[:], keys[:], over(k2), ALU.is_equal))
                    tt(both[:], one1[:], one2[:], ALU.add).then_inc(both_ready, 1)
                    link(tt(tot, top, top2, ALU.add))
                    link(tsc(tot, tot, 1e-20, None, ALU.add))
                    link(nc.vector.reciprocal(rtot, tot))
                    tt(gate[:, 0, :], top, rtot, ALU.mult)
                    link(tt(gate[:, 1, :], top2, rtot, ALU.mult))

                def place():
                    within = psum[:, LG, NT * E:2 * NT * E].rearrange("p (t e) -> p t e", e=E)
                    total = psum[:, LG, 2 * NT * E:3 * NT * E].rearrange("p (t e) -> p t e", e=E)
                    link(nc.vector.memset(before_t[:, 0, :], 0.0))
                    dve.wait_ge(pre_ps, 1)
                    for t in range(1, NT):
                        link(tt(before_t[:, t, :], before_t[:, t - 1, :], total[:, t - 1, :], ALU.add))
                    link(tt(count[:], before_t[:, NT - 1, :], total[:, NT - 1, :], ALU.add))
                    link(tsc(jobs_e[:], count[:], J / 2.0 - 0.5, 1.0 / J, ALU.add, ALU.mult))
                    link(tsc(jobs_e[:], jobs_e[:], MAGIC, None, ALU.add))
                    link(tsc(jobs_e[:], jobs_e[:], MAGIC, None, ALU.subtract))
                    link(nc.vector.tensor_copy(end_e[:, 0:1], jobs_e[:, 0:1]))
                    for x in range(1, E):
                        link(tt(end_e[:, x:x + 1], end_e[:, x - 1:x], jobs_e[:, x:x + 1], ALU.add))
                    link(tt(base_e[:], end_e[:], jobs_e[:], ALU.subtract))
                    link(tt(le[:], end_e[:].unsqueeze(1).to_broadcast([P, RJOBS, E]), job_no[:].unsqueeze(2).to_broadcast([P, RJOBS, E]),
                            ALU.is_le))
                    link(tr(exp_of[:], le[:], X, ALU.add))
                    link(tsc(exp_i[:], exp_of[:], float(E - 1), None, ALU.min))
                    link(tsc(base_e[:], base_e[:], float(J), None, ALU.mult))
                    link(tt(slots[:], before_t[:], within, ALU.add))
                    link(tt(slots[:], slots[:], per_expert(base_e[:]), ALU.add))
                    link(tt(keys[:], slots[:], one1[:], ALU.mult))
                    link(tr(slot_f[:, 0, :], keys[:], X, ALU.add))
                    link(tt(keys[:], slots[:], one2[:], ALU.mult))
                    link(tr(slot_f[:, 1, :], keys[:], X, ALU.add))
                    nc.vector.tensor_copy(slot_i[:], slot_f[:]).then_inc(slot_ready, 1)

                def low_part(n, e, i):
                    dve.wait_ge(whi_gu if i < 2 else whi_d, 2 * n + i + 1 if i < 2 else n + 1)
                    for r, k in split_rows(i):
                        ins = nc.vector.tensor_tensor(wl[e][i][r, k, :], stg[i][r, k, :], wh[e][i][r, k, :].bitcast(F32), ALU.subtract)
                    ins.then_inc(wlo_gu if i < 2 else wlo_d, 1)

                def low_rows(m, e):
                    dve.wait_ge(xh_ready, m + 1)
                    for t in range(JT):
                        part = slice(t * P, (t + 1) * P)
                        ins = nc.vector.tensor_tensor(xl[e][:, :, part], psum[:, TR + t, :].rearrange("p (k n) -> p k n", n=P),
                                                      xh[e][:, :, part].bitcast(F32), ALU.subtract)
                    ins.then_inc(xl_ready, 1)

                def row(a, t):
                    return a[:, ds(t, 1), :].rearrange("p a c -> p (a c)")

                def hidden(j):
                    for f, (_, w) in enumerate(FT):
                        dve.wait_ge(sil_ready, NF * j.m + f + 1)
                        if not (isinstance(j.m, int) and j.m == 0):
                            dve.wait_ge(hl_ready, NF * j.m + f + 1 - NF)
                        nc.vector.tensor_tensor(hr[0:w, f, :], sil[0:w, f, :], psum[0:w, f, J:2 * J], ALU.mult).then_inc(hr_ready, 1)
                        dve.wait_ge(hh_ready, NF * j.m + f + 1)
                        nc.vector.tensor_tensor(hl[j.e][0:w, f, :], hr[0:w, f, :], hh[j.e][0:w, f, :].bitcast(F32), ALU.subtract)\
                          .then_inc(hl_ready, 1)
                        if f == 0 and not last(j):
                            low_rows(j.m + 1, 1 - j.e)
                        if f < 2 and j.next_gu:
                            low_part(j.wset + 1, 1 - j.wp, f)
                        if f == 2 and j.own_d:
                            low_part(j.wset, j.wp, 2)

                def down_into_acc(prev):
                    dve.wait_ge(dn_ps, JT * prev.m + JT)
                    for t in range(JT):
                        so_far = xs if prev.kind == "a" else acc
                        ins = nc.vector.tensor_tensor(row(acc, JT * prev.c + t), row(so_far, JT * prev.c + t), psum[:, DN + t, :], ALU.add)
                    ins.then_inc(down_out, 1)

                def job(j, prev):
                    if j:
                        hidden(j)
                    if j and last(j):
                        gather_rows(0, 0)
                        gather_rows(1, 1)
                    if prev and prev.kind != "r":
                        down_into_acc(prev)

                def gather_rows(c, e):
                    f = fin[e]
                    fixed = isinstance(c, int)
                    nth = 8 * JT * c * 2 + (32 * JT if e == 0 else 16 * JT)
                    dve.wait_ge(s_got[e], nth)
                    for t in range(JT):
                        g = gate[:, 0, :][:, ds(JT * c + t, 1)]
                        ins = nc.vector.scalar_tensor_tensor(got[e][:, t, 0, :], got[e][:, t, 0, :], g, row(acc, JT * c + t), ALU.mult, ALU.add)
                    ins.then_inc(own_f["sum"], 1)
                    if not (fixed and c < 2):
                        dve.wait_ge(fin_ready, c - 1)
                    dve.wait_ge(own_f["sum"], c + 1)
                    for t in range(JT):
                        g = gate[:, 1, :][:, ds(JT * c + t, 1)]
                        ins = nc.vector.scalar_tensor_tensor(f[:, t, :], got[e][:, t, 1, :], g, got[e][:, t, 0, :], ALU.mult, ALU.add)
                    ins.then_inc(got_used, 1)
                    dve.wait_ge(got_used, c + 1)
                    for t in range(JT):
                        ins = nc.vector.bn_stats(stats3[:, t, :], f[:, t, :])
                    ins.then_inc(own_f["stats"], 1)
                    dve.wait_ge(own_f["stats"], c + 1)
                    if not (fixed and c == 0):
                        scales(c - 1, 1 - e)
                    for t in range(JT):
                        ins = nc.vector.bn_aggr(mv3[e][:, t, :], stats3[:, t, :])
                    ins.then_inc(own_f["aggr"], 1)
                    dve.wait_ge(own_f["aggr"], c + 1)
                    nc.vector.tensor_scalar(ve3[e][:], mv3[e][:, :, 1], LN_EPS, None, ALU.add).then_inc(ve3_ready, 1)

                def scales(c, e):
                    dve.wait_ge(g3_ready, c + 1)
                    nc.vector.tensor_tensor(m1[:], g3[:], g3[:], ALU.mult).then_inc(own_f["m1"], 1)
                    dve.wait_ge(own_f["m1"], c + 1)
                    nc.vector.tensor_tensor(m2[:], m1[:], ve3[e][:], ALU.mult).then_inc(own_f["m2"], 1)
                    dve.wait_ge(own_f["m2"], c + 1)
                    nc.vector.tensor_scalar(m1[:], m2[:], -0.5, 1.5, ALU.mult, ALU.add).then_inc(own_f["m3"], 1)
                    dve.wait_ge(own_f["m3"], c + 1)
                    nc.vector.tensor_tensor(rstd3[e][:], m1[:], g3[:], ALU.mult).then_inc(own_f["m4"], 1)
                    dve.wait_ge(own_f["m4"], c + 1)
                    nc.vector.scalar_tensor_tensor(shift3[e][:], mv3[e][:, :, 0], -1.0, rstd3[e][:], ALU.mult, ALU.mult).then_inc(shift_ready, 1)

                low_rows(0, 0)
                for i in range(3):
                    low_part(0, 0, i)
                passes(dve, job, after_a=choose, after_s=place)
                with dve.Fori(1, NA // 2) as i:
                    for e in range(2):
                        gather_rows(2 * i + e, e)
                scales(NA - 1, (NA - 1) % 2)

            @block.tensor
            def _(pe):
                mm = nc.tensor.matmul
                pe.wait_ge(s_r, 16)
                for k in range(KC):
                    ins = nc.tensor.transpose(psum[:, LG, k * E:(k + 1) * E], rin[:, k * P:(k + 1) * P], ident[0:E, 0:E])
                ins.then_inc(rt_ps, 1)
                pe.wait_ge(rt_ready, 1)

                def logits(c, e):
                    for k in range(KC):
                        for xx, rr in ((xh, rth), (xl, rth), (xh, rtl)):
                            ins = mm(psum[0:E, LG, J:2 * J], rr[:, k, :], xx[e][:, k, :],
                                     start=(k == 0 and xx is xh and rr is rth), stop=(k == KC - 1 and rr is rtl))
                    ins.then_inc(lgt_ps, 1)

                def turn_logits(c):
                    pe.wait_ge(lgt_ready, c + 1)
                    for t in range(JT):
                        ins = mm(psum[:, LG, ds((JT * c + t) * E, E)], lgt[:, t * P:(t + 1) * P], ident[0:E, 0:E], start=True, stop=True)
                    ins.then_inc(lg_ps, 1)

                def prefix():
                    pe.wait_ge(both_ready, 1)
                    mm(psum[:, LG, NT * E:2 * NT * E], below[:], both[:].rearrange("p t e -> p (t e)"), start=True, stop=True)
                    mm(psum[:, LG, 2 * NT * E:3 * NT * E], ones[:], both[:].rearrange("p t e -> p (t e)"), start=True, stop=True)\
                        .then_inc(pre_ps, 1)

                def turn_rows(m, e):
                    pe.wait_ge(s_row[e], 8 * m + 16 - 8 * e)
                    for t in range(JT):
                        for k in range(KC):
                            ins = nc.tensor.transpose(psum[:, TR + t, k * P:(k + 1) * P], xrow[e][:, t, k * P:(k + 1) * P], ident[:])
                    ins.then_inc(xt_ps, 1)

                def down_banks_free(j):
                    if j.kind == "r":
                        if isinstance(j.c, int) and j.c == 0:
                            pe.wait_ge(down_out, FIRST_R)
                        else:
                            pe.wait_ge(y_copied, j.c)
                    elif j.kind == "b" and j.c == NE:
                        pe.wait_ge(y_copied, RJOBS)
                    elif j.kind == "a":
                        if not (isinstance(j.c, int) and j.c == 0):
                            pe.wait_ge(down_out, j.c)
                    else:
                        pe.wait_ge(down_out, j.c + NA)

                def gate_and_up(j):
                    pe.wait_ge(xl_ready, j.m + 1)
                    pe.wait_ge(wlo_gu, 2 * j.wset + 2)
                    for f, (f0, w) in enumerate(FT):
                        if not (isinstance(j.m, int) and j.m == 0):
                            pe.wait_ge(hr_ready, NF * j.m + f + 1 - NF)
                        for i in range(2):
                            for k in range(KC):
                                for ww, xx in ((wh, xh), (wh, xl), (wl, xh)):
                                    ins = mm(psum[0:w, f, i * J:(i + 1) * J], ww[j.wp][i][:, k, f0:f0 + w], xx[j.e][:, k, :],
                                             start=(k == 0 and ww is wh and xx is xh), stop=(k == KC - 1 and ww is wl))
                        ins.then_inc(gu_ps, 1)
                        if f == 0 and not last(j):
                            turn_rows(j.m + 1, 1 - j.e)
                        if f == 1 and j.kind == "a":
                            logits(j.c, j.e)
                        if f == 0 and (j.kind == "a" or j.kind == "s" and isinstance(j.c, int) and j.c == 0):
                            if not (isinstance(j.m, int) and j.m == 0):
                                turn_logits(j.m - 1)

                def down(j):
                    pe.wait_ge(wlo_d, j.wset + 1)
                    down_banks_free(j)
                    for f, (f0, w) in enumerate(FT):
                        pe.wait_ge(hl_ready, NF * j.m + f + 1)
                        for t in range(JT):
                            for aa, ww in ((hh, wh), (hl, wh), (hh, wl)):
                                ins = mm(psum[:, DN + t, :], aa[j.e][0:w, f, t * P:(t + 1) * P], ww[j.wp][2][0:w, f, :],
                                         start=(f == 0 and aa is hh and ww is wh), stop=(f == NF - 1 and ww is wl))
                            if f == NF - 1:
                                ins.then_inc(dn_ps, 1)

                def job(j, prev):
                    if j:
                        gate_and_up(j)
                    if prev:
                        down(prev)

                turn_rows(0, 0)
                passes(pe, job, after_s=prefix)


_NAMES = {"x": "x", "ctx": "ctx_2048", "w_qkv": "L0_attn_w_qkv", "w_proj": "L0_attn_w_proj", "ssm": "L0_xattn_ssm_kernel",
          "D": "L0_xattn_D", "router": "L0_ffn_router_w", "wg": "L0_ffn_wg", "wu": "L0_ffn_wu", "wd": "L0_ffn_wd",
          "sg": "L0_ffn_sg", "su": "L0_ffn_su", "sd": "L0_ffn_sd"}


def kernel(**inputs):
    import numpy as _np
    import concourse.bacc as _bacc
    from concourse.bass_utils import run_bass_kernel_spmd as _run

    nc = _bacc.Bacc("TRN2", target_bir_lowering=False, num_devices=1)
    arrays, aps = {}, {}
    for short, name in _NAMES.items():
        a = _np.ascontiguousarray(inputs[name])
        arrays[f"in_{short}"] = a
        aps[short] = nc.dram_tensor(f"in_{short}", a.shape, mybir.dt.from_np(a.dtype), kind="ExternalInput").ap()
    shape = inputs["x"].shape
    aps["out"] = nc.dram_tensor("out", shape, F32, kind="ExternalOutput").ap()
    build(nc, aps)
    r = _run(nc, [arrays], core_ids=[0])
    return r.results[0]["out"]
```
